# Optimizing a Trainium2 kernel written in Bass

```python
import numpy as np
import jax
import jax.numpy as jnp

def _softmax(x, axis=-1):
    return jax.nn.softmax(x, axis=axis)

def _gelu(x):
    return jax.nn.gelu(x, approximate=True)

def _silu(x):
    return jax.nn.silu(x)

def _sigmoid(x):
    return jax.nn.sigmoid(x)

def _layernorm(x, axis=-1, eps=1e-05):
    m = jnp.mean(x, axis=axis, keepdims=True)
    v = jnp.var(x, axis=axis, keepdims=True)
    return (x - m) / jnp.sqrt(v + eps)

def _scatter_add(tgt, idx, src, axis=0):
    return tgt.at[idx].add(src)

def _segment_sum(src, seg, n):
    return jax.ops.segment_sum(src, seg, n)
kernel_name = 'mk_lm_tower_d1_tok_ids1024_r4_bc1b83'

def setup_inputs(seed: int=0):
    np.random.seed(seed)
    _w = jnp.asarray

    def _rec_inputs():
        import jax
        import jax.numpy as jnp
        _rk = jax.random.key(seed)
        x = jax.random.randint(jax.random.fold_in(_rk, 1), (4, 512), 0, 8000, jnp.int32)
        return x
    x = _rec_inputs()

    def _L0_tok_setup():
        import jax, jax.numpy as jnp
        import numpy as np
        MAX_SEQ_LEN = 512
        D_MODEL = 256
        VOCAB = 8000

        def sinusoidal_pe(max_seq_len, d_model, dtype=jnp.float32):
            pos = jnp.arange(max_seq_len, dtype=dtype)[:, None]
            i = jnp.arange(d_model)
            denom = jnp.power(jnp.asarray(10000.0, dtype), (2 * (i // 2)).astype(dtype) / d_model)
            angle = pos / denom
            pe = jnp.where(i % 2 == 0, jnp.sin(angle), jnp.cos(angle))
            return pe
        key = jax.random.key(seed)
        k1, k2 = jax.random.split(key)
        tokens = jax.random.randint(k1, (16, MAX_SEQ_LEN), 0, VOCAB, dtype=jnp.int64 if jax.config.jax_enable_x64 else jnp.int32)
        emb = jax.random.normal(k2, (VOCAB, D_MODEL), dtype=jnp.float32)
        return {'tokens': tokens, 'emb': emb}
    _L0_tok_all = _L0_tok_setup()
    _L0_tok_in = {k: v for k, v in _L0_tok_all.items() if k in ('emb',)}
    del _L0_tok_all

    def _L0_attn_setup():
        import jax, jax.numpy as jnp
        import numpy as np
        N_HEAD = 16
        LATENT = 32

        def _rotate_half(x):
            xe = x[..., ::2]
            xo = x[..., 1::2]
            return jnp.stack((-xo, xe), axis=-1).reshape(x.shape)

        def _rope_tables(T, latent_dim, dtype):
            inv_freq = 1.0 / 10000.0 ** (jnp.arange(0, latent_dim, 2, dtype=jnp.float32) / latent_dim)
            t = jnp.arange(T, dtype=jnp.float32)
            freqs = jnp.outer(t, inv_freq)
            cos = jnp.repeat(jnp.cos(freqs), 2, axis=-1)[:, :latent_dim]
            sin = jnp.repeat(jnp.sin(freqs), 2, axis=-1)[:, :latent_dim]
            return (cos.astype(dtype), sin.astype(dtype))
        key = jax.random.key(seed)
        ks = jax.random.split(key, 14)
        C = 256
        hd = C // N_HEAD
        L = LATENT
        s = 0.02
        return {'x': jax.random.normal(ks[0], (4, 512, C), jnp.float32), 'c_attn_w': jax.random.normal(ks[1], (3 * C, C), jnp.float32) * s, 'c_attn_b': jnp.zeros((3 * C,), jnp.float32), 'q2l_w': jax.random.normal(ks[2], (L, hd), jnp.float32) * s, 'q2l_b': jnp.zeros((L,), jnp.float32), 'kv2l_w': jax.random.normal(ks[3], (L, hd), jnp.float32) * s, 'kv2l_b': jnp.zeros((L,), jnp.float32), 'l2o_w': jax.random.normal(ks[4], (hd, L), jnp.float32) * s, 'l2o_b': jnp.zeros((hd,), jnp.float32), 'wqk_w': jax.random.normal(ks[5], (L, L), jnp.float32) * s, 'wqk_b': jnp.zeros((L,), jnp.float32), 'cproj_w': jax.random.normal(ks[6], (C, C), jnp.float32) * s, 'cproj_b': jnp.zeros((C,), jnp.float32)}
    _L0_attn_all = _L0_attn_setup()
    _L0_attn_in = {k: v for k, v in _L0_attn_all.items() if k in ('c_attn_w', 'c_attn_b', 'q2l_w', 'q2l_b', 'kv2l_w', 'kv2l_b', 'l2o_w', 'l2o_b', 'wqk_w', 'wqk_b', 'cproj_w', 'cproj_b')}
    del _L0_attn_all

    def _L0_ffn_setup():
        import jax, jax.numpy as jnp
        import numpy as np
        B, S, H = (1, 512, 256)
        E, K = (16, 4)
        G, TG = (4, 2)
        I_MOE = 128
        N_SH = 2
        SCALE = 2.5

        def _mlp(x, gw, uw, dw):
            return jax.nn.silu(x @ gw.T) * (x @ uw.T) @ dw.T

        def _route(x2d, router_weight, e_bias):
            T = x2d.shape[0]
            scores = jax.nn.sigmoid(x2d @ router_weight.T)
            sc = scores + e_bias[None, :]
            group_scores = jnp.sum(jax.lax.top_k(sc.reshape(T, G, E // G), 2)[0], axis=-1)
            _, gidx = jax.lax.top_k(group_scores, TG)
            gmask = jnp.zeros((T, G), sc.dtype).at[jnp.arange(T)[:, None], gidx].set(1.0)
            smask = jnp.repeat(gmask, E // G, axis=1)
            masked = jnp.where(smask > 0, sc, 0.0)
            _, tidx = jax.lax.top_k(masked, K)
            tw = jnp.take_along_axis(scores, tidx, axis=1)
            tw = tw / (jnp.sum(tw, axis=-1, keepdims=True) + 1e-20)
            tw = tw * SCALE
            return (tidx, tw)

        def _moe_forward(hidden_states, router_weight, e_bias, gate_w, up_w, down_w, sh_gate_w, sh_up_w, sh_down_w):
            orig_shape = hidden_states.shape
            x = hidden_states.reshape(-1, H)
            T = x.shape[0]
            tidx, tw = _route(x, router_weight, e_bias)
            g = jnp.einsum('th,eih->tei', x, gate_w)
            u = jnp.einsum('th,eih->tei', x, up_w)
            h = jax.nn.silu(g) * u
            yo = jnp.einsum('tei,ehi->teh', h, down_w)
            combine = jnp.zeros((T, E), tw.dtype).at[jnp.arange(T)[:, None], tidx].add(tw)
            routed = jnp.einsum('te,teh->th', combine, yo)
            shared = _mlp(hidden_states.reshape(-1, H), sh_gate_w, sh_up_w, sh_down_w)
            return (routed + shared).reshape(orig_shape)
        key = jax.random.key(seed)
        ks = jax.random.split(key, 9)
        s = 0.02
        return {'hidden_states': jax.random.normal(ks[0], (B, S, H), jnp.float32), 'router_weight': jax.random.normal(ks[1], (E, H), jnp.float32) * s, 'e_bias': jnp.zeros((E,), jnp.float32), 'gate_w': jax.random.normal(ks[2], (E, I_MOE, H), jnp.float32) * s, 'up_w': jax.random.normal(ks[3], (E, I_MOE, H), jnp.float32) * s, 'down_w': jax.random.normal(ks[4], (E, H, I_MOE), jnp.float32) * s, 'sh_gate_w': jax.random.normal(ks[5], (N_SH * I_MOE, H), jnp.float32) * s, 'sh_up_w': jax.random.normal(ks[6], (N_SH * I_MOE, H), jnp.float32) * s, 'sh_down_w': jax.random.normal(ks[7], (H, N_SH * I_MOE), jnp.float32) * s}
    _L0_ffn_all = _L0_ffn_setup()
    _L0_ffn_in = {k: v for k, v in _L0_ffn_all.items() if k in ('router_weight', 'e_bias', 'gate_w', 'up_w', 'down_w', 'sh_gate_w', 'sh_up_w', 'sh_down_w')}
    del _L0_ffn_all
    return {'x': x, 'L0_tok_emb': _L0_tok_in['emb'], 'L0_attn_c_attn_w': _L0_attn_in['c_attn_w'], 'L0_attn_c_attn_b': _L0_attn_in['c_attn_b'], 'L0_attn_q2l_w': _L0_attn_in['q2l_w'], 'L0_attn_q2l_b': _L0_attn_in['q2l_b'], 'L0_attn_kv2l_w': _L0_attn_in['kv2l_w'], 'L0_attn_kv2l_b': _L0_attn_in['kv2l_b'], 'L0_attn_l2o_w': _L0_attn_in['l2o_w'], 'L0_attn_l2o_b': _L0_attn_in['l2o_b'], 'L0_attn_wqk_w': _L0_attn_in['wqk_w'], 'L0_attn_wqk_b': _L0_attn_in['wqk_b'], 'L0_attn_cproj_w': _L0_attn_in['cproj_w'], 'L0_attn_cproj_b': _L0_attn_in['cproj_b'], 'L0_ffn_router_weight': _L0_ffn_in['router_weight'], 'L0_ffn_e_bias': _L0_ffn_in['e_bias'], 'L0_ffn_gate_w': _L0_ffn_in['gate_w'], 'L0_ffn_up_w': _L0_ffn_in['up_w'], 'L0_ffn_down_w': _L0_ffn_in['down_w'], 'L0_ffn_sh_gate_w': _L0_ffn_in['sh_gate_w'], 'L0_ffn_sh_up_w': _L0_ffn_in['sh_up_w'], 'L0_ffn_sh_down_w': _L0_ffn_in['sh_down_w']}

def reference(x, L0_tok_emb, L0_attn_c_attn_w, L0_attn_c_attn_b, L0_attn_q2l_w, L0_attn_q2l_b, L0_attn_kv2l_w, L0_attn_kv2l_b, L0_attn_l2o_w, L0_attn_l2o_b, L0_attn_wqk_w, L0_attn_wqk_b, L0_attn_cproj_w, L0_attn_cproj_b, L0_ffn_router_weight, L0_ffn_e_bias, L0_ffn_gate_w, L0_ffn_up_w, L0_ffn_down_w, L0_ffn_sh_gate_w, L0_ffn_sh_up_w, L0_ffn_sh_down_w):
    import jax
    import jax.numpy as jnp

    def _L0_tok_ref(tokens, emb):
        import jax, jax.numpy as jnp
        import numpy as np
        MAX_SEQ_LEN = 512
        D_MODEL = 256
        VOCAB = 8000

        def sinusoidal_pe(max_seq_len, d_model, dtype=jnp.float32):
            pos = jnp.arange(max_seq_len, dtype=dtype)[:, None]
            i = jnp.arange(d_model)
            denom = jnp.power(jnp.asarray(10000.0, dtype), (2 * (i // 2)).astype(dtype) / d_model)
            angle = pos / denom
            pe = jnp.where(i % 2 == 0, jnp.sin(angle), jnp.cos(angle))
            return pe
        we = jnp.take(emb, tokens, axis=0)
        pe = sinusoidal_pe(MAX_SEQ_LEN, D_MODEL, we.dtype)
        return we + pe[None, :, :]

    def _L0_attn_ref(x, c_attn_w, c_attn_b, q2l_w, q2l_b, kv2l_w, kv2l_b, l2o_w, l2o_b, wqk_w, wqk_b, cproj_w, cproj_b):
        import jax, jax.numpy as jnp
        import numpy as np
        N_HEAD = 16
        LATENT = 32

        def _rotate_half(x):
            xe = x[..., ::2]
            xo = x[..., 1::2]
            return jnp.stack((-xo, xe), axis=-1).reshape(x.shape)

        def _rope_tables(T, latent_dim, dtype):
            inv_freq = 1.0 / 10000.0 ** (jnp.arange(0, latent_dim, 2, dtype=jnp.float32) / latent_dim)
            t = jnp.arange(T, dtype=jnp.float32)
            freqs = jnp.outer(t, inv_freq)
            cos = jnp.repeat(jnp.cos(freqs), 2, axis=-1)[:, :latent_dim]
            sin = jnp.repeat(jnp.sin(freqs), 2, axis=-1)[:, :latent_dim]
            return (cos.astype(dtype), sin.astype(dtype))
        B, T, C = x.shape
        H = N_HEAD
        hd = C // H
        L = q2l_w.shape[0]
        qkv = x @ c_attn_w.T + c_attn_b
        q, k, v = jnp.split(qkv, 3, axis=2)

        def heads(t):
            return t.reshape(B, T, H, hd).transpose(0, 2, 1, 3)
        q, k, v = (heads(q), heads(k), heads(v))
        q_lat = q @ q2l_w.T + q2l_b
        k_lat = k @ kv2l_w.T + kv2l_b
        v_lat = v @ kv2l_w.T + kv2l_b
        cos, sin = _rope_tables(T, L, x.dtype)
        cos = cos[None, None]
        sin = sin[None, None]
        q_lat = q_lat * cos + _rotate_half(q_lat) * sin
        k_lat = k_lat * cos + _rotate_half(k_lat) * sin
        q_for_k = q_lat @ wqk_w.T + wqk_b
        att = jnp.einsum('bhql,bhkl->bhqk', q_for_k, k_lat) * L ** (-0.5)
        causal = jnp.tril(jnp.ones((T, T), dtype=bool))
        att = jnp.where(causal[None, None], att, -jnp.inf)
        att = jax.nn.softmax(att, axis=-1)
        y_lat = jnp.einsum('bhqk,bhkl->bhql', att, v_lat)
        y = y_lat @ l2o_w.T + l2o_b
        y = y.transpose(0, 2, 1, 3).reshape(B, T, C)
        return y @ cproj_w.T + cproj_b

    def _L0_ffn_ref(hidden_states, router_weight, e_bias, gate_w, up_w, down_w, sh_gate_w, sh_up_w, sh_down_w):
        import jax, jax.numpy as jnp
        import numpy as np
        B, S, H = (1, 512, 256)
        E, K = (16, 4)
        G, TG = (4, 2)
        I_MOE = 128
        N_SH = 2
        SCALE = 2.5

        def _mlp(x, gw, uw, dw):
            return jax.nn.silu(x @ gw.T) * (x @ uw.T) @ dw.T

        def _route(x2d, router_weight, e_bias):
            T = x2d.shape[0]
            scores = jax.nn.sigmoid(x2d @ router_weight.T)
            sc = scores + e_bias[None, :]
            group_scores = jnp.sum(jax.lax.top_k(sc.reshape(T, G, E // G), 2)[0], axis=-1)
            _, gidx = jax.lax.top_k(group_scores, TG)
            gmask = jnp.zeros((T, G), sc.dtype).at[jnp.arange(T)[:, None], gidx].set(1.0)
            smask = jnp.repeat(gmask, E // G, axis=1)
            masked = jnp.where(smask > 0, sc, 0.0)
            _, tidx = jax.lax.top_k(masked, K)
            tw = jnp.take_along_axis(scores, tidx, axis=1)
            tw = tw / (jnp.sum(tw, axis=-1, keepdims=True) + 1e-20)
            tw = tw * SCALE
            return (tidx, tw)

        def _moe_forward(hidden_states, router_weight, e_bias, gate_w, up_w, down_w, sh_gate_w, sh_up_w, sh_down_w):
            orig_shape = hidden_states.shape
            x = hidden_states.reshape(-1, H)
            T = x.shape[0]
            tidx, tw = _route(x, router_weight, e_bias)
            g = jnp.einsum('th,eih->tei', x, gate_w)
            u = jnp.einsum('th,eih->tei', x, up_w)
            h = jax.nn.silu(g) * u
            yo = jnp.einsum('tei,ehi->teh', h, down_w)
            combine = jnp.zeros((T, E), tw.dtype).at[jnp.arange(T)[:, None], tidx].add(tw)
            routed = jnp.einsum('te,teh->th', combine, yo)
            shared = _mlp(hidden_states.reshape(-1, H), sh_gate_w, sh_up_w, sh_down_w)
            return (routed + shared).reshape(orig_shape)
        return _moe_forward(hidden_states, router_weight, e_bias, gate_w, up_w, down_w, sh_gate_w, sh_up_w, sh_down_w)
    h = _L0_tok_ref(x, L0_tok_emb)
    h = h + _L0_attn_ref(_layernorm(h, axis=-1), L0_attn_c_attn_w, L0_attn_c_attn_b, L0_attn_q2l_w, L0_attn_q2l_b, L0_attn_kv2l_w, L0_attn_kv2l_b, L0_attn_l2o_w, L0_attn_l2o_b, L0_attn_wqk_w, L0_attn_wqk_b, L0_attn_cproj_w, L0_attn_cproj_b)
    h = h + _L0_ffn_ref(_layernorm(h, axis=-1), L0_ffn_router_weight, L0_ffn_e_bias, L0_ffn_gate_w, L0_ffn_up_w, L0_ffn_down_w, L0_ffn_sh_gate_w, L0_ffn_sh_up_w, L0_ffn_sh_down_w)
    return h

_drawn_inputs = setup_inputs


def setup_inputs(seed=0):
    import zlib

    import numpy as np

    out = dict(_drawn_inputs(seed))
    spreads = {'L0_attn_c_attn_b': (0.0, 0.8),
     'L0_attn_q2l_b': (0.0, 0.8),
     'L0_attn_kv2l_b': (0.0, 0.8),
     'L0_attn_l2o_b': (0.0, 0.1),
     'L0_attn_wqk_b': (0.0, 0.8),
     'L0_attn_cproj_b': (0.0, 0.1),
     'L0_ffn_e_bias': (0.0, 0.576)}
    factors = {'L0_attn_c_attn_w': 8.0,
     'L0_attn_q2l_w': 8.0,
     'L0_attn_kv2l_w': 8.0,
     'L0_attn_l2o_w': 8.0,
     'L0_attn_wqk_w': 8.0,
     'L0_ffn_router_weight': 8.0,
     'L0_ffn_gate_w': 4.682,
     'L0_ffn_up_w': 4.625,
     'L0_ffn_down_w': 4.631,
     'L0_ffn_sh_gate_w': 4.134,
     'L0_ffn_sh_up_w': 4.122,
     'L0_ffn_sh_down_w': 4.145}
    for name, (base, spread) in spreads.items():
        noise = np.random.default_rng([zlib.crc32(name.encode()), seed]).standard_normal(out[name].shape)
        drawn = base * np.exp(spread * noise) if base else spread * noise
        out[name] = jnp.asarray(drawn.astype(out[name].dtype))
    for name, factor in factors.items():
        out[name] = (out[name] * factor).astype(out[name].dtype)
    return out
```

```python
from contextlib import ExitStack

import numpy as np

import concourse.bass as bass
from concourse import mybir

F32 = mybir.dt.float32
F32R = mybir.dt.float32r
BF16 = mybir.dt.bfloat16
I32 = mybir.dt.int32
ALU = mybir.AluOpType
ACT = mybir.ActivationFunctionType
AX_X = mybir.AxisListType.X

P = 128
B, T, C = 4, 512, 256
NT = T // P
NC = C // P
NH, HD, L = 16, 16, 32
GH = 4
NGB = NH // GH
NG = B * NGB
HALF = 8
NHALF = B * NH // HALF
NE, TOPK, NGRP = 16, 4, 4
EPG = NE // NGRP
NSH = 2
NX = NE + NSH
I = 128
WCOLS = 2 * NC * I + C
LN_EPS = 1e-5
ROUTE_SCALE = 2.5
SCORE_SCALE = float(L) ** -0.5
ST_UNITS = 10
P_SLOTS = 12

ST_TILES = ([[(h, 0, 0)] for h in range(GH)]
            + [[(h, 1, 0), (h, 3, T - P)] for h in range(GH)]
            + [[(h, 2, 0), (h + 1, 2, T - 2 * P)] for h in (0, 2)])
MAX_TILES = ([(3, h, 1) for h in range(GH)] + [(2, h, 1) for h in range(GH)]
             + [(1, 0, 2), (1, 2, 2)] + [(0, 0, 4)])


def attention_steps():
    steps = []
    for g in range(-2, NG + 2):
        if g == -2:
            steps.append(("norm1", 0))
        if g >= 5 and g % NGB == 1:
            steps.append(("cproj", g // NGB - 1))
        if 0 <= g - 1 < NG:
            steps.append(("values", g - 1))
        if 0 <= g < NG and g % NGB == 0:
            steps.append(("vproj", g // NGB))
        if g >= 5 and g % NGB == 1:
            steps.append(("tail", g // NGB - 1))
        if 0 <= g < NG and g % NGB == 1 and g // NGB + 1 < B:
            steps.append(("norm1", g // NGB + 1))
        if g % 2 == 0 and 0 <= g // 2 + 1 < NHALF:
            steps.append(("rope", g // 2 + 1))
        if -1 <= g < NG:
            steps.append(("scores", g))
        if 0 <= g + 2 < NG:
            steps.append(("latq", g + 2))
    return steps


def fill_order(steps):
    fills = []
    for kind, n in steps:
        if kind == "norm1":
            fills += [("xT", n, c) for c in range(NC)]
        elif kind in ("cproj", "vproj"):
            fills += [(kind, n, i) for i in range(NT // 2)]
        elif kind == "rope":
            fills += [("rope", 2 * n + q, s) for q in range(2) for s in range(2)]
        elif kind == "latq":
            fills += [("latq", n)]
        elif kind == "scores" and n + 1 < NG:
            fills += [("maxT", n + 1)]
        elif kind == "tail":
            fills += [("x2T", n, c) for c in range(NC)] + [("router", n)]
    return {name: k for k, name in enumerate(fills)}


def passes(w, x):
    return (w[0], x[0]), (w[1], x[0]), (w[0], x[1])


def build_program(nc, io):
    steps = attention_steps()
    fills = fill_order(steps)
    fill_names = list(fills)
    norms = [s for s in steps if s[0] in ("norm1", "tail")]
    with ExitStack() as ctx:
        def sem(name):
            return ctx.enter_context(nc.semaphore(name))

        def sb(scope, name, shape, dt=F32):
            return scope.enter_context(nc.sbuf_tensor(name, shape, dt))

        def pair(scope, name, shape):
            return [sb(scope, f"{name}_{x}", shape, F32R) for x in ("hi", "lo")]

        ident = sb(ctx, "ident", [P, P])
        h_all = sb(ctx, "h_all", [P, B * NT, C])
        x2T = sb(ctx, "x2T", [P, NC, B * T])
        comb = sb(ctx, "comb", [P, B, NT * NE])
        onehot = sb(ctx, "onehot", [48, NE], F32R)

        att = ctx.enter_context(ExitStack())
        tok_idx = sb(att, "tok_idx", [P, B * NT], I32)
        pos_enc = sb(att, "pos_enc", [P, NT, C])
        cproj_bias = sb(att, "cproj_bias", [P, C])
        rope_cos = sb(att, "rope_cos", [P, T])
        rope_sin = sb(att, "rope_sin", [P, T])
        ident_b = sb(att, "ident_b", [P, P], BF16)
        mask_kq = sb(att, "mask_kq", [P, P], BF16)
        mask_qk = sb(att, "mask_qk", [P, P], BF16)
        wlat = pair(att, "wlat", [P, 2, 2, NC, 2, P])
        wval = pair(att, "wval", [P, NC, C])
        wqk = pair(att, "wqk", [P, 2, HALF, L])
        wcp = pair(att, "wcp", [P, NGB, C])
        small = sb(att, "small", [P, 12])
        blat = sb(att, "blat", [P, 8])
        vconst = sb(att, "vconst", [P, NGB])
        lat32 = sb(att, "lat32", [L, 3 * P + 1])
        router_w = sb(att, "router_w", [P, NC, NE])
        ebias = sb(att, "ebias", [P, NT * NE])
        same_row = sb(att, "same_row", [P, NT * NE])
        earlier = sb(att, "earlier", [P, NT, NGRP, NGRP])
        onehot_raw = sb(att, "onehot_raw", [48, NE])
        stats = sb(att, "stats", [P, NT, 6])
        meanvar = sb(att, "meanvar", [P, NT, 2])
        rstd = sb(att, "rstd", [P, NT])
        neghalf = sb(att, "neghalf", [P, NT])
        xn = sb(att, "xn", [P, NT, C])
        xT = pair(att, "xT", [P, NC, T])
        prod = sb(att, "prod", [P, 4, T])
        roped = sb(att, "roped", [P, 2, 2, T])
        qrope = pair(att, "qrope", [P, 2, T])
        krope_hi = sb(att, "krope_hi", [P, 2, T], F32R)
        qlat = pair(att, "qlat", [P, T])
        qstack = [sb(att, f"qstack{p}", [97, GH, T], F32R) for p in range(2)]
        kstack = [sb(att, f"kstack{p}", [97, GH, T], F32R) for p in range(2)]
        rowmax = sb(att, "rowmax", [P, NT * GH])
        rowmaxT = sb(att, "rowmaxT", [NT * GH, P], F32R)
        val = sb(att, "val", [P, NT, NH, L])
        probs = sb(att, "probs", [P, P_SLOTS, T])
        yn = sb(att, "yn", [P, T])
        yT = pair(att, "yT", [P, NGB, T])
        rt = sb(att, "rt", [P, 12, NT * NE])

        ring = probs[:, :, :].rearrange("p s t -> p (s t)")
        cuts = np.cumsum([0, 6 * C, 4 * P, 2 * HALF * L, NGB * C, P, HALF * L])
        raw = [ring[:, a:b] for a, b in zip(cuts[:-1].tolist(), cuts[1:].tolist())]
        raw_rows = raw[0].rearrange("p (n c) -> p n c", n=6)
        raw_bd = raw[1].rearrange("p (x c) -> p x c", x=2)
        raw_wqk, raw_wcp, block_mask = raw[2], raw[3], raw[4]
        l2o_kv2l = raw[5].rearrange("p (h l) -> p h l", h=HALF)

        banks = [ctx.enter_context(nc.psum_tensor(f"bank{i}", [P, T], F32)) for i in range(8)]
        work_banks, st_banks, mx_banks, pv_bank = banks[0:2], banks[2:5], banks[5:7], banks[7]
        fold_banks = banks[2:7]

        tok_in, raw_in, consts_in = sem("tok_in"), sem("raw_in"), sem("consts_in")
        rows_in = [sem(f"rows_in{b}") for b in range(B)]
        pool_init, dve_init = sem("pool_init"), sem("dve_init")
        m_mm, m_ready = sem("m_mm"), sem("m_ready")
        fold_mm, fold_hi, fold_lo = sem("fold_mm"), sem("fold_hi"), sem("fold_lo")
        bias_ready, raw_hi, raw_lo = sem("bias_ready"), sem("raw_hi"), sem("raw_lo")
        h_ready, h_biased, h2_ready = sem("h_ready"), sem("h_biased"), sem("h2_ready")
        ln_stats, ln_aggr, ln_eps, ln_rstd = sem("ln_stats"), sem("ln_aggr"), sem("ln_eps"), sem("ln_rstd")
        xn_ready = sem("xn_ready")
        filled = sem("filled")
        xT_hi, xT_lo = sem("xT_hi"), sem("xT_lo")
        prod_ready, sum_roped, rope_hi, rope_lo = sem("prod_ready"), sem("sum_roped"), sem("rope_hi"), sem("rope_lo")
        latq_hi, latq_lo = sem("latq_hi"), sem("latq_lo")
        stack_in = [sem(f"stack_in{p}") for p in range(2)]
        maxrow_in = [sem(f"maxrow_in{p}") for p in range(2)]
        mx_mm, mx_red, maxT_ready = sem("mx_mm"), sem("mx_red"), sem("maxT_ready")
        st_mm, st_exp = sem("st_mm"), sem("st_exp")
        val_ready, pv_mm = sem("val_ready"), sem("pv_mm")
        den_ready, rden_ready, yn_ready = sem("den_ready"), sem("rden_ready"), sem("yn_ready")
        y_hi, y_lo = sem("y_hi"), sem("y_lo")
        x2T_ready, sig_ready, routed = sem("x2T_ready"), sem("sig_ready"), sem("routed")
        comb_ready, att_done = sem("comb_ready"), sem("att_done")
        wstage_in = [sem(f"wstage_in{i}") for i in range(2)]
        ex_hi, ex_lo = sem("ex_hi"), sem("ex_lo")
        xs_hi, xs_lo = sem("xs_hi"), sem("xs_lo")
        combT_mm, combT_hi, combT_lo = sem("combT_mm"), sem("combT_hi"), sem("combT_lo")
        combT_init = sem("combT_init")
        gate_mm, up_mm, spread_mm, down_mm = sem("gate_mm"), sem("up_mm"), sem("spread_mm"), sem("down_mm")
        silu_ready, weighted, hid_ready = sem("silu_ready"), sem("weighted"), sem("hid_ready")
        hid_hi, hid_lo = sem("hid_hi"), sem("hid_lo")
        y_copied = [sem(f"y_copied{c}") for c in range(NC)]
        yback_mm, sum_ready = sem("yback_mm"), sem("sum_ready")
        out_done = [sem(f"out_done{i}") for i in range(2)]

        CONSTS = (("pos_enc", pos_enc[:]), ("small", small[:]), ("lat32", lat32[:]), ("block_mask", block_mask),
                  ("ident", ident[:]), ("rope_cos", rope_cos[:]), ("rope_sin", rope_sin[:]),
                  ("ident_b", ident_b[:]), ("mask_kq", mask_kq[:]), ("mask_qk", mask_qk[:]),
                  ("cproj_bias", cproj_bias[:]), ("router", router_w[:]), ("ebias", ebias[:]),
                  ("same_row", same_row[:]), ("earlier", earlier[:]), ("onehot", onehot_raw[:]))
        RAWS = (("c_attn_rows", raw_rows), ("lat_bd", raw_bd), ("wqk_bd", raw_wqk), ("cproj_pad", raw_wcp))
        BQKV, LATB, WQKB, L2OB = 0, 6, 10, 11
        STACK_DMAS = 9 * GH
        NMX = len(MAX_TILES)

        def hof(g):
            return g % 2 * GH

        def wait_stack(eng, g):
            eng.wait_ge(stack_in[g % 2], 16 * STACK_DMAS * (g // 2 + 1))

        def wait_read(eng, name):
            kind, n = name[0], name[1]
            if kind == "xT":
                eng.wait_ge(xT_hi, NC * n + name[2] + 1)
                eng.wait_ge(xT_lo, NC * n + name[2] + 1)
            elif kind == "rope":
                eng.wait_ge(prod_ready, 4 * n + 2 * (name[2] + 1))
            elif kind == "latq":
                eng.wait_ge(latq_hi, n + 1)
                eng.wait_ge(latq_lo, n + 1)
            elif kind == "maxT":
                eng.wait_ge(maxT_ready, n + 1)
            elif kind == "vproj":
                eng.wait_ge(val_ready, NT // 2 * n + name[2] + 1)
            elif kind == "cproj":
                eng.wait_ge(h2_ready, NT // 2 * n + name[2] + 1)
            elif kind == "x2T":
                eng.wait_ge(x2T_ready, NC * n + name[2] + 1)
            elif kind == "router":
                eng.wait_ge(sig_ready, n + 1)

        def bank_to_fill(pe, name):
            k = fills[name]
            if k >= 2:
                wait_read(pe, fill_names[k - 2])
            return work_banks[k % 2]

        def filled_bank(eng, name):
            eng.wait_ge(filled, fills[name] + 1)
            return work_banks[fills[name] % 2]

        def sp_setup(sp):
            sp.dma_start(tok_idx[:], io["tok"]).then_inc(tok_in, 16)
            for name, dst in RAWS:
                sp.dma_start(dst, io[name]).then_inc(raw_in, 16)
            for name, dst in CONSTS:
                sp.dma_start(dst, io[name]).then_inc(consts_in, 16)

        def sp_latq(sp, g):
            par, rows = g % 2, hof(g) * HD
            if g >= 2:
                sp.wait_ge(st_mm, ST_UNITS * (g - 1))
            sp.wait_ge(rope_hi, 4 * (g // 2) + 2)
            sp.wait_ge(rope_lo, 4 * (g // 2) + 2)
            for r in range(3):
                for s in range(2):
                    for h in range(GH):
                        at, to = rows + HD * h, 32 * r + HD * s
                        part = roped[at:at + HD, 1, s, :] if r == 1 else krope_hi[at:at + HD, s, :].bitcast(F32)
                        sp.dma_start(kstack[par][to:to + HD, h, :].bitcast(F32), part).then_inc(stack_in[par], 16)
            sp.wait_ge(latq_hi, g + 1)
            sp.wait_ge(latq_lo, g + 1)
            for r in range(3):
                for h in range(GH):
                    sp.dma_start(qstack[par][L * r:L * r + L, h, :].bitcast(F32),
                                 qlat[r // 2][L * h:L * h + L, :].bitcast(F32)).then_inc(stack_in[par], 16)

        def sp_scores(sp, g):
            n = g + 1
            if n < NG:
                sp.wait_ge(maxT_ready, n + 1)
                for i in range(NT):
                    sp.dma_start(qstack[n % 2][96:97, :, i * P:(i + 1) * P].bitcast(F32),
                                 rowmaxT[i * GH:(i + 1) * GH, :].bitcast(F32)).then_inc(maxrow_in[n % 2], 16)

        def pool_embed(pool, b):
            pool.wait_ge(rows_in[b], 16 * NT)
            rows = h_all[:, b * NT:(b + 1) * NT, :]
            nc.gpsimd.tensor_tensor(rows, rows, pos_enc[:], ALU.add).then_inc(h_ready, 1)

        def pool_setup(pool):
            nc.gpsimd.memset(neghalf[:], -0.5).then_inc(pool_init, 1)
            pool.wait_ge(tok_in, 16)
            for t in range(B * NT):
                nc.gpsimd.indirect_dma_start(
                    out=h_all[:, t, :], out_offset=None, in_=io["emb"],
                    in_offset=bass.IndirectOffsetOnAxis(ap=tok_idx[:, t:t + 1], axis=0)).then_inc(rows_in[t // NT], 16)
            pool.wait_ge(consts_in, 16 * len(CONSTS))
            pool.wait_ge(pool_init, 1)
            pool_embed(pool, 0)

        def pool_rstd(pool, m):
            pool.wait_ge(ln_aggr, NT * (m + 1))
            if m >= 1:
                pool.wait_ge(xn_ready, NT * m)
            nc.gpsimd.tensor_scalar(rstd[:], meanvar[:, :, 1], LN_EPS, None, ALU.add).then_inc(ln_eps, 1)
            pool.wait_ge(ln_eps, m + 1)
            nc.gpsimd.tensor_tensor(rstd[:], rstd[:], neghalf[:], ALU.pow).then_inc(ln_rstd, 1)

        def pool_norm1(pool, b):
            m = norms.index(("norm1", b))
            pool_rstd(pool, m)
            pool.wait_ge(xn_ready, NT * (m + 1))
            for t in range(b * NT, (b + 1) * NT):
                nc.gpsimd.tensor_tensor(h_all[:, t, :], h_all[:, t, :], cproj_bias[:], ALU.add).then_inc(h_biased, 1)
            if b + 1 < B:
                pool_embed(pool, b + 1)

        def pool_tail(pool, b):
            pool_rstd(pool, norms.index(("tail", b)))

        def pool_rope(pool, n):
            for u in (2 * n, 2 * n + 1):
                kq = 1 - u % 2
                pool.wait_ge(prod_ready, 4 * (u + 1))
                if u >= 2:
                    pool.wait_ge(rope_lo, 2 * (u - 1))
                    if kq:
                        wait_stack(pool, 2 * n - 1)
                nc.gpsimd.tensor_tensor(roped[:, kq, 0, :], prod[:, 0, :], prod[:, 1, :],
                                        ALU.subtract).then_inc(sum_roped, 1)
                nc.gpsimd.tensor_tensor(roped[:, kq, 1, :], prod[:, 2, :], prod[:, 3, :],
                                        ALU.add).then_inc(sum_roped, 1)
                for s in range(2):
                    pool.wait_ge(rope_hi, 2 * u + s + 1)
                    hi = krope_hi if kq else qrope[0]
                    lo = roped[:, 1, s, :].bitcast(F32R) if kq else qrope[1][:, s, :]
                    nc.gpsimd.tensor_tensor(lo, roped[:, kq, s, :], hi[:, s, :].bitcast(F32),
                                            ALU.subtract).then_inc(rope_lo, 1)

        def pe_setup(pe):
            pe.wait_ge(raw_in, 16 * len(RAWS))
            pe.wait_ge(consts_in, 16 * len(CONSTS))
            nc.tensor.matmul(pv_bank[:, 0:P], lat32[:, 0:P], lat32[:, P:2 * P], start=True, stop=True).then_inc(m_mm, 1)
            for kq in range(2):
                for hf in range(2):
                    for c in range(NC):
                        mm = nc.tensor.matmul(fold_banks[2 * kq + hf][:, c * C:(c + 1) * C],
                                              raw_rows[:, 2 * kq + hf, c * P:(c + 1) * P], raw_bd[:, kq, :],
                                              start=True, stop=True)
                    mm.then_inc(fold_mm, 1)
            pe.wait_ge(m_ready, 2)
            for c in range(NC):
                for hf in range(2):
                    mm = nc.tensor.matmul(fold_banks[4][:, c * C + hf * P:c * C + (hf + 1) * P],
                                          raw_rows[:, 4 + hf, c * P:(c + 1) * P], l2o_kv2l[:, :, 0:HD],
                                          start=True, stop=True)
            mm.then_inc(fold_mm, 1)
            for k in range(8):
                nc.tensor.matmul(pv_bank[:, k:k + 1], raw_bd[:, k // 4, k % 2 * P:(k % 2 + 1) * P],
                                 small[:, BQKV + k // 2:BQKV + k // 2 + 1], start=True, stop=True)
            for g in range(NGB):
                col = pv_bank[:, 8 + g:9 + g]
                nc.tensor.matmul(col, l2o_kv2l[:, hof(g):hof(g) + GH, :],
                                 small[:, BQKV + 4 + g // 2:BQKV + 5 + g // 2], start=True, stop=False)
                mm = nc.tensor.matmul(col, lat32[:, 2 * P:3 * P], lat32[:, 3 * P:3 * P + 1], start=False, stop=True)
            mm.then_inc(fold_mm, 1)
            pe.wait_ge(bias_ready, 2)

        def pe_transposes(pe, kind, b):
            for c in range(NC):
                bank = bank_to_fill(pe, (kind, b, c))
                for i in range(NT):
                    mm = nc.tensor.transpose(bank[:, i * P:(i + 1) * P], xn[:, i, c * P:(c + 1) * P], ident[:])
                mm.then_inc(filled, 1)

        def pe_norm1(pe, b):
            pe.wait_ge(xn_ready, NT * (norms.index(("norm1", b)) + 1))
            pe_transposes(pe, "xT", b)

        def pe_rope(pe, n):
            pe.wait_ge(xT_hi, NC * (n // 2 + 1))
            pe.wait_ge(xT_lo, NC * (n // 2 + 1))
            if n == 0:
                pe.wait_ge(fold_hi, 5)
                pe.wait_ge(fold_lo, 5)
            for u in (2 * n, 2 * n + 1):
                for s in range(2):
                    bank = bank_to_fill(pe, ("rope", u, s))
                    terms = [(w[:, 1 - u % 2, n % 2, c, s, :], x[:, c, :]) for c in range(NC)
                             for w, x in passes(wlat, xT)]
                    for k, (w, x) in enumerate(terms):
                        mm = nc.tensor.matmul(bank[:], w, x, start=(k == 0), stop=(k == len(terms) - 1))
                    mm.then_inc(filled, 1)

        def pe_latq(pe, g):
            pe.wait_ge(rope_hi, 4 * (g // 2) + 4)
            pe.wait_ge(rope_lo, 4 * (g // 2) + 4)
            if g == 0:
                pe.wait_ge(raw_hi, 2)
                pe.wait_ge(raw_lo, 2)
            bank = bank_to_fill(pe, ("latq", g))
            terms = [(w[:, s, hof(g):hof(g) + GH, :], x[:, s, :]) for s in range(2) for w, x in passes(wqk, qrope)]
            for k, (w, x) in enumerate(terms):
                mm = nc.tensor.matmul(bank[:], w, x, start=(k == 0), stop=(k == len(terms) - 1))
            mm.then_inc(filled, 1)

        def pe_max_tile(pe, n, u):
            i, h0, heads = MAX_TILES[u]
            k = n * NMX + u
            if k >= 2:
                pe.wait_ge(mx_red, k - 1)
            bank, width = mx_banks[k % 2], P * (i + 1)
            for h in range(heads):
                col = h * width
                nc.tensor.matmul(bank[:, col:col + width], qstack[n % 2][0:96, h0 + h, i * P:(i + 1) * P],
                                 kstack[n % 2][0:96, h0 + h, 0:width], start=True, stop=False)
                mm = nc.tensor.matmul(bank[:, col + i * P:col + width], ident_b[:], mask_qk[:], start=False, stop=True)
            mm.then_inc(mx_mm, 1)

        def pe_score_tile(pe, g, u):
            k = g * ST_UNITS + u
            if k >= 3:
                pe.wait_ge(st_exp, k - 2)
            bank = st_banks[k % 3]
            for h, j, col in ST_TILES[u]:
                nc.tensor.matmul(bank[:, col:col + T - P * j], kstack[g % 2][:, h, j * P:(j + 1) * P],
                                 qstack[g % 2][:, h, j * P:T], start=True, stop=False)
                mm = nc.tensor.matmul(bank[:, col:col + P], ident_b[:], mask_kq[:], start=False, stop=True)
            mm.then_inc(st_mm, 1)

        def pe_scores(pe, g):
            n = g + 1
            if n < NG:
                wait_stack(pe, n)
            if g >= 0:
                pe.wait_ge(maxrow_in[g % 2], 16 * NT * (g // 2 + 1))
            if g == 0:
                pe.wait_ge(dve_init, 3)
            for u in range(max(ST_UNITS, NMX)):
                if g >= 0 and u < ST_UNITS:
                    pe_score_tile(pe, g, u)
                if n < NG and u < NMX:
                    pe_max_tile(pe, n, u)
            if n < NG:
                bank = bank_to_fill(pe, ("maxT", n))
                pe.wait_ge(mx_red, NMX * (n + 1))
                nc.tensor.transpose(bank[0:NT * GH, 0:P], rowmax[:], ident[:]).then_inc(filled, 1)

        def pe_values(pe, g):
            pe.wait_ge(st_exp, ST_UNITS * (g + 1))
            if g % NGB == 0:
                pe.wait_ge(val_ready, NT // 2 * (g // NGB + 1))
            if g >= 1:
                pe.wait_ge(yn_ready, g)
            where = {(h, j): (u, col) for u in range(ST_UNITS) for h, j, col in ST_TILES[u]}
            for j in range(NT):
                for h in range(GH):
                    u, col = where[(h, j)]
                    mm = nc.tensor.matmul(pv_bank[32 * h:32 * h + 32, j * P:T], val[:, j, g % NGB * GH + h, :],
                                          probs[:, (g * ST_UNITS + u) % P_SLOTS, col:col + T - P * j],
                                          start=(j == 0), stop=(j == NT - 1))
            mm.then_inc(pv_mm, 1)

        def pe_token_rows(pe, kind, b, chunks, lhs, w):
            for i in range(NT // 2):
                bank = bank_to_fill(pe, (kind, b, i))
                for t in range(2):
                    tok = (2 * i + t) * P
                    terms = [(x[:, c, tok:tok + P], y[:, c, :]) for c in range(chunks) for x, y in passes(lhs, w)]
                    for k, (x, y) in enumerate(terms):
                        mm = nc.tensor.matmul(bank[:, t * C:(t + 1) * C], x, y, start=(k == 0),
                                              stop=(k == len(terms) - 1))
                mm.then_inc(filled, 1)

        def pe_vproj(pe, b):
            pe_token_rows(pe, "vproj", b, NC, xT, wval)

        def pe_cproj(pe, b):
            pe.wait_ge(y_hi, NGB * (b + 1))
            pe.wait_ge(y_lo, NGB * (b + 1))
            pe_token_rows(pe, "cproj", b, NGB, yT, wcp)

        def pe_tail(pe, b):
            pe.wait_ge(xn_ready, NT * (norms.index(("tail", b)) + 1))
            pe_transposes(pe, "x2T", b)
            pe.wait_ge(x2T_ready, NC * (b + 1))
            bank = bank_to_fill(pe, ("router", b))
            for i in range(NT):
                tok = b * T + i * P
                for c in range(NC):
                    mm = nc.tensor.matmul(bank[:, i * NE:(i + 1) * NE], x2T[:, c, tok:tok + P], router_w[:, c, :],
                                          start=(c == 0), stop=(c == NC - 1))
            mm.then_inc(filled, 1)

        def act_setup(act):
            act.wait_ge(raw_in, 16 * len(RAWS))
            nc.scalar.copy(wqk[0][:].rearrange("p s h l -> p (s h l)"), raw_wqk).then_inc(raw_hi, 1)
            nc.scalar.copy(wcp[0][:].rearrange("p g c -> p (g c)"), raw_wcp).then_inc(raw_hi, 1)
            for k in range(5):
                act.wait_ge(fold_mm, k + 1)
                nc.scalar.copy(folded(0, k), fold_banks[k][:]).then_inc(fold_hi, 1)
            act.wait_ge(consts_in, 16 * len(CONSTS))
            nc.scalar.copy(onehot[:], onehot_raw[:])

        def folded(part, k):
            return wlat[part][:, k // 2, k % 2, :, :, :].rearrange("p c s r -> p (c s r)") if k < 4 else \
                wval[part][:].rearrange("p c n -> p (c n)")

        def act_norm1(act, b):
            if b >= 1:
                act.wait_ge(filled, fills[("vproj", b - 1, NT // 2 - 1)] + 1)
            for c in range(NC):
                bank = filled_bank(act, ("xT", b, c))
                nc.scalar.copy(xT[0][:, c, :], bank[:]).then_inc(xT_hi, 1)

        def act_rope(act, n):
            for u in (2 * n, 2 * n + 1):
                kq = 1 - u % 2
                for s in range(2):
                    act.wait_ge(sum_roped, 2 * u + s + 1)
                    if s == 0 and n >= 1:
                        if kq:
                            wait_stack(act, 2 * n - 1)
                        else:
                            act.wait_ge(filled, fills[("latq", 2 * n - 1)] + 1)
                    nc.scalar.copy((krope_hi if kq else qrope[0])[:, s, :], roped[:, kq, s, :]).then_inc(rope_hi, 1)

        def act_latq(act, g):
            if g == 0:
                act.wait_ge(consts_in, 16 * len(CONSTS))
            else:
                wait_stack(act, g - 1)
            bank = filled_bank(act, ("latq", g))
            nc.scalar.activation(qlat[0][:], bank[:], ACT.Identity, bias=small[:, WQKB:WQKB + 1]).then_inc(latq_hi, 1)

        def act_scores(act, g):
            if g < 0:
                return
            for u in range(ST_UNITS):
                k = g * ST_UNITS + u
                act.wait_ge(st_mm, k + 1)
                if k >= P_SLOTS:
                    act.wait_ge(pv_mm, (k - P_SLOTS) // ST_UNITS + 1)
                nc.scalar.activation(probs[:, k % P_SLOTS, :], st_banks[k % 3][:], ACT.Exp,
                                     scale=SCORE_SCALE).then_inc(st_exp, 1)

        def act_values(act, g):
            b = g // NGB
            act.wait_ge(yn_ready, g + 1)
            if g % NGB == 0 and b >= 1:
                act.wait_ge(filled, fills[("cproj", b - 1, NT // 2 - 1)] + 1)
            if g == 0:
                act.wait_ge(bias_ready, 2)
            nc.scalar.activation(yT[0][:, g % NGB, :], yn[:], ACT.Identity,
                                 bias=vconst[:, g % NGB:g % NGB + 1]).then_inc(y_hi, 1)

        def act_vproj(act, b):
            if b == 0:
                act.wait_ge(dve_init, 3)
            else:
                act.wait_ge(pv_mm, NGB * b)
            for i in range(NT // 2):
                bank = filled_bank(act, ("vproj", b, i))
                nc.scalar.copy(val[:, 2 * i:2 * i + 2, :, 0:HD],
                               bank[:].rearrange("p (t h d) -> p t h d", t=2, h=NH)).then_inc(val_ready, 1)

        def act_tail(act, b):
            for c in range(NC):
                bank = filled_bank(act, ("x2T", b, c))
                nc.scalar.copy(x2T[:, c, b * T:(b + 1) * T], bank[:]).then_inc(x2T_ready, 1)
            bank = filled_bank(act, ("router", b))
            if b >= 1:
                act.wait_ge(comb_ready, b)
            nc.scalar.activation(rt[:, 0, :], bank[:, 0:NT * NE], ACT.Sigmoid).then_inc(sig_ready, 1)

        def dve_setup(dve):
            nc.vector.memset(val[:, :, :, HD:L], 1.0).then_inc(dve_init, 1)
            for p in range(2):
                nc.vector.memset(kstack[p][96:97, :, :].bitcast(F32), -1.0).then_inc(dve_init, 1)
            nc.vector.memset(l2o_kv2l, 0.0).then_inc(m_ready, 1)
            dve.wait_ge(consts_in, 16 * len(CONSTS))
            dve.wait_ge(m_mm, 1)
            dve.wait_ge(m_ready, 1)
            nc.vector.tensor_tensor(l2o_kv2l[:, :, 0:HD], pv_bank[:, 0:P].rearrange("p (h d) -> p h d", h=HALF),
                                    block_mask.rearrange("p (h d) -> p h d", h=HALF), ALU.mult).then_inc(m_ready, 1)
            dve.wait_ge(raw_in, 16 * len(RAWS))
            for k, (w, src) in enumerate(((wqk, raw_wqk), (wcp, raw_wcp))):
                dve.wait_ge(raw_hi, k + 1)
                pat = "p s h l -> p (s h l)" if k == 0 else "p g c -> p (g c)"
                nc.vector.tensor_tensor(w[1][:].rearrange(pat), src, w[0][:].rearrange(pat).bitcast(F32),
                                        ALU.subtract).then_inc(raw_lo, 1)
            for k in range(5):
                dve.wait_ge(fold_hi, k + 1)
                nc.vector.tensor_tensor(folded(1, k), fold_banks[k][:], folded(0, k).bitcast(F32),
                                        ALU.subtract).then_inc(fold_lo, 1)
            dve.wait_ge(fold_mm, 6)
            lat_b = small[:, LATB:LATB + 4].rearrange("p (x s) -> p x s", x=2).unsqueeze(2).broadcast_to([P, 2, 2, 2])
            nc.vector.tensor_tensor(blat[:].rearrange("p (x f s) -> p x f s", x=2, f=2),
                                    pv_bank[:, 0:8].rearrange("p (x f s) -> p x f s", x=2, f=2), lat_b,
                                    ALU.add).then_inc(bias_ready, 1)
            nc.vector.tensor_scalar(vconst[:], pv_bank[:, 8:8 + NGB], small[:, L2OB:L2OB + 1], None,
                                    ALU.add).then_inc(bias_ready, 1)

        def dve_layernorm(dve, m, b):
            for i in range(NT):
                nc.vector.bn_stats(stats[:, i, :], h_all[:, b * NT + i, :]).then_inc(ln_stats, 1)
            for i in range(NT):
                dve.wait_ge(ln_stats, NT * m + i + 1)
                if m >= 1 and i == 0:
                    dve.wait_ge(ln_rstd, m)
                nc.vector.bn_aggr(meanvar[:, i, :], stats[:, i, :]).then_inc(ln_aggr, 1)
            dve.wait_ge(ln_aggr, NT * (m + 1))
            dve.wait_ge(ln_rstd, m + 1)
            for i in range(NT):
                nc.vector.tensor_scalar(xn[:, i, :], h_all[:, b * NT + i, :], meanvar[:, i, 0:1], rstd[:, i:i + 1],
                                        ALU.subtract, ALU.mult).then_inc(xn_ready, 1)

        def wait_xn_used(eng, m):
            kind, b = norms[m]
            eng.wait_ge(filled, fills[("xT" if kind == "norm1" else "x2T", b, NC - 1)] + 1)

        def dve_norm1(dve, b):
            m = norms.index(("norm1", b))
            dve.wait_ge(h_ready, b + 1)
            if m >= 1:
                wait_xn_used(dve, m - 1)
            dve_layernorm(dve, m, b)
            if b >= 1:
                dve.wait_ge(filled, fills[("vproj", b - 1, NT // 2 - 1)] + 1)
            for c in range(NC):
                bank = filled_bank(dve, ("xT", b, c))
                dve.wait_ge(xT_hi, NC * b + c + 1)
                nc.vector.tensor_tensor(xT[1][:, c, :], bank[:], xT[0][:, c, :].bitcast(F32),
                                        ALU.subtract).then_inc(xT_lo, 1)

        def dve_rope(dve, n):
            if n == 0:
                dve.wait_ge(bias_ready, 2)
            for u in (2 * n, 2 * n + 1):
                if u >= 1:
                    dve.wait_ge(sum_roped, 2 * u)
                for s in range(2):
                    bank = filled_bank(dve, ("rope", u, s))
                    k = 4 * (1 - u % 2) + 2 * (n % 2) + s
                    for slot, table in (((0, rope_cos), (3, rope_sin)), ((1, rope_sin), (2, rope_cos)))[s]:
                        nc.vector.scalar_tensor_tensor(out=prod[:, slot, :], in0=bank[:], scalar=blat[:, k:k + 1],
                                                       in1=table[:], op0=ALU.add,
                                                       op1=ALU.mult).then_inc(prod_ready, 1)

        def dve_latq(dve, g):
            if g >= 1:
                wait_stack(dve, g - 1)
            bank = filled_bank(dve, ("latq", g))
            dve.wait_ge(latq_hi, g + 1)
            nc.vector.scalar_tensor_tensor(out=qlat[1][:], in0=bank[:], scalar=small[:, WQKB:WQKB + 1],
                                           in1=qlat[0][:].bitcast(F32), op0=ALU.add,
                                           op1=ALU.subtract).then_inc(latq_lo, 1)

        def dve_scores(dve, g):
            n = g + 1
            if n >= NG:
                return
            if n >= 1:
                dve.wait_ge(filled, fills[("maxT", n - 1)] + 1)
            for u, (i, h0, heads) in enumerate(MAX_TILES):
                k = n * NMX + u
                dve.wait_ge(mx_mm, k + 1)
                width = P * (i + 1)
                nc.vector.tensor_reduce(rowmax[:, i * GH + h0:i * GH + h0 + heads],
                                        mx_banks[k % 2][:, 0:heads * width].rearrange("p (h w) -> p h w", h=heads),
                                        AX_X, ALU.max).then_inc(mx_red, 1)
            bank = filled_bank(dve, ("maxT", n))
            if n >= 1:
                dve.wait_ge(maxrow_in[(n - 1) % 2], 16 * NT * ((n - 1) // 2 + 1))
            nc.vector.tensor_copy(rowmaxT[:], bank[0:NT * GH, 0:P]).then_inc(maxT_ready, 1)

        def dve_values(dve, g):
            dve.wait_ge(pv_mm, g + 1)
            if g >= 1:
                dve.wait_ge(yn_ready, g)
            if g >= 1:
                dve.wait_ge(y_hi, g)
                dve.wait_ge(y_lo, g)
            nc.vector.stream_shuffle(yn[:], pv_bank[:], [HD] * 32).then_inc(den_ready, 1)
            dve.wait_ge(den_ready, g + 1)
            nc.vector.reciprocal(yn[:], yn[:]).then_inc(rden_ready, 1)
            dve.wait_ge(rden_ready, g + 1)
            nc.vector.tensor_tensor(yn[:], pv_bank[:], yn[:], ALU.mult).then_inc(yn_ready, 1)
            dve.wait_ge(y_hi, g + 1)
            nc.vector.scalar_tensor_tensor(out=yT[1][:, g % NGB, :], in0=yn[:], scalar=vconst[:, g % NGB:g % NGB + 1],
                                           in1=yT[0][:, g % NGB, :].bitcast(F32), op0=ALU.add,
                                           op1=ALU.subtract).then_inc(y_lo, 1)

        def dve_cproj(dve, b):
            dve.wait_ge(h_biased, NT * (b + 1))
            for i in range(NT // 2):
                bank = filled_bank(dve, ("cproj", b, i))
                rows = h_all[:, b * NT + 2 * i:b * NT + 2 * i + 2, :].rearrange("p t c -> p (t c)")
                nc.vector.tensor_tensor(rows, bank[:], rows, ALU.add).then_inc(h2_ready, 1)

        def dve_tail(dve, b):
            m = norms.index(("tail", b))
            dve.wait_ge(h2_ready, NT // 2 * (b + 1))
            wait_xn_used(dve, m - 1)
            dve_layernorm(dve, m, b)
            dve.wait_ge(sig_ready, b + 1)
            dve_route(dve, b)

        def dve_route(dve, b):
            count = [ROUTE_OPS * b]

            def after(ins):
                count[0] += 1
                ins.then_inc(routed, 1)
                return count[0]

            v = nc.vector
            score, sc, masked, gt4, eq4, prefix, chosen = (rt[:, k, :] for k in range(7))
            a1, a2 = rt[:, 7, :], rt[:, 8, :]
            hi2, lo2 = rt[:, 9, 0:32], rt[:, 9, 32:64]
            top1, mid, low, gsum = (rt[:, 10, 16 * k:16 * k + 16] for k in range(4))
            gmask, top8 = rt[:, 11, 0:16], rt[:, 11, 16:48]
            above, wsum = rt[:, 11, 48:52], rt[:, 11, 52:56]
            rank = rt[:, 11, 56:64]
            n = after(v.tensor_tensor(sc, score, ebias[:], ALU.add))
            dve.wait_ge(routed, n)
            pairs = sc.rearrange("p (g a two) -> p g a two", a=2, two=2)
            h2v, l2v = (x.rearrange("p (g a) -> p g a", a=2) for x in (hi2, lo2))
            after(v.tensor_tensor(h2v, pairs[:, :, :, 0], pairs[:, :, :, 1], ALU.max))
            n = after(v.tensor_tensor(l2v, pairs[:, :, :, 0], pairs[:, :, :, 1], ALU.min))
            dve.wait_ge(routed, n)
            after(v.tensor_tensor(top1, h2v[:, :, 0], h2v[:, :, 1], ALU.max))
            after(v.tensor_tensor(mid, h2v[:, :, 0], h2v[:, :, 1], ALU.min))
            n = after(v.tensor_tensor(low, l2v[:, :, 0], l2v[:, :, 1], ALU.max))
            dve.wait_ge(routed, n)
            n = after(v.tensor_tensor(mid, mid, low, ALU.max))
            dve.wait_ge(routed, n)
            n = after(v.tensor_tensor(gsum, top1, mid, ALU.add))
            dve.wait_ge(routed, n)
            gs = gsum.rearrange("p (t g) -> p t g", t=NT)
            gs_j = gs.unsqueeze(2).broadcast_to([P, NT, NGRP, NGRP])
            gs_i = gs.unsqueeze(3).broadcast_to([P, NT, NGRP, NGRP])
            q4 = "p (t i j) -> p t i j"
            a1v, a2v = a1.rearrange(q4, t=NT, i=NGRP), a2.rearrange(q4, t=NT, i=NGRP)
            after(v.tensor_tensor(a1v, gs_j, gs_i, ALU.is_gt))
            n = after(v.tensor_tensor(a2v, gs_j, gs_i, ALU.is_equal))
            dve.wait_ge(routed, n)
            n = after(v.tensor_tensor(a2v, a2v, earlier[:], ALU.mult))
            dve.wait_ge(routed, n)
            n = after(v.tensor_tensor(a1, a1, a2, ALU.add))
            dve.wait_ge(routed, n)
            n = after(v.tensor_reduce(top1, a1.rearrange("p (x j) -> p x j", j=NGRP), AX_X, ALU.add))
            dve.wait_ge(routed, n)
            n = after(v.tensor_scalar(gmask, top1, 2.0, None, ALU.is_lt))
            dve.wait_ge(routed, n)
            by_group = "p (x e) -> p x e"
            n = after(v.tensor_tensor(masked.rearrange(by_group, e=EPG), sc.rearrange(by_group, e=EPG),
                                      gmask.unsqueeze(2).broadcast_to([P, NT * NGRP, EPG]), ALU.mult))
            dve.wait_ge(routed, n)
            for t in range(NT):
                n = after(v.max(top8[:, 8 * t:8 * t + 8], masked[:, t * NE:(t + 1) * NE]))
            dve.wait_ge(routed, n)
            row = "p (t e) -> p t e"
            fourth = top8.rearrange("p (t k) -> p t k", t=NT)[:, :, TOPK - 1:TOPK].broadcast_to([P, NT, NE])
            after(v.tensor_tensor(gt4.rearrange(row, t=NT), masked.rearrange(row, t=NT), fourth, ALU.is_gt))
            n = after(v.tensor_tensor(eq4.rearrange(row, t=NT), masked.rearrange(row, t=NT), fourth, ALU.is_equal))
            dve.wait_ge(routed, n)
            after(v.tensor_reduce(above, gt4.rearrange(row, t=NT), AX_X, ALU.add))
            n = after(v.tensor_tensor_scan(prefix, same_row[:], eq4, 0.0, ALU.mult, ALU.add))
            dve.wait_ge(routed, n)
            n = after(v.tensor_tensor(a1.rearrange(row, t=NT), prefix.rearrange(row, t=NT),
                                      above.unsqueeze(2).broadcast_to([P, NT, NE]), ALU.add))
            dve.wait_ge(routed, n)
            n = after(v.scalar_tensor_tensor(out=a2, in0=a1, scalar=float(TOPK), in1=eq4, op0=ALU.is_le,
                                             op1=ALU.mult))
            dve.wait_ge(routed, n)
            n = after(v.tensor_tensor(chosen, gt4, a2, ALU.add))
            dve.wait_ge(routed, n)
            n = after(v.tensor_tensor(a1, score, chosen, ALU.mult))
            dve.wait_ge(routed, n)
            n = after(v.tensor_reduce(wsum, a1.rearrange(row, t=NT), AX_X, ALU.add))
            dve.wait_ge(routed, n)
            n = after(v.tensor_scalar(wsum, wsum, 1e-20, None, ALU.add))
            dve.wait_ge(routed, n)
            n = after(v.reciprocal(wsum, wsum))
            dve.wait_ge(routed, n)
            assert count[0] == ROUTE_OPS * (b + 1), count
            v.scalar_tensor_tensor(out=comb[:, b, :].rearrange(row, t=NT), in0=a1.rearrange(row, t=NT),
                                   scalar=ROUTE_SCALE, in1=wsum.unsqueeze(2).broadcast_to([P, NT, NE]),
                                   op0=ALU.mult, op1=ALU.mult).then_inc(comb_ready, 1)

        def nothing(eng, n):
            pass

        STAGES = {
            "sp": dict(latq=sp_latq, scores=sp_scores),
            "pool": dict(norm1=pool_norm1, tail=pool_tail, rope=pool_rope),
            "pe": dict(norm1=pe_norm1, rope=pe_rope, latq=pe_latq, scores=pe_scores, values=pe_values,
                       vproj=pe_vproj, cproj=pe_cproj, tail=pe_tail),
            "act": dict(norm1=act_norm1, rope=act_rope, latq=act_latq, scores=act_scores, values=act_values,
                        vproj=act_vproj, tail=act_tail),
            "dve": dict(norm1=dve_norm1, rope=dve_rope, latq=dve_latq, scores=dve_scores, values=dve_values,
                        cproj=dve_cproj, tail=dve_tail),
        }

        def attention(eng, engine):
            for kind, n in steps:
                STAGES[engine].get(kind, nothing)(eng, n)

        att.close()
        moe = ctx.enter_context(ExitStack())
        wex = pair(moe, "wex", [P, NX, WCOLS])
        wstage = [sb(moe, f"wstage{i}", [P, WCOLS]) for i in range(2)]
        xs = [pair(moe, f"xs{p}", [P, NC, T]) for p in range(2)]
        combT = [sb(moe, f"combT{p}", [48, T], F32R) for p in range(2)]
        gated = [sb(moe, f"gated{p}", [P, T]) for p in range(2)]
        hid = [sb(moe, f"hid{p}", [P, T]) for p in range(2)]
        hidr = [pair(moe, f"hidr{p}", [P, T]) for p in range(2)]
        ysb = sb(moe, "ysb", [P, NC, T])
        outbuf = [sb(moe, f"outbuf{i}", [P, 2, C]) for i in range(2)]
        gate_banks, up_banks, y_banks, spread_bank, misc_bank = banks[0:2], banks[2:4], banks[4:6], banks[6], banks[7]
        order = [NE + s for s in range(NSH)] + list(range(NE))
        NS = B * NX
        routed_before = [sum(order[k % NX] < NE for k in range(n)) for n in range(NS + 1)]

        def sp_moe(sp):
            sp.wait_ge(att_done, 4)
            for e in range(NX):
                if e >= 2:
                    sp.wait_ge(ex_hi, e - 1)
                    sp.wait_ge(ex_lo, e - 1)
                sp.dma_start(wstage[e % 2][:], io["experts"][order[e]]).then_inc(wstage_in[e % 2], 16)
            for k in range(B * NT // 2):
                sp.wait_ge(sum_ready, k + 1)
                b, i = k // 2, k % 2
                sp.dma_start(io["out"][b].rearrange("(i t p) c -> i p t c", t=2, p=P)[i],
                             outbuf[i][:]).then_inc(out_done[i], 16)
            for i in range(2):
                sp.wait_ge(out_done[i], 16 * B)

        def pe_moe(pe):
            def transposed_weights(b):
                pe.wait_ge(comb_ready, b + 1)
                if b >= 1:
                    pe.wait_ge(sum_ready, 2 * (b - 1))
                    pe.wait_ge(combT_hi, b)
                    pe.wait_ge(combT_lo, b)
                for i in range(NT):
                    mm = nc.tensor.transpose(misc_bank[0:NE, i * P:(i + 1) * P], comb[:, b, i * NE:(i + 1) * NE],
                                             ident[:])
                mm.then_inc(combT_mm, 1)

            def gate_up(n):
                b, k = n // NX, n % NX
                if k == 0:
                    pe.wait_ge(xs_hi, NC * (b + 1))
                    pe.wait_ge(xs_lo, NC * (b + 1))
                if b == 0:
                    pe.wait_ge(ex_hi, k + 1)
                    pe.wait_ge(ex_lo, k + 1)
                if n >= 2:
                    pe.wait_ge(silu_ready, n - 1)
                    pe.wait_ge(hid_ready, n - 1)
                for bank, first, done in ((gate_banks[n % 2], 0, gate_mm), (up_banks[n % 2], NC * I, up_mm)):
                    terms = [(w[:, k, first + c * I:first + (c + 1) * I], x[:, c, :]) for c in range(NC)
                             for w, x in passes(wex, xs[b % 2])]
                    for j, (w, x) in enumerate(terms):
                        mm = nc.tensor.matmul(bank[:], w, x, start=(j == 0), stop=(j == len(terms) - 1))
                    mm.then_inc(done, 1)

            def spread(n):
                b, e = n // NX, order[n % NX]
                if e >= NE:
                    return
                r = routed_before[n]
                if e == 0:
                    pe.wait_ge(combT_hi, b + 1)
                    pe.wait_ge(combT_lo, b + 1)
                if r >= 1:
                    pe.wait_ge(weighted, r)
                nc.tensor.matmul(spread_bank[:], onehot[:, e:e + 1].broadcast_to([48, P]), combT[b % 2][:],
                                 start=True, stop=True).then_inc(spread_mm, 1)

            def down(n):
                b, k = n // NX, n % NX
                pe.wait_ge(hid_hi, n + 1)
                pe.wait_ge(hid_lo, n + 1)
                if k == 0 and b >= 1:
                    for c in range(NC):
                        pe.wait_ge(y_copied[c], b)
                for c in range(NC):
                    cols = 2 * NC * I + c * P
                    for j, (w, x) in enumerate(passes(wex, hidr[n % 2])):
                        mm = nc.tensor.matmul(y_banks[c][:], w[:, k, cols:cols + P], x[:], start=(k == 0 and j == 0),
                                              stop=(k == NX - 1 and j == 2))
                mm.then_inc(down_mm, 1)

            def rows_back(b, i):
                if i == 0:
                    for c in range(NC):
                        pe.wait_ge(y_copied[c], b + 1)
                    pe.wait_ge(combT_hi, min(b + 2, B))
                    pe.wait_ge(combT_lo, min(b + 2, B))
                if i == 1 or b >= 1:
                    pe.wait_ge(sum_ready, 2 * b + i)
                for t in range(2):
                    for c in range(NC):
                        tok = (2 * i + t) * P
                        mm = nc.tensor.transpose(misc_bank[:, t * C + c * P:t * C + (c + 1) * P],
                                                 ysb[:, c, tok:tok + P], ident[:])
                mm.then_inc(yback_mm, 1)

            transposed_weights(0)
            for n in range(NS):
                gate_up(n)
                spread(n)
                if n >= 1:
                    down(n - 1)
                if n % NX == NX - 4 and n // NX + 1 < B:
                    transposed_weights(n // NX + 1)
                if n % NX in (2, 4) and n >= NX:
                    rows_back(n // NX - 1, n % NX // 2 - 1)
            down(NS - 1)
            for i in range(2):
                rows_back(B - 1, i)

        def act_moe(act):
            def load_x(b):
                if b >= 2:
                    act.wait_ge(up_mm, NX * (b - 1))
                for c in range(NC):
                    nc.scalar.copy(xs[b % 2][0][:, c, :], x2T[:, c, b * T:(b + 1) * T]).then_inc(xs_hi, 1)
                act.wait_ge(combT_mm, b + 1)
                if b == 0:
                    act.wait_ge(combT_init, 2)
                if b >= 2:
                    act.wait_ge(spread_mm, NE * (b - 1))
                nc.scalar.copy(combT[b % 2][0:NE, :], misc_bank[0:NE, :]).then_inc(combT_hi, 1)

            act.wait_ge(att_done, 4)
            for n in range(NS + 1):
                b, k = n // NX, n % NX
                if n == 0:
                    load_x(0)
                if b == 0 and n < NX:
                    act.wait_ge(wstage_in[n % 2], 16 * (n // 2 + 1))
                    nc.scalar.copy(wex[0][:, n, :], wstage[n % 2][:]).then_inc(ex_hi, 1)
                if n < NS:
                    act.wait_ge(gate_mm, n + 1)
                    if n >= 2:
                        act.wait_ge(hid_ready, n - 1)
                    nc.scalar.activation(gated[n % 2][:], gate_banks[n % 2][:], ACT.Silu).then_inc(silu_ready, 1)
                if n >= 1:
                    act.wait_ge(hid_ready, n)
                    if n >= 3:
                        act.wait_ge(down_mm, n - 2)
                    nc.scalar.copy(hidr[(n - 1) % 2][0][:], hid[(n - 1) % 2][:]).then_inc(hid_hi, 1)
                if n < NS and k == NX - 4 and b + 1 < B:
                    load_x(b + 1)
                if n >= NX and k == 0 and n < NS:
                    copy_y(act, nc.scalar.copy, b - 1, 0)
            copy_y(act, nc.scalar.copy, B - 1, 0)

        def copy_y(eng, copy, b, c):
            eng.wait_ge(down_mm, NX * (b + 1))
            if b >= 1:
                eng.wait_ge(yback_mm, 2 * b)
            copy(ysb[:, c, :], y_banks[c][:]).then_inc(y_copied[c], 1)

        def dve_moe(dve):
            def load_x(b):
                if b >= 2:
                    dve.wait_ge(up_mm, NX * (b - 1))
                for c in range(NC):
                    dve.wait_ge(xs_hi, NC * b + c + 1)
                    nc.vector.tensor_tensor(xs[b % 2][1][:, c, :], x2T[:, c, b * T:(b + 1) * T],
                                            xs[b % 2][0][:, c, :].bitcast(F32), ALU.subtract).then_inc(xs_lo, 1)
                dve.wait_ge(combT_hi, b + 1)
                nc.vector.tensor_tensor(combT[b % 2][32:32 + NE, :], misc_bank[0:NE, :],
                                        combT[b % 2][0:NE, :].bitcast(F32), ALU.subtract).then_inc(combT_lo, 1)

            def split_weights(e):
                dve.wait_ge(ex_hi, e + 1)
                nc.vector.tensor_tensor(wex[1][:, e, :], wstage[e % 2][:], wex[0][:, e, :].bitcast(F32),
                                        ALU.subtract).then_inc(ex_lo, 1)

            def add_rows(b, i):
                dve.wait_ge(yback_mm, 2 * b + i + 1)
                if b >= 1:
                    dve.wait_ge(out_done[i], 16 * b)
                rows = h_all[:, b * NT + 2 * i:b * NT + 2 * i + 2, :].rearrange("p t c -> p (t c)")
                nc.vector.tensor_tensor(outbuf[i][:].rearrange("p t c -> p (t c)"), misc_bank[:], rows,
                                        ALU.add).then_inc(sum_ready, 1)

            dve.wait_ge(att_done, 4)
            for p in range(2):
                nc.vector.memset(combT[p][:].bitcast(F32), 0.0).then_inc(combT_init, 1)
            dve.wait_ge(combT_init, 2)
            load_x(0)
            split_weights(0)
            for n in range(NS):
                b, k = n // NX, n % NX
                dve.wait_ge(silu_ready, n + 1)
                if order[k] < NE:
                    dve.wait_ge(spread_mm, routed_before[n] + 1)
                    nc.vector.tensor_tensor(gated[n % 2][:], gated[n % 2][:], spread_bank[:],
                                            ALU.mult).then_inc(weighted, 1)
                    dve.wait_ge(weighted, routed_before[n] + 1)
                dve.wait_ge(up_mm, n + 1)
                if n >= 2:
                    dve.wait_ge(hid_hi, n - 1)
                    dve.wait_ge(hid_lo, n - 1)
                nc.vector.tensor_tensor(hid[n % 2][:], up_banks[n % 2][:], gated[n % 2][:],
                                        ALU.mult).then_inc(hid_ready, 1)
                if n + 1 < NX:
                    split_weights(n + 1)
                dve.wait_ge(hid_hi, n + 1)
                nc.vector.tensor_tensor(hidr[n % 2][1][:], hid[n % 2][:], hidr[n % 2][0][:].bitcast(F32),
                                        ALU.subtract).then_inc(hid_lo, 1)
                if k == NX - 4 and b + 1 < B:
                    load_x(b + 1)
                if n >= NX and k == 0 and n < NS:
                    copy_y(dve, nc.vector.tensor_copy, b - 1, 1)
                if n >= NX and k in (2, 4):
                    add_rows(b - 1, k // 2 - 1)
            copy_y(dve, nc.vector.tensor_copy, B - 1, 1)
            for i in range(2):
                add_rows(B - 1, i)

        block = ctx.enter_context(nc.Block())

        @block.sync
        def _(sp):
            sp_setup(sp)
            attention(sp, "sp")
            sp_moe(sp)

        @block.gpsimd
        def _(pool):
            pool_setup(pool)
            attention(pool, "pool")
            pool.wait_ge(ln_rstd, len(norms))
            nc.gpsimd.memset(neghalf[:], 0.0).then_inc(att_done, 1)

        @block.tensor
        def _(pe):
            pe_setup(pe)
            attention(pe, "pe")
            nc.tensor.transpose(misc_bank[0:NE, 0:P], comb[:, 0, 0:NE], ident[:]).then_inc(att_done, 1)
            pe_moe(pe)

        @block.scalar
        def _(act):
            act_setup(act)
            attention(act, "act")
            nc.scalar.copy(rstd[:, 0:1], small[:, 0:1]).then_inc(att_done, 1)
            act_moe(act)

        @block.vector
        def _(dve):
            dve_setup(dve)
            attention(dve, "dve")
            dve.wait_ge(comb_ready, B)
            nc.vector.memset(yn[:, 0:1], 0.0).then_inc(att_done, 1)
            dve_moe(dve)


ROUTE_OPS = 30


def kernel(x, L0_tok_emb, L0_attn_c_attn_w, L0_attn_c_attn_b, L0_attn_q2l_w, L0_attn_q2l_b, L0_attn_kv2l_w,
           L0_attn_kv2l_b, L0_attn_l2o_w, L0_attn_l2o_b, L0_attn_wqk_w, L0_attn_wqk_b, L0_attn_cproj_w,
           L0_attn_cproj_b, L0_ffn_router_weight, L0_ffn_e_bias, L0_ffn_gate_w, L0_ffn_up_w, L0_ffn_down_w,
           L0_ffn_sh_gate_w, L0_ffn_sh_up_w, L0_ffn_sh_down_w):
    import concourse.bacc as bacc
    import ml_dtypes
    from concourse.bass_utils import run_bass_kernel_spmd

    f4 = np.float32
    arr = {}
    arr["tok"] = np.ascontiguousarray(np.asarray(x).reshape(B * NT, P).T)
    arr["emb"] = np.asarray(L0_tok_emb)

    pos = np.arange(T, dtype=f4)[:, None]
    col = np.arange(C)
    angle = pos / np.power(f4(10000.0), (2 * (col // 2)).astype(f4) / f4(C)).astype(f4)
    table = np.where(col % 2 == 0, np.sin(angle), np.cos(angle)).astype(f4)
    arr["pos_enc"] = np.ascontiguousarray(table.reshape(NT, P, C).transpose(1, 0, 2))
    inv_freq = (f4(1.0) / np.power(f4(10000.0), np.arange(0, L, 2, dtype=f4) / f4(L))).astype(f4)
    freqs = np.outer(np.arange(T, dtype=f4), inv_freq).astype(f4)
    arr["rope_cos"] = np.ascontiguousarray(np.tile(np.cos(freqs).T, (HALF, 1)).astype(f4))
    arr["rope_sin"] = np.ascontiguousarray(np.tile(np.sin(freqs).T, (HALF, 1)).astype(f4))
    arr["ident"] = np.eye(P, dtype=f4)
    arr["ident_b"] = np.eye(P).astype(ml_dtypes.bfloat16)
    later = np.tril(np.ones((P, P), f4), -1) * f4(-1e30)
    arr["mask_kq"] = later.astype(ml_dtypes.bfloat16)
    arr["mask_qk"] = np.ascontiguousarray(later.T).astype(ml_dtypes.bfloat16)
    arr["block_mask"] = np.kron(np.eye(HALF), np.ones((HD, HD))).astype(f4)
    same = np.ones((P, NT, NE), f4)
    same[:, :, 0] = 0
    arr["same_row"] = same.reshape(P, NT * NE)
    arr["earlier"] = np.ascontiguousarray(
        np.broadcast_to(np.tril(np.ones((NGRP, NGRP), f4), -1), (P, NT, NGRP, NGRP)))
    onehot = np.zeros((48, NE), f4)
    onehot[0:NE] = onehot[32:48] = np.eye(NE)
    arr["onehot"] = onehot

    bqkv, wq2l, wkv2l = (np.asarray(a) for a in (L0_attn_c_attn_b, L0_attn_q2l_w, L0_attn_kv2l_w))
    arr["c_attn_rows"] = np.ascontiguousarray(np.asarray(L0_attn_c_attn_w).reshape(6, P, C).transpose(1, 0, 2))
    bd = np.zeros((HALF, HD, 2, 2, HALF, HD), f4)
    for h in range(HALF):
        for k, w in enumerate((wq2l, wkv2l)):
            for s in range(2):
                bd[h, :, k, s, h, :] = w[s::2].T
    arr["lat_bd"] = bd.reshape(P, 2, 2 * P)
    perm = np.concatenate([np.arange(0, L, 2), np.arange(1, L, 2)])
    wqk = np.asarray(L0_attn_wqk_w)
    qk = np.zeros((HALF, HD, 2, HALF, L), f4)
    for h in range(HALF):
        for s in range(2):
            qk[h, :, s, h, :] = wqk[perm][:, s::2].T
    arr["wqk_bd"] = qk.reshape(P, 2 * HALF * L)
    cp = np.zeros((GH, L, NGB, C), f4)
    cp[:, 0:HD] = np.asarray(L0_attn_cproj_w).reshape(C, NGB, GH, HD).transpose(2, 3, 1, 0)
    arr["cproj_pad"] = cp.reshape(P, NGB * C)
    l2o = np.asarray(L0_attn_l2o_w)
    pad = np.zeros((L, GH, L), f4)
    pad[:, :, 0:HD] = l2o.T[:, None, :]
    arr["lat32"] = np.concatenate([np.tile(wkv2l, (1, HALF)), np.tile(l2o.T, (1, HALF)), pad.reshape(L, P),
                                   np.asarray(L0_attn_kv2l_b)[:, None]], axis=1)
    small = np.zeros((P, 12), f4)
    small[:, 0:6] = bqkv.reshape(6, P).T
    for k, bias in enumerate((np.asarray(L0_attn_q2l_b), np.asarray(L0_attn_kv2l_b))):
        for s in range(2):
            small[:, 6 + 2 * k + s] = np.tile(bias[s::2], HALF)
    small[:, 10] = np.tile(np.asarray(L0_attn_wqk_b)[perm], GH)
    small.reshape(GH, L, 12)[:, 0:HD, 11] = np.asarray(L0_attn_l2o_b)
    arr["small"] = small
    arr["cproj_bias"] = np.ascontiguousarray(np.broadcast_to(np.asarray(L0_attn_cproj_b), (P, C)))
    arr["router"] = np.ascontiguousarray(np.asarray(L0_ffn_router_weight).T.reshape(NC, P, NE).transpose(1, 0, 2))
    arr["ebias"] = np.ascontiguousarray(np.tile(np.broadcast_to(np.asarray(L0_ffn_e_bias), (P, NE)), (1, NT)))

    def rows_in_first(w):
        return w.transpose(0, 2, 1).reshape(-1, NC, P, I).transpose(0, 2, 1, 3).reshape(-1, P, NC * I)

    gate, up = (np.concatenate([np.asarray(a), np.asarray(s).reshape(NSH, I, C)]) for a, s in
                ((L0_ffn_gate_w, L0_ffn_sh_gate_w), (L0_ffn_up_w, L0_ffn_sh_up_w)))
    down = np.concatenate([np.asarray(L0_ffn_down_w).transpose(0, 2, 1),
                           np.asarray(L0_ffn_sh_down_w).T.reshape(NSH, I, C)])
    arr["experts"] = np.ascontiguousarray(np.concatenate([rows_in_first(gate), rows_in_first(up), down], axis=2))

    nc = bacc.Bacc("TRN2", target_bir_lowering=False, num_devices=1)
    from concourse import mybir as mb
    io = {n: nc.dram_tensor(f"in_{n}", a.shape, mb.dt.from_np(a.dtype), kind="ExternalInput").ap()
          for n, a in arr.items()}
    io["out"] = nc.dram_tensor("out_0", (B, T, C), F32, kind="ExternalOutput").ap()
    build_program(nc, io)
    r = run_bass_kernel_spmd(nc, [{f"in_{n}": a for n, a in arr.items()}], core_ids=[0])
    return r.results[0]["out_0"]
```

```python
from contextlib import ExitStack

import numpy as np

import concourse.bass as bass
from concourse import mybir

F32 = mybir.dt.float32
F32R = mybir.dt.float32r
BF16 = mybir.dt.bfloat16
I32 = mybir.dt.int32
ALU = mybir.AluOpType
ACT = mybir.ActivationFunctionType
AX_X = mybir.AxisListType.X

P = 128
B, T, C = 4, 512, 256
NT = T // P
NC = C // P
NH, HD, L = 16, 16, 32
GH = 4
NGB = NH // GH
NG = B * NGB
HALF = 8
NHALF = B * NH // HALF
NE, TOPK, NGRP = 16, 4, 4
EPG = NE // NGRP
NSH = 2
NX = NE + NSH
I = 128
WCOLS = 2 * NC * I + C
LN_EPS = 1e-5
ROUTE_SCALE = 2.5
SCORE_SCALE = float(L) ** -0.5
ST_UNITS = 10
P_SLOTS = 10
NSTACK = 3

ST_TILES = ([[(h, 0, 0)] for h in range(GH)]
            + [[(h, 1, 0), (h, 3, T - P)] for h in range(GH)]
            + [[(h, 2, 0), (h + 1, 2, T - 2 * P)] for h in (0, 2)])
WHERE = {(h, j): (u, col) for u, tile in enumerate(ST_TILES) for h, j, col in tile}
MAX_TILES = ([(3, h, 1) for h in range(GH)] + [(2, h, 1) for h in range(GH)]
             + [(1, 0, 2), (1, 2, 2)] + [(0, 0, 4)])
NMX = len(MAX_TILES)
ROUTE_PARTS, ROUTE_OPS, ROUTE_BEFORE = 3, 30, (0, 8, 15)
MAX_LEAD = 3

CONST_COLS = dict(rope_cos=T, rope_sin=T, cproj_bias=C, router=NC * NE, ebias=NT * NE, same_row=NT * NE,
                  earlier=NT * NGRP * NGRP, small=12)


def spread_over(main, extras):
    out, done = [], 0
    for k, piece in enumerate(main):
        out.append(piece)
        due = (k + 1) * len(extras) // len(main)
        out += extras[done:due]
        done = due
    return out + extras[done:]


def attention_pieces():
    pieces = []
    for g in range(-3, NG + 1):
        b, head, main, extras = g // NGB, [], [], []
        if 0 <= g - 1 < NG:
            head += [("values", g - 1, j) for j in range(1, NT)] + [("pv_out", g - 1)]
        if 0 <= g + 2 < NG:
            head += [("latq", g + 2)]
        if 0 <= g < NG and g % NGB == 0:
            head += [("vproj", b, i) for i in range(NT // 2)]
        for u in range(NMX + MAX_LEAD):
            if 0 <= g + 1 < NG and u < NMX:
                main.append(("max", g + 1, u))
            if u == 1 and 0 <= g - 1 < NG:
                main.append(("renorm", g - 1))
            if 0 <= g < NG and 0 <= u - MAX_LEAD + 1 < ST_UNITS:
                main.append(("score", g, u - MAX_LEAD + 1))
                if u - MAX_LEAD + 1 == 6:
                    main.append(("values", g, 0))
            if 0 <= g + 1 < NG and u == NMX:
                main.append(("maxT", g + 1))
        if g % NGB == 0 and 0 <= b - 1:
            extras += [("yT", b - 1, c) for c in range(NC)]
        nb = 0 if g == -3 else b + 1
        if (g == -3 or g >= 0 and g % NGB == 0) and nb < B:
            extras += [("stats", "norm1", nb), ("xnorm", "norm1", nb)] + [("xT", nb, c) for c in range(NC)]
        if g % 2 and 0 <= (g + 3) // 2 < NHALF:
            extras += [("rope", g + 3 + q, s) for q in range(2) for s in range(2)]
        for db in range(B):
            if g == min(NGB * db + 6, NG):
                extras += ([("cproj", db, i) for i in range(NT // 2)] + [("stats", "tail", db), ("xnorm", "tail", db)]
                           + [("x2T", db, c) for c in range(NC)] + [("router", db)]
                           + [("route", db, k) for k in range(ROUTE_PARTS)])
        pieces += head + spread_over(main, extras)
    return pieces


def fill_order(pieces):
    fills = [p for p in pieces if p[0] in ("xT", "yT", "x2T", "cproj", "vproj", "rope", "latq", "maxT", "router",
                                           "renorm")]
    return {name: k for k, name in enumerate(fills)}


def passes(w, x):
    return (w[0], x[0]), (w[1], x[0]), (w[0], x[1])


def build_program(nc, io):
    pieces = attention_pieces()
    fills = fill_order(pieces)
    fill_names = list(fills)
    norms = [piece[1:] for piece in pieces if piece[0] == "stats"]
    with ExitStack() as ctx:
        def sem(name):
            return ctx.enter_context(nc.semaphore(name))

        def sb(scope, name, shape, dt=F32):
            return scope.enter_context(nc.sbuf_tensor(name, shape, dt))

        def pair(scope, name, shape):
            return [sb(scope, f"{name}_{x}", shape, F32R) for x in ("hi", "lo")]

        ident = sb(ctx, "ident", [P, P])
        h_all = sb(ctx, "h_all", [P, B * NT, C])
        x2T = sb(ctx, "x2T", [P, NC, B * T])
        comb = sb(ctx, "comb", [P, B, NT * NE])
        onehot = sb(ctx, "onehot", [48, NE], F32R)

        att = ctx.enter_context(ExitStack())
        tok_idx = sb(att, "tok_idx", [P, B * NT], I32)
        pos_enc = sb(att, "pos_enc", [P, NT * C])
        consts = sb(att, "consts", [P, sum(CONST_COLS.values())])
        masks = sb(att, "masks", [P, 3, P], BF16)
        wlat = pair(att, "wlat", [P, 2, 2, NC, 2, P])
        wval = pair(att, "wval", [P, NC, C])
        wqk = pair(att, "wqk", [P, 2, HALF, L])
        wcp = pair(att, "wcp", [P, NC, C])
        blat = sb(att, "blat", [P, 8])
        vconst = sb(att, "vconst", [P, NC])
        lat32 = sb(att, "lat32", [L, 2 * P + 1])
        onehot_raw = sb(att, "onehot_raw", [48, NE])
        stats = sb(att, "stats", [P, NT, 6])
        meanvar = sb(att, "meanvar", [P, NT, 2])
        rstd = sb(att, "rstd", [P, NT])
        neghalf = sb(att, "neghalf", [P, NT])
        xn = sb(att, "xn", [P, NT, C])
        xT = pair(att, "xT", [P, NC, T])
        prod = sb(att, "prod", [P, 4, T])
        qrope = pair(att, "qrope", [P, 2, T])
        krope = pair(att, "krope", [P, 2, T])
        qlat = pair(att, "qlat", [P, T])
        qstack = [sb(att, f"qstack{p}", [97, GH, T], F32R) for p in range(NSTACK)]
        kstack = [sb(att, f"kstack{p}", [97, GH, T], F32R) for p in range(NSTACK)]
        rowmax = sb(att, "rowmax", [P, GH, NT])
        rowmaxT = sb(att, "rowmaxT", [NT * GH, P], F32R)
        val = sb(att, "val", [P, NT, NH, L])
        probs = sb(att, "probs", [P, P_SLOTS, T])
        pvs = sb(att, "pvs", [P, T])
        rden = sb(att, "rden", [P, NT, GH])
        ytok = sb(att, "ytok", [P, NT, C])
        yT = pair(att, "yT", [P, NC, T])
        rt = sb(att, "rt", [P, 12, NT * NE])

        cut, parts = 0, {}
        for name, cols in CONST_COLS.items():
            parts[name] = consts[:, cut:cut + cols]
            cut += cols
        rope_cos, rope_sin, cproj_bias, small = (parts[k] for k in ("rope_cos", "rope_sin", "cproj_bias", "small"))
        router_w = parts["router"].rearrange("p (c e) -> p c e", c=NC)
        ebias, same_row = parts["ebias"], parts["same_row"]
        earlier = parts["earlier"].rearrange("p (t i j) -> p t i j", t=NT, i=NGRP)
        ident_b, mask_kq, mask_qk = (masks[:, k, :] for k in range(3))

        ring = probs[:, :, :].rearrange("p s t -> p (s t)")
        cuts = np.cumsum([0, 4 * C, 4 * P, 2 * C, 2 * HALF * L, NC * C, P, P]).tolist()
        raw_qk, raw_rest = ring[:, 0:cuts[2]], ring[:, cuts[2]:cuts[6]]
        raw = [ring[:, a:b] for a, b in zip(cuts[:-1], cuts[1:])]
        raw_rows = raw[0].rearrange("p (n c) -> p n c", n=4)
        raw_bd = raw[1].rearrange("p (x c) -> p x c", x=2)
        raw_vrows = raw[2].rearrange("p (n c) -> p n c", n=2)
        raw_wqk, raw_wcp, block_mask, l2o_kv2l = raw[3:7]

        k_dram = nc.dram_tensor("k_dram", (2, 2, 2, HD, HALF, T), F32, kind="Internal").ap()
        q_dram = nc.dram_tensor("q_dram", (2, 2, L, GH, T), F32, kind="Internal").ap()

        banks = [ctx.enter_context(nc.psum_tensor(f"bank{i}", [P, T], F32)) for i in range(8)]
        work_banks, st_banks, mx_banks, pv_bank = banks[0:2], banks[2:5], banks[5:7], banks[7]
        fold_banks = banks[2:7]

        tok_in, raw_qk_in, raw_in, consts_in = sem("tok_in"), sem("raw_qk_in"), sem("raw_in"), sem("consts_in")
        pos_in, ident_in = sem("pos_in"), sem("ident_in")
        rows_in = [sem(f"rows_in{b}") for b in range(B)]
        pool_init, dve_init = sem("pool_init"), sem("dve_init")
        m_mm, m_ready = sem("m_mm"), sem("m_ready")
        fold_mm, fold_hi, fold_lo = sem("fold_mm"), sem("fold_hi"), sem("fold_lo")
        bias_ready, raw_hi, raw_lo = sem("bias_ready"), sem("raw_hi"), sem("raw_lo")
        h_ready, h_biased, h2_ready = sem("h_ready"), sem("h_biased"), sem("h2_ready")
        ln_stats, ln_aggr, ln_eps, ln_rstd = sem("ln_stats"), sem("ln_aggr"), sem("ln_eps"), sem("ln_rstd")
        xn_ready = sem("xn_ready")
        filled = sem("filled")
        xT_hi, xT_lo = sem("xT_hi"), sem("xT_lo")
        prod_ready, sum_roped, rope_hi, rope_lo = sem("prod_ready"), sem("sum_roped"), sem("rope_hi"), sem("rope_lo")
        latq_hi, latq_lo = sem("latq_hi"), sem("latq_lo")
        k_stored, q_stored = ([sem(f"{x}_stored{p}") for p in range(2)] for x in "kq")
        stack_in = [sem(f"stack_in{p}") for p in range(NSTACK)]
        maxrow_in = [sem(f"maxrow_in{p}") for p in range(NSTACK)]
        mx_mm, mx_red, maxT_ready = sem("mx_mm"), sem("mx_red"), sem("maxT_ready")
        st_mm, st_exp = sem("st_mm"), sem("st_exp")
        val_ready, pv_mm = sem("val_ready"), sem("pv_mm")
        pv_copied, rden_ready, ytok_ready = sem("pv_copied"), sem("rden_ready"), sem("ytok_ready")
        y_hi, y_lo = sem("y_hi"), sem("y_lo")
        x2T_ready, sig_ready, routed = sem("x2T_ready"), sem("sig_ready"), sem("routed")
        comb_ready, att_done = sem("comb_ready"), sem("att_done")
        wstage_in = [sem(f"wstage_in{i}") for i in range(2)]
        ex_hi, ex_lo = sem("ex_hi"), sem("ex_lo")
        xs_hi, xs_lo = sem("xs_hi"), sem("xs_lo")
        combT_mm, combT_hi, combT_lo = sem("combT_mm"), sem("combT_hi"), sem("combT_lo")
        combT_init = sem("combT_init")
        gate_mm, up_mm, spread_mm, down_mm = sem("gate_mm"), sem("up_mm"), sem("spread_mm"), sem("down_mm")
        silu_ready, weighted, hid_ready = sem("silu_ready"), sem("weighted"), sem("hid_ready")
        hid_hi, hid_lo = sem("hid_hi"), sem("hid_lo")
        y_copied = [sem(f"y_copied{c}") for c in range(NC)]
        yback_mm, sum_ready = sem("yback_mm"), sem("sum_ready")
        out_done = [sem(f"out_done{i}") for i in range(2)]

        CONSTS = (("consts", consts[:]), ("lat32", lat32[:]), ("masks", masks[:]), ("onehot", onehot_raw[:]))
        BQKV, LATB, WQKB, L2OB = 0, 6, 10, 11
        STACK_DMAS = 4

        def hof(g):
            return g % 2 * GH

        def wait_stack(eng, g):
            eng.wait_ge(stack_in[g % NSTACK], 16 * STACK_DMAS * (g // NSTACK + 1))

        def wait_maxrow(eng, g):
            eng.wait_ge(maxrow_in[g % NSTACK], 16 * (g // NSTACK + 1))

        def wait_read(eng, name):
            kind, n = name[0], name[1]
            if kind == "xT":
                eng.wait_ge(xT_hi, NC * n + name[2] + 1)
                eng.wait_ge(xT_lo, NC * n + name[2] + 1)
            elif kind == "rope":
                eng.wait_ge(prod_ready, 4 * n + 2 * (name[2] + 1))
            elif kind == "latq":
                eng.wait_ge(latq_hi, n + 1)
                eng.wait_ge(latq_lo, n + 1)
            elif kind == "maxT":
                eng.wait_ge(maxT_ready, n + 1)
            elif kind == "renorm":
                eng.wait_ge(ytok_ready, n + 1)
            elif kind == "yT":
                eng.wait_ge(y_hi, NC * n + name[2] + 1)
                eng.wait_ge(y_lo, NC * n + name[2] + 1)
            elif kind == "vproj":
                eng.wait_ge(val_ready, NT // 2 * n + name[2] + 1)
            elif kind == "cproj":
                eng.wait_ge(h2_ready, NT // 2 * n + name[2] + 1)
            elif kind == "x2T":
                eng.wait_ge(x2T_ready, NC * n + name[2] + 1)
            elif kind == "router":
                eng.wait_ge(sig_ready, n + 1)

        def bank_to_fill(pe, name):
            k = fills[name]
            if k >= 2:
                wait_read(pe, fill_names[k - 2])
            return work_banks[k % 2]

        def filled_bank(eng, name):
            eng.wait_ge(filled, fills[name] + 1)
            return work_banks[fills[name] % 2]

        def sp_setup(sp):
            sp.dma_start(tok_idx[:], io["tok"]).then_inc(tok_in, 16)
            sp.dma_start(raw_qk, io["raw_qk"]).then_inc(raw_qk_in, 16)
            sp.dma_start(pos_enc[:], io["pos_enc"]).then_inc(pos_in, 16)
            sp.dma_start(ident[:], io["ident"]).then_inc(ident_in, 16)
            for dst, name in ((consts[:], "consts"), (lat32[:], "lat32")):
                sp.dma_start(dst, io[name]).then_inc(consts_in, 16)
            sp.dma_start(raw_rest, io["raw_rest"]).then_inc(raw_in, 16)
            for dst, name in ((masks[:], "masks"), (onehot_raw[:], "onehot")):
                sp.dma_start(dst, io[name]).then_inc(consts_in, 16)

        def sp_latq(sp, g):
            n, kp, qp, heads = g // 2, g // 2 % 2, g % 2, slice(hof(g), hof(g) + GH)
            if g % 2 == 0:
                sp.wait_ge(rope_hi, 4 * n + 2)
                sp.wait_ge(rope_lo, 4 * n + 2)
                if n >= 2:
                    wait_stack(sp, g - 3)
                for x in range(2):
                    for s in range(2):
                        sp.dma_start(k_dram[kp, x, s].rearrange("f h t -> h f t"),
                                     krope[x][:, s, :].bitcast(F32)).then_inc(k_stored[kp], 16)
            if g >= NSTACK:
                sp.wait_ge(st_mm, ST_UNITS * (g - NSTACK + 1))
            sp.wait_ge(k_stored[kp], 64 * (n // 2 + 1))
            rows = k_dram[kp].rearrange("x s f h t -> (x s f) h t")
            stack_q, stack_k = qstack[g % NSTACK], kstack[g % NSTACK]
            sp.dma_start(stack_k[0:2 * L, :, :].bitcast(F32), rows[:, heads, :]).then_inc(stack_in[g % NSTACK], 16)
            sp.dma_start(stack_k[2 * L:3 * L, :, :].bitcast(F32),
                         rows[0:L, heads, :]).then_inc(stack_in[g % NSTACK], 16)
            sp.wait_ge(latq_hi, g + 1)
            sp.wait_ge(latq_lo, g + 1)
            if g >= 2:
                wait_stack(sp, g - 2)
            for x in range(2):
                sp.dma_start(q_dram[qp, x].rearrange("l h t -> h l t"), qlat[x][:].bitcast(F32)).then_inc(q_stored[qp], 16)
            sp.wait_ge(q_stored[qp], 32 * (g // 2 + 1))
            sp.dma_start(stack_q[0:2 * L, :, :].bitcast(F32),
                         q_dram[qp, 0].unsqueeze(0).broadcast_to([2, L, GH, T])).then_inc(stack_in[g % NSTACK], 16)
            sp.dma_start(stack_q[2 * L:3 * L, :, :].bitcast(F32), q_dram[qp, 1]).then_inc(stack_in[g % NSTACK], 16)

        def sp_maxT(sp, g):
            sp.wait_ge(maxT_ready, g + 1)
            sp.dma_start(qstack[g % NSTACK][96:97, :, :].rearrange("o h (i t) -> o (h i) t", t=P).bitcast(F32),
                         rowmaxT[:].bitcast(F32)).then_inc(maxrow_in[g % NSTACK], 16)

        def pool_embed(pool, b):
            pool.wait_ge(rows_in[b], 16 * NT)
            rows = h_all[:, b * NT:(b + 1) * NT, :]
            nc.gpsimd.tensor_tensor(rows, rows, pos_enc[:].rearrange("p (t c) -> p t c", t=NT),
                                    ALU.add).then_inc(h_ready, 1)

        def pool_setup(pool):
            nc.gpsimd.memset(neghalf[:], -0.5).then_inc(pool_init, 1)
            pool.wait_ge(tok_in, 16)
            for t in range(B * NT):
                nc.gpsimd.indirect_dma_start(
                    out=h_all[:, t, :], out_offset=None, in_=io["emb"],
                    in_offset=bass.IndirectOffsetOnAxis(ap=tok_idx[:, t:t + 1], axis=0)).then_inc(rows_in[t // NT], 16)
            pool.wait_ge(pos_in, 16)
            pool.wait_ge(pool_init, 1)
            pool_embed(pool, 0)

        def pool_rstd(pool, m):
            pool.wait_ge(ln_aggr, NT * (m + 1))
            if m >= 1:
                pool.wait_ge(xn_ready, NT * m)
            nc.gpsimd.tensor_scalar(rstd[:], meanvar[:, :, 1], LN_EPS, None, ALU.add).then_inc(ln_eps, 1)
            pool.wait_ge(ln_eps, m + 1)
            nc.gpsimd.tensor_tensor(rstd[:], rstd[:], neghalf[:], ALU.pow).then_inc(ln_rstd, 1)

        def pool_stats(pool, kind, b):
            pool_rstd(pool, norms.index((kind, b)))

        def pool_xnorm(pool, kind, b):
            if kind == "tail":
                return
            if b == 0:
                pool.wait_ge(consts_in, 16 * len(CONSTS))
            pool.wait_ge(xn_ready, NT * (norms.index((kind, b)) + 1))
            for t in range(b * NT, (b + 1) * NT):
                nc.gpsimd.tensor_tensor(h_all[:, t, :], h_all[:, t, :], cproj_bias, ALU.add).then_inc(h_biased, 1)
            if b + 1 < B:
                pool_embed(pool, b + 1)

        def pool_rope(pool, u, s):
            part = (krope, qrope)[u % 2][1]
            if s == 0:
                return
            pool.wait_ge(prod_ready, 4 * (u + 1))
            nc.gpsimd.tensor_tensor(prod[:, 0, :], prod[:, 0, :], prod[:, 3, :], ALU.subtract).then_inc(sum_roped, 1)
            nc.gpsimd.tensor_tensor(prod[:, 1, :], prod[:, 1, :], prod[:, 2, :], ALU.add).then_inc(sum_roped, 1)
            if u >= 2:
                wait_rope_used(pool, u)
            for x in range(2):
                pool.wait_ge(rope_hi, 2 * u + x + 1)
                nc.gpsimd.tensor_tensor(part[:, x, :], prod[:, x, :], (krope, qrope)[u % 2][0][:, x, :].bitcast(F32),
                                        ALU.subtract).then_inc(rope_lo, 1)

        def pe_setup(pe):
            pe.wait_ge(raw_qk_in, 16)
            for kq in range(2):
                for hf in range(2):
                    for c in range(NC):
                        mm = nc.tensor.matmul(fold_banks[2 * kq + hf][:, c * C:(c + 1) * C],
                                              raw_rows[:, 2 * kq + hf, c * P:(c + 1) * P], raw_bd[:, kq, :],
                                              start=True, stop=True)
                    mm.then_inc(fold_mm, 1)
            pe.wait_ge(consts_in, 16 * len(CONSTS))
            nc.tensor.matmul(pv_bank[:, 0:P], lat32[:, 0:P], lat32[:, P:2 * P], start=True, stop=True).then_inc(m_mm, 1)
            pe.wait_ge(raw_in, 16)
            pe.wait_ge(m_ready, 1)
            for c in range(NC):
                for hf in range(2):
                    mm = nc.tensor.matmul(fold_banks[4][:, c * C + hf * P:c * C + (hf + 1) * P],
                                          raw_vrows[:, hf, c * P:(c + 1) * P], l2o_kv2l, start=True, stop=True)
            mm.then_inc(fold_mm, 1)
            for k in range(8):
                nc.tensor.matmul(pv_bank[:, k:k + 1], raw_bd[:, k // 4, k % 2 * P:(k % 2 + 1) * P],
                                 small[:, BQKV + k // 2:BQKV + k // 2 + 1], start=True, stop=True)
            for c in range(NC):
                col = pv_bank[:, 8 + c:9 + c]
                nc.tensor.matmul(col, l2o_kv2l, small[:, BQKV + 4 + c:BQKV + 5 + c], start=True, stop=False)
                mm = nc.tensor.matmul(col, lat32[:, P:2 * P], lat32[:, 2 * P:2 * P + 1], start=False, stop=True)
            mm.then_inc(fold_mm, 1)
            pe.wait_ge(bias_ready, 2)

        def pe_transposes(pe, kind, b, c, rows):
            bank = bank_to_fill(pe, (kind, b, c))
            for i in range(NT):
                mm = nc.tensor.transpose(bank[:, i * P:(i + 1) * P], rows[:, i, c * P:(c + 1) * P], ident[:])
            mm.then_inc(filled, 1)

        def pe_xT(pe, b, c):
            if b == 0:
                pe.wait_ge(ident_in, 16)
            pe.wait_ge(xn_ready, NT * (norms.index(("norm1", b)) + 1))
            pe_transposes(pe, "xT", b, c, xn)

        def pe_x2T(pe, b, c):
            pe.wait_ge(xn_ready, NT * (norms.index(("tail", b)) + 1))
            pe_transposes(pe, "x2T", b, c, xn)

        def pe_yT(pe, b, c):
            pe.wait_ge(ytok_ready, NGB * (b + 1))
            pe_transposes(pe, "yT", b, c, ytok)

        def pe_rope(pe, u, s):
            n = u // 2
            pe.wait_ge(xT_hi, NC * (n // 2 + 1))
            pe.wait_ge(xT_lo, NC * (n // 2 + 1))
            if n < 2:
                pe.wait_ge(fold_hi, (3, 1, 4, 2)[u])
                pe.wait_ge(fold_lo, (3, 1, 4, 2)[u])
            bank = bank_to_fill(pe, ("rope", u, s))
            terms = [(w[:, 1 - u % 2, n % 2, c, s, :], x[:, c, :]) for c in range(NC) for w, x in passes(wlat, xT)]
            for k, (w, x) in enumerate(terms):
                mm = nc.tensor.matmul(bank[:], w, x, start=(k == 0), stop=(k == len(terms) - 1))
            mm.then_inc(filled, 1)

        def pe_latq(pe, g):
            pe.wait_ge(rope_hi, 4 * (g // 2) + 4)
            pe.wait_ge(rope_lo, 4 * (g // 2) + 4)
            if g == 0:
                pe.wait_ge(raw_hi, 2)
                pe.wait_ge(raw_lo, 2)
            bank = bank_to_fill(pe, ("latq", g))
            terms = [(w[:, s, hof(g):hof(g) + GH, :], x[:, s, :]) for s in range(2) for w, x in passes(wqk, qrope)]
            for k, (w, x) in enumerate(terms):
                mm = nc.tensor.matmul(bank[:], w, x, start=(k == 0), stop=(k == len(terms) - 1))
            mm.then_inc(filled, 1)

        def pe_max(pe, g, u):
            i, h0, heads = MAX_TILES[u]
            k = g * NMX + u
            if u == 0:
                wait_stack(pe, g)
            if k >= 2:
                pe.wait_ge(mx_red, k - 1)
            bank, width = mx_banks[k % 2], P * (i + 1)
            for h in range(heads):
                col = h * width
                nc.tensor.matmul(bank[:, col:col + width], qstack[g % NSTACK][0:96, h0 + h, i * P:(i + 1) * P],
                                 kstack[g % NSTACK][0:96, h0 + h, 0:width], start=True, stop=False)
                mm = nc.tensor.matmul(bank[:, col + i * P:col + width], ident_b, mask_qk, start=False, stop=True)
            mm.then_inc(mx_mm, 1)

        def pe_maxT(pe, g):
            bank = bank_to_fill(pe, ("maxT", g))
            pe.wait_ge(mx_red, NMX * (g + 1))
            nc.tensor.transpose(bank[0:NT * GH, 0:P], rowmax[:], ident[:]).then_inc(filled, 1)

        def pe_score(pe, g, u):
            if u == 0:
                wait_maxrow(pe, g)
            if g == 0:
                pe.wait_ge(dve_init, 1 + NSTACK)
            k = g * ST_UNITS + u
            if k >= 3:
                pe.wait_ge(st_exp, k - 2)
            bank = st_banks[k % 3]
            for h, j, col in ST_TILES[u]:
                nc.tensor.matmul(bank[:, col:col + T - P * j], kstack[g % NSTACK][:, h, j * P:(j + 1) * P],
                                 qstack[g % NSTACK][:, h, j * P:T], start=True, stop=False)
                mm = nc.tensor.matmul(bank[:, col:col + P], ident_b, mask_kq, start=False, stop=True)
            mm.then_inc(st_mm, 1)

        def pe_values(pe, g, j):
            pe.wait_ge(st_exp, ST_UNITS * g + 1 + max(WHERE[(h, j)][0] for h in range(GH)))
            if j == 0:
                if g % NGB == 0:
                    pe.wait_ge(val_ready, NT // 2 * (g // NGB + 1))
                if g >= 1:
                    pe.wait_ge(pv_copied, g)
            for h in range(GH):
                u, col = WHERE[(h, j)]
                mm = nc.tensor.matmul(pv_bank[32 * h:32 * h + 32, j * P:T], val[:, j, g % NGB * GH + h, :],
                                      probs[:, (g * ST_UNITS + u) % P_SLOTS, col:col + T - P * j],
                                      start=(j == 0), stop=(j == NT - 1))
            mm.then_inc(pv_mm, 1)

        def pe_renorm(pe, g):
            bank = bank_to_fill(pe, ("renorm", g))
            pe.wait_ge(pv_copied, g + 1)
            for i in range(NT):
                mm = nc.tensor.transpose(bank[:, i * P:(i + 1) * P], pvs[:, i * P:(i + 1) * P], ident[:])
            mm.then_inc(filled, 1)

        def pe_token_rows(pe, kind, b, i, lhs, w):
            bank = bank_to_fill(pe, (kind, b, i))
            for t in range(2):
                tok = (2 * i + t) * P
                terms = [(x[:, c, tok:tok + P], y[:, c, :]) for c in range(NC) for x, y in passes(lhs, w)]
                for k, (x, y) in enumerate(terms):
                    mm = nc.tensor.matmul(bank[:, t * C:(t + 1) * C], x, y, start=(k == 0),
                                          stop=(k == len(terms) - 1))
            mm.then_inc(filled, 1)

        def pe_vproj(pe, b, i):
            if b == 0:
                pe.wait_ge(fold_hi, 5)
                pe.wait_ge(fold_lo, 5)
            pe_token_rows(pe, "vproj", b, i, xT, wval)

        def pe_cproj(pe, b, i):
            pe.wait_ge(y_hi, NC * (b + 1))
            pe.wait_ge(y_lo, NC * (b + 1))
            pe_token_rows(pe, "cproj", b, i, yT, wcp)

        def pe_router(pe, b):
            pe.wait_ge(x2T_ready, NC * (b + 1))
            bank = bank_to_fill(pe, ("router", b))
            for i in range(NT):
                tok = b * T + i * P
                for c in range(NC):
                    mm = nc.tensor.matmul(bank[:, i * NE:(i + 1) * NE], x2T[:, c, tok:tok + P], router_w[:, c, :],
                                          start=(c == 0), stop=(c == NC - 1))
            mm.then_inc(filled, 1)

        def act_setup(act):
            for k in range(4):
                act.wait_ge(fold_mm, k + 1)
                nc.scalar.copy(folded(0, k), fold_banks[k][:]).then_inc(fold_hi, 1)
            act.wait_ge(raw_in, 16)
            nc.scalar.copy(wqk[0][:].rearrange("p s h l -> p (s h l)"), raw_wqk).then_inc(raw_hi, 1)
            nc.scalar.copy(wcp[0][:].rearrange("p g c -> p (g c)"), raw_wcp).then_inc(raw_hi, 1)
            act.wait_ge(fold_mm, 5)
            nc.scalar.copy(folded(0, 4), fold_banks[4][:]).then_inc(fold_hi, 1)
            act.wait_ge(consts_in, 16 * len(CONSTS))
            nc.scalar.copy(onehot[:], onehot_raw[:])

        def wait_rope_used(eng, u):
            n = u // 2
            if u % 2 == 0:
                eng.wait_ge(k_stored[(n - 1) % 2], 64 * ((n - 1) // 2 + 1))
            else:
                eng.wait_ge(filled, fills[("latq", 2 * n - 1)] + 1)

        def folded(part, k):
            return wlat[part][:, k // 2, k % 2, :, :, :].rearrange("p c s r -> p (c s r)") if k < 4 else \
                wval[part][:].rearrange("p c n -> p (c n)")

        def act_xT(act, b, c):
            if b >= 1:
                act.wait_ge(filled, fills[("vproj", b - 1, NT // 2 - 1)] + 1)
            bank = filled_bank(act, ("xT", b, c))
            nc.scalar.copy(xT[0][:, c, :], bank[:]).then_inc(xT_hi, 1)

        def act_rope(act, u, s):
            if s == 0:
                return
            for x in range(2):
                act.wait_ge(sum_roped, 2 * u + x + 1)
                if u >= 2 and x == 0:
                    wait_rope_used(act, u)
                nc.scalar.copy((krope, qrope)[u % 2][0][:, x, :], prod[:, x, :]).then_inc(rope_hi, 1)

        def act_latq(act, g):
            if g == 0:
                act.wait_ge(consts_in, 16 * len(CONSTS))
            else:
                act.wait_ge(q_stored[(g - 1) % 2], 32 * ((g - 1) // 2 + 1))
            bank = filled_bank(act, ("latq", g))
            nc.scalar.activation(qlat[0][:], bank[:], ACT.Identity, bias=small[:, WQKB:WQKB + 1]).then_inc(latq_hi, 1)

        def act_score(act, g, u):
            k = g * ST_UNITS + u
            act.wait_ge(st_mm, k + 1)
            if k >= P_SLOTS:
                gg, uu = divmod(k - P_SLOTS, ST_UNITS)
                act.wait_ge(pv_mm, NT * gg + 1 + max(j for _, j, _ in ST_TILES[uu]))
            nc.scalar.activation(probs[:, k % P_SLOTS, :], st_banks[k % 3][:], ACT.Exp,
                                 scale=SCORE_SCALE).then_inc(st_exp, 1)

        def act_pv_out(act, g):
            act.wait_ge(pv_mm, NT * (g + 1))
            if g >= 1:
                act.wait_ge(filled, fills[("renorm", g - 1)] + 1)
            nc.scalar.copy(pvs[:], pv_bank[:]).then_inc(pv_copied, 1)

        def act_yT(act, b, c):
            if b >= 1:
                act.wait_ge(filled, fills[("cproj", b - 1, NT // 2 - 1)] + 1)
            bank = filled_bank(act, ("yT", b, c))
            nc.scalar.activation(yT[0][:, c, :], bank[:], ACT.Identity, bias=vconst[:, c:c + 1]).then_inc(y_hi, 1)

        def act_vproj(act, b, i):
            if b == 0:
                act.wait_ge(dve_init, 1)
                act.wait_ge(bias_ready, 2)
            else:
                act.wait_ge(pv_mm, NT * NGB * b)
            bank = filled_bank(act, ("vproj", b, i))
            nc.scalar.copy(val[:, 2 * i:2 * i + 2, :, 0:HD],
                           bank[:].rearrange("p (t h d) -> p t h d", t=2, h=NH)).then_inc(val_ready, 1)

        def act_x2T(act, b, c):
            bank = filled_bank(act, ("x2T", b, c))
            nc.scalar.copy(x2T[:, c, b * T:(b + 1) * T], bank[:]).then_inc(x2T_ready, 1)

        def act_router(act, b):
            bank = filled_bank(act, ("router", b))
            if b >= 1:
                act.wait_ge(comb_ready, b)
            nc.scalar.activation(rt[:, 0, :], bank[:, 0:NT * NE], ACT.Sigmoid).then_inc(sig_ready, 1)

        def dve_setup(dve):
            nc.vector.memset(val[:, :, :, HD:L], 1.0).then_inc(dve_init, 1)
            for p in range(NSTACK):
                nc.vector.memset(kstack[p][96:97, :, :].bitcast(F32), -1.0).then_inc(dve_init, 1)
            for k in range(4):
                dve.wait_ge(fold_hi, k + 1)
                nc.vector.tensor_tensor(folded(1, k), fold_banks[k][:], folded(0, k).bitcast(F32),
                                        ALU.subtract).then_inc(fold_lo, 1)
            dve.wait_ge(raw_in, 16)
            dve.wait_ge(m_mm, 1)
            nc.vector.tensor_tensor(l2o_kv2l, pv_bank[:, 0:P], block_mask, ALU.mult).then_inc(m_ready, 1)
            for k, (w, src) in enumerate(((wqk, raw_wqk), (wcp, raw_wcp))):
                dve.wait_ge(raw_hi, k + 1)
                pat = "p s h l -> p (s h l)" if k == 0 else "p g c -> p (g c)"
                nc.vector.tensor_tensor(w[1][:].rearrange(pat), src, w[0][:].rearrange(pat).bitcast(F32),
                                        ALU.subtract).then_inc(raw_lo, 1)
            dve.wait_ge(fold_hi, 5)
            nc.vector.tensor_tensor(folded(1, 4), fold_banks[4][:], folded(0, 4).bitcast(F32),
                                    ALU.subtract).then_inc(fold_lo, 1)
            dve.wait_ge(consts_in, 16 * len(CONSTS))
            dve.wait_ge(fold_mm, 6)
            lat_b = small[:, LATB:LATB + 4].rearrange("p (x s) -> p x s", x=2).unsqueeze(2).broadcast_to([P, 2, 2, 2])
            nc.vector.tensor_tensor(blat[:].rearrange("p (x f s) -> p x f s", x=2, f=2),
                                    pv_bank[:, 0:8].rearrange("p (x f s) -> p x f s", x=2, f=2), lat_b,
                                    ALU.add).then_inc(bias_ready, 1)
            nc.vector.tensor_scalar(vconst[:], pv_bank[:, 8:8 + NC], small[:, L2OB:L2OB + 1], None,
                                    ALU.add).then_inc(bias_ready, 1)

        def wait_xn_used(eng, m):
            kind, b = norms[m]
            eng.wait_ge(filled, fills[("xT" if kind == "norm1" else "x2T", b, NC - 1)] + 1)

        def dve_stats(dve, kind, b):
            m = norms.index((kind, b))
            if kind == "norm1":
                dve.wait_ge(h_ready, b + 1)
            else:
                dve.wait_ge(h2_ready, NT // 2 * (b + 1))
            for i in range(NT):
                nc.vector.bn_stats(stats[:, i, :], h_all[:, b * NT + i, :]).then_inc(ln_stats, 1)
            for i in range(NT):
                dve.wait_ge(ln_stats, NT * m + i + 1)
                if m >= 1 and i == 0:
                    dve.wait_ge(ln_rstd, m)
                nc.vector.bn_aggr(meanvar[:, i, :], stats[:, i, :]).then_inc(ln_aggr, 1)

        def dve_xnorm(dve, kind, b):
            m = norms.index((kind, b))
            if m >= 1:
                wait_xn_used(dve, m - 1)
            dve.wait_ge(ln_aggr, NT * (m + 1))
            dve.wait_ge(ln_rstd, m + 1)
            for i in range(NT):
                nc.vector.tensor_scalar(xn[:, i, :], h_all[:, b * NT + i, :], meanvar[:, i, 0:1], rstd[:, i:i + 1],
                                        ALU.subtract, ALU.mult).then_inc(xn_ready, 1)

        def dve_xT(dve, b, c):
            if b >= 1:
                dve.wait_ge(filled, fills[("vproj", b - 1, NT // 2 - 1)] + 1)
            bank = filled_bank(dve, ("xT", b, c))
            dve.wait_ge(xT_hi, NC * b + c + 1)
            nc.vector.tensor_tensor(xT[1][:, c, :], bank[:], xT[0][:, c, :].bitcast(F32),
                                    ALU.subtract).then_inc(xT_lo, 1)

        def dve_rope(dve, u, s):
            if u == 0 and s == 0:
                dve.wait_ge(bias_ready, 2)
            if u >= 1 and s == 0:
                dve.wait_ge(rope_lo, 2 * u)
                dve.wait_ge(rope_hi, 2 * u)
            bank = filled_bank(dve, ("rope", u, s))
            k = 4 * (1 - u % 2) + 2 * (u // 2 % 2) + s
            for slot, table in (((0, rope_cos), (1, rope_sin)), ((2, rope_cos), (3, rope_sin)))[s]:
                nc.vector.scalar_tensor_tensor(out=prod[:, slot, :], in0=bank[:], scalar=blat[:, k:k + 1],
                                               in1=table, op0=ALU.add, op1=ALU.mult).then_inc(prod_ready, 1)

        def dve_latq(dve, g):
            if g >= 1:
                dve.wait_ge(q_stored[(g - 1) % 2], 32 * ((g - 1) // 2 + 1))
            bank = filled_bank(dve, ("latq", g))
            dve.wait_ge(latq_hi, g + 1)
            nc.vector.scalar_tensor_tensor(out=qlat[1][:], in0=bank[:], scalar=small[:, WQKB:WQKB + 1],
                                           in1=qlat[0][:].bitcast(F32), op0=ALU.add,
                                           op1=ALU.subtract).then_inc(latq_lo, 1)

        def dve_max(dve, g, u):
            if g >= 1 and u == 0:
                dve.wait_ge(filled, fills[("maxT", g - 1)] + 1)
            i, h0, heads = MAX_TILES[u]
            k = g * NMX + u
            dve.wait_ge(mx_mm, k + 1)
            width = P * (i + 1)
            nc.vector.tensor_reduce(rowmax[:, h0:h0 + heads, i],
                                    mx_banks[k % 2][:, 0:heads * width].rearrange("p (h w) -> p h w", h=heads),
                                    AX_X, ALU.max).then_inc(mx_red, 1)

        def dve_maxT(dve, g):
            bank = filled_bank(dve, ("maxT", g))
            if g >= 1:
                wait_maxrow(dve, g - 1)
            nc.vector.tensor_copy(rowmaxT[:], bank[0:NT * GH, 0:P]).then_inc(maxT_ready, 1)

        def dve_renorm(dve, g):
            bank = filled_bank(dve, ("renorm", g))[:].rearrange("p (t h l) -> p t h l", t=NT, h=GH)
            if g >= 1:
                dve.wait_ge(ytok_ready, g)
            nc.vector.reciprocal(rden[:], bank[:, :, :, HD]).then_inc(rden_ready, 1)
            dve.wait_ge(rden_ready, g + 1)
            if g % NGB == 0 and g >= NGB:
                dve.wait_ge(filled, fills[("yT", g // NGB - 1, NC - 1)] + 1)
            cols = g % NGB * GH * HD
            nc.vector.tensor_tensor(ytok[:, :, cols:cols + GH * HD].rearrange("p t (h d) -> p t h d", h=GH),
                                    bank[:, :, :, 0:HD], rden[:].unsqueeze(3).broadcast_to([P, NT, GH, HD]),
                                    ALU.mult).then_inc(ytok_ready, 1)

        def dve_yT(dve, b, c):
            bank = filled_bank(dve, ("yT", b, c))
            dve.wait_ge(y_hi, NC * b + c + 1)
            nc.vector.scalar_tensor_tensor(out=yT[1][:, c, :], in0=bank[:], scalar=vconst[:, c:c + 1],
                                           in1=yT[0][:, c, :].bitcast(F32), op0=ALU.add,
                                           op1=ALU.subtract).then_inc(y_lo, 1)

        def dve_cproj(dve, b, i):
            dve.wait_ge(h_biased, NT * (b + 1))
            bank = filled_bank(dve, ("cproj", b, i))
            rows = h_all[:, b * NT + 2 * i:b * NT + 2 * i + 2, :].rearrange("p t c -> p (t c)")
            nc.vector.tensor_tensor(rows, bank[:], rows, ALU.add).then_inc(h2_ready, 1)

        def dve_route(dve, b, part):
            count = [ROUTE_OPS * b + ROUTE_BEFORE[part]]

            def after(ins):
                count[0] += 1
                ins.then_inc(routed, 1)
                return count[0]

            v = nc.vector
            score, sc, masked, gt4, eq4, prefix, chosen = (rt[:, k, :] for k in range(7))
            a1, a2 = rt[:, 7, :], rt[:, 8, :]
            hi2, lo2 = rt[:, 9, 0:32], rt[:, 9, 32:64]
            top1, mid, low, gsum = (rt[:, 10, 16 * k:16 * k + 16] for k in range(4))
            gmask, top8 = rt[:, 11, 0:16], rt[:, 11, 16:48]
            above, wsum = rt[:, 11, 48:52], rt[:, 11, 52:56]
            rank = rt[:, 11, 56:64]
            if part == 0:
                dve.wait_ge(sig_ready, b + 1)
                n = after(v.tensor_tensor(sc, score, ebias, ALU.add))
                dve.wait_ge(routed, n)
                pairs = sc.rearrange("p (g a two) -> p g a two", a=2, two=2)
                h2v, l2v = (x.rearrange("p (g a) -> p g a", a=2) for x in (hi2, lo2))
                after(v.tensor_tensor(h2v, pairs[:, :, :, 0], pairs[:, :, :, 1], ALU.max))
                n = after(v.tensor_tensor(l2v, pairs[:, :, :, 0], pairs[:, :, :, 1], ALU.min))
                dve.wait_ge(routed, n)
                after(v.tensor_tensor(top1, h2v[:, :, 0], h2v[:, :, 1], ALU.max))
                after(v.tensor_tensor(mid, h2v[:, :, 0], h2v[:, :, 1], ALU.min))
                n = after(v.tensor_tensor(low, l2v[:, :, 0], l2v[:, :, 1], ALU.max))
                dve.wait_ge(routed, n)
                n = after(v.tensor_tensor(mid, mid, low, ALU.max))
                dve.wait_ge(routed, n)
                n = after(v.tensor_tensor(gsum, top1, mid, ALU.add))
                dve.wait_ge(routed, n)
            elif part == 1:
                gs = gsum.rearrange("p (t g) -> p t g", t=NT)
                gs_j = gs.unsqueeze(2).broadcast_to([P, NT, NGRP, NGRP])
                gs_i = gs.unsqueeze(3).broadcast_to([P, NT, NGRP, NGRP])
                q4 = "p (t i j) -> p t i j"
                a1v, a2v = a1.rearrange(q4, t=NT, i=NGRP), a2.rearrange(q4, t=NT, i=NGRP)
                after(v.tensor_tensor(a1v, gs_j, gs_i, ALU.is_gt))
                n = after(v.tensor_tensor(a2v, gs_j, gs_i, ALU.is_equal))
                dve.wait_ge(routed, n)
                n = after(v.tensor_tensor(a2v, a2v, earlier, ALU.mult))
                dve.wait_ge(routed, n)
                n = after(v.tensor_tensor(a1, a1, a2, ALU.add))
                dve.wait_ge(routed, n)
                n = after(v.tensor_reduce(top1, a1.rearrange("p (x j) -> p x j", j=NGRP), AX_X, ALU.add))
                dve.wait_ge(routed, n)
                n = after(v.tensor_scalar(gmask, top1, 2.0, None, ALU.is_lt))
                dve.wait_ge(routed, n)
                by_group = "p (x e) -> p x e"
                n = after(v.tensor_tensor(masked.rearrange(by_group, e=EPG), sc.rearrange(by_group, e=EPG),
                                          gmask.unsqueeze(2).broadcast_to([P, NT * NGRP, EPG]), ALU.mult))
                dve.wait_ge(routed, n)
            else:
                for t in range(NT):
                    n = after(v.max(top8[:, 8 * t:8 * t + 8], masked[:, t * NE:(t + 1) * NE]))
                dve.wait_ge(routed, n)
                row = "p (t e) -> p t e"
                fourth = top8.rearrange("p (t k) -> p t k", t=NT)[:, :, TOPK - 1:TOPK].broadcast_to([P, NT, NE])
                after(v.tensor_tensor(gt4.rearrange(row, t=NT), masked.rearrange(row, t=NT), fourth, ALU.is_gt))
                n = after(v.tensor_tensor(eq4.rearrange(row, t=NT), masked.rearrange(row, t=NT), fourth, ALU.is_equal))
                dve.wait_ge(routed, n)
                after(v.tensor_reduce(above, gt4.rearrange(row, t=NT), AX_X, ALU.add))
                n = after(v.tensor_tensor_scan(prefix, same_row, eq4, 0.0, ALU.mult, ALU.add))
                dve.wait_ge(routed, n)
                n = after(v.tensor_tensor(a1.rearrange(row, t=NT), prefix.rearrange(row, t=NT),
                                          above.unsqueeze(2).broadcast_to([P, NT, NE]), ALU.add))
                dve.wait_ge(routed, n)
                n = after(v.scalar_tensor_tensor(out=a2, in0=a1, scalar=float(TOPK), in1=eq4, op0=ALU.is_le,
                                                 op1=ALU.mult))
                dve.wait_ge(routed, n)
                n = after(v.tensor_tensor(chosen, gt4, a2, ALU.add))
                dve.wait_ge(routed, n)
                n = after(v.tensor_tensor(a1, score, chosen, ALU.mult))
                dve.wait_ge(routed, n)
                n = after(v.tensor_reduce(wsum, a1.rearrange(row, t=NT), AX_X, ALU.add))
                dve.wait_ge(routed, n)
                n = after(v.tensor_scalar(wsum, wsum, 1e-20, None, ALU.add))
                dve.wait_ge(routed, n)
                n = after(v.reciprocal(wsum, wsum))
                dve.wait_ge(routed, n)
                v.scalar_tensor_tensor(out=comb[:, b, :].rearrange(row, t=NT), in0=a1.rearrange(row, t=NT),
                                       scalar=ROUTE_SCALE, in1=wsum.unsqueeze(2).broadcast_to([P, NT, NE]),
                                       op0=ALU.mult, op1=ALU.mult).then_inc(comb_ready, 1)

            assert count[0] == ROUTE_OPS * b + (ROUTE_BEFORE + (ROUTE_OPS,))[part + 1], count[0]

        def nothing(eng, *piece):
            pass

        STAGES = {
            "sp": dict(latq=sp_latq, maxT=sp_maxT),
            "pool": dict(stats=pool_stats, xnorm=pool_xnorm, rope=pool_rope),
            "pe": dict(xT=pe_xT, rope=pe_rope, latq=pe_latq, max=pe_max, maxT=pe_maxT, score=pe_score,
                       values=pe_values, renorm=pe_renorm, yT=pe_yT, vproj=pe_vproj, cproj=pe_cproj, x2T=pe_x2T,
                       router=pe_router),
            "act": dict(xT=act_xT, rope=act_rope, latq=act_latq, score=act_score, pv_out=act_pv_out, yT=act_yT,
                        vproj=act_vproj, x2T=act_x2T, router=act_router),
            "dve": dict(stats=dve_stats, xnorm=dve_xnorm, xT=dve_xT, rope=dve_rope, latq=dve_latq, max=dve_max,
                        maxT=dve_maxT, renorm=dve_renorm, yT=dve_yT, cproj=dve_cproj, route=dve_route),
        }

        def attention(eng, engine):
            for piece in pieces:
                STAGES[engine].get(piece[0], nothing)(eng, *piece[1:])

        att.close()
        moe = ctx.enter_context(ExitStack())
        wex = pair(moe, "wex", [P, NX, WCOLS])
        wstage = [sb(moe, f"wstage{i}", [P, WCOLS]) for i in range(2)]
        xs = [pair(moe, f"xs{p}", [P, NC, T]) for p in range(2)]
        combT = [sb(moe, f"combT{p}", [48, T], F32R) for p in range(2)]
        gated = [sb(moe, f"gated{p}", [P, T]) for p in range(2)]
        hid = [sb(moe, f"hid{p}", [P, T]) for p in range(2)]
        hidr = [pair(moe, f"hidr{p}", [P, T]) for p in range(2)]
        ysb = sb(moe, "ysb", [P, NC, T])
        outbuf = [sb(moe, f"outbuf{i}", [P, 2, C]) for i in range(2)]
        gate_banks, up_banks, y_banks, spread_bank, misc_bank = banks[0:2], banks[2:4], banks[4:6], banks[6], banks[7]
        order = [NE + s for s in range(NSH)] + list(range(NE))
        NS = B * NX
        routed_before = [sum(order[k % NX] < NE for k in range(n)) for n in range(NS + 1)]

        def sp_moe(sp):
            sp.wait_ge(att_done, 4)
            for e in range(NX):
                if e >= 2:
                    sp.wait_ge(ex_hi, e - 1)
                    sp.wait_ge(ex_lo, e - 1)
                sp.dma_start(wstage[e % 2][:], io["experts"][order[e]]).then_inc(wstage_in[e % 2], 16)
            for k in range(B * NT // 2):
                sp.wait_ge(sum_ready, k + 1)
                b, i = k // 2, k % 2
                sp.dma_start(io["out"][b].rearrange("(i t p) c -> i p t c", t=2, p=P)[i],
                             outbuf[i][:]).then_inc(out_done[i], 16)
            for i in range(2):
                sp.wait_ge(out_done[i], 16 * B)

        def pe_moe(pe):
            def transposed_weights(b):
                pe.wait_ge(comb_ready, b + 1)
                if b >= 1:
                    pe.wait_ge(sum_ready, 2 * (b - 1))
                    pe.wait_ge(combT_hi, b)
                    pe.wait_ge(combT_lo, b)
                for i in range(NT):
                    mm = nc.tensor.transpose(misc_bank[0:NE, i * P:(i + 1) * P], comb[:, b, i * NE:(i + 1) * NE],
                                             ident[:])
                mm.then_inc(combT_mm, 1)

            def gate_up(n):
                b, k = n // NX, n % NX
                if k == 0:
                    pe.wait_ge(xs_hi, NC * (b + 1))
                    pe.wait_ge(xs_lo, NC * (b + 1))
                if b == 0:
                    pe.wait_ge(ex_hi, k + 1)
                    pe.wait_ge(ex_lo, k + 1)
                if n >= 2:
                    pe.wait_ge(silu_ready, n - 1)
                    pe.wait_ge(hid_ready, n - 1)
                for bank, first, done in ((gate_banks[n % 2], 0, gate_mm), (up_banks[n % 2], NC * I, up_mm)):
                    terms = [(w[:, k, first + c * I:first + (c + 1) * I], x[:, c, :]) for c in range(NC)
                             for w, x in passes(wex, xs[b % 2])]
                    for j, (w, x) in enumerate(terms):
                        mm = nc.tensor.matmul(bank[:], w, x, start=(j == 0), stop=(j == len(terms) - 1))
                    mm.then_inc(done, 1)

            def spread(n):
                b, e = n // NX, order[n % NX]
                if e >= NE:
                    return
                r = routed_before[n]
                if e == 0:
                    pe.wait_ge(combT_hi, b + 1)
                    pe.wait_ge(combT_lo, b + 1)
                if r >= 1:
                    pe.wait_ge(weighted, r)
                nc.tensor.matmul(spread_bank[:], onehot[:, e:e + 1].broadcast_to([48, P]), combT[b % 2][:],
                                 start=True, stop=True).then_inc(spread_mm, 1)

            def down(n):
                b, k = n // NX, n % NX
                pe.wait_ge(hid_hi, n + 1)
                pe.wait_ge(hid_lo, n + 1)
                if k == 0 and b >= 1:
                    for c in range(NC):
                        pe.wait_ge(y_copied[c], b)
                for c in range(NC):
                    cols = 2 * NC * I + c * P
                    for j, (w, x) in enumerate(passes(wex, hidr[n % 2])):
                        mm = nc.tensor.matmul(y_banks[c][:], w[:, k, cols:cols + P], x[:], start=(k == 0 and j == 0),
                                              stop=(k == NX - 1 and j == 2))
                mm.then_inc(down_mm, 1)

            def rows_back(b, i):
                if i == 0:
                    for c in range(NC):
                        pe.wait_ge(y_copied[c], b + 1)
                    pe.wait_ge(combT_hi, min(b + 2, B))
                    pe.wait_ge(combT_lo, min(b + 2, B))
                if i == 1 or b >= 1:
                    pe.wait_ge(sum_ready, 2 * b + i)
                for t in range(2):
                    for c in range(NC):
                        tok = (2 * i + t) * P
                        mm = nc.tensor.transpose(misc_bank[:, t * C + c * P:t * C + (c + 1) * P],
                                                 ysb[:, c, tok:tok + P], ident[:])
                mm.then_inc(yback_mm, 1)

            transposed_weights(0)
            for n in range(NS):
                gate_up(n)
                spread(n)
                if n >= 1:
                    down(n - 1)
                if n % NX == NX - 4 and n // NX + 1 < B:
                    transposed_weights(n // NX + 1)
                if n % NX in (2, 4) and n >= NX:
                    rows_back(n // NX - 1, n % NX // 2 - 1)
            down(NS - 1)
            for i in range(2):
                rows_back(B - 1, i)

        def act_moe(act):
            def load_x(b):
                if b >= 2:
                    act.wait_ge(up_mm, NX * (b - 1))
                for c in range(NC):
                    nc.scalar.copy(xs[b % 2][0][:, c, :], x2T[:, c, b * T:(b + 1) * T]).then_inc(xs_hi, 1)
                act.wait_ge(combT_mm, b + 1)
                if b == 0:
                    act.wait_ge(combT_init, 2)
                if b >= 2:
                    act.wait_ge(spread_mm, NE * (b - 1))
                nc.scalar.copy(combT[b % 2][0:NE, :], misc_bank[0:NE, :]).then_inc(combT_hi, 1)

            act.wait_ge(att_done, 4)
            for n in range(NS + 1):
                b, k = n // NX, n % NX
                if n == 0:
                    load_x(0)
                if b == 0 and n < NX:
                    act.wait_ge(wstage_in[n % 2], 16 * (n // 2 + 1))
                    nc.scalar.copy(wex[0][:, n, :], wstage[n % 2][:]).then_inc(ex_hi, 1)
                if n < NS:
                    act.wait_ge(gate_mm, n + 1)
                    if n >= 2:
                        act.wait_ge(hid_ready, n - 1)
                    nc.scalar.activation(gated[n % 2][:], gate_banks[n % 2][:], ACT.Silu).then_inc(silu_ready, 1)
                if n >= 1:
                    act.wait_ge(hid_ready, n)
                    if n >= 3:
                        act.wait_ge(down_mm, n - 2)
                    nc.scalar.copy(hidr[(n - 1) % 2][0][:], hid[(n - 1) % 2][:]).then_inc(hid_hi, 1)
                if n < NS and k == NX - 4 and b + 1 < B:
                    load_x(b + 1)
                if n >= NX and k == 0 and n < NS:
                    copy_y(act, nc.scalar.copy, b - 1, 0)
            copy_y(act, nc.scalar.copy, B - 1, 0)

        def copy_y(eng, copy, b, c):
            eng.wait_ge(down_mm, NX * (b + 1))
            if b >= 1:
                eng.wait_ge(yback_mm, 2 * b)
            copy(ysb[:, c, :], y_banks[c][:]).then_inc(y_copied[c], 1)

        def dve_moe(dve):
            def load_x(b):
                if b >= 2:
                    dve.wait_ge(up_mm, NX * (b - 1))
                for c in range(NC):
                    dve.wait_ge(xs_hi, NC * b + c + 1)
                    nc.vector.tensor_tensor(xs[b % 2][1][:, c, :], x2T[:, c, b * T:(b + 1) * T],
                                            xs[b % 2][0][:, c, :].bitcast(F32), ALU.subtract).then_inc(xs_lo, 1)
                dve.wait_ge(combT_hi, b + 1)
                nc.vector.tensor_tensor(combT[b % 2][32:32 + NE, :], misc_bank[0:NE, :],
                                        combT[b % 2][0:NE, :].bitcast(F32), ALU.subtract).then_inc(combT_lo, 1)

            def split_weights(e):
                dve.wait_ge(ex_hi, e + 1)
                nc.vector.tensor_tensor(wex[1][:, e, :], wstage[e % 2][:], wex[0][:, e, :].bitcast(F32),
                                        ALU.subtract).then_inc(ex_lo, 1)

            def add_rows(b, i):
                dve.wait_ge(yback_mm, 2 * b + i + 1)
                if b >= 1:
                    dve.wait_ge(out_done[i], 16 * b)
                rows = h_all[:, b * NT + 2 * i:b * NT + 2 * i + 2, :].rearrange("p t c -> p (t c)")
                nc.vector.tensor_tensor(outbuf[i][:].rearrange("p t c -> p (t c)"), misc_bank[:], rows,
                                        ALU.add).then_inc(sum_ready, 1)

            dve.wait_ge(att_done, 4)
            for p in range(2):
                nc.vector.memset(combT[p][:].bitcast(F32), 0.0).then_inc(combT_init, 1)
            dve.wait_ge(combT_init, 2)
            load_x(0)
            split_weights(0)
            for n in range(NS):
                b, k = n // NX, n % NX
                dve.wait_ge(silu_ready, n + 1)
                if order[k] < NE:
                    dve.wait_ge(spread_mm, routed_before[n] + 1)
                    nc.vector.tensor_tensor(gated[n % 2][:], gated[n % 2][:], spread_bank[:],
                                            ALU.mult).then_inc(weighted, 1)
                    dve.wait_ge(weighted, routed_before[n] + 1)
                dve.wait_ge(up_mm, n + 1)
                if n >= 2:
                    dve.wait_ge(hid_hi, n - 1)
                    dve.wait_ge(hid_lo, n - 1)
                nc.vector.tensor_tensor(hid[n % 2][:], up_banks[n % 2][:], gated[n % 2][:],
                                        ALU.mult).then_inc(hid_ready, 1)
                if n + 1 < NX:
                    split_weights(n + 1)
                dve.wait_ge(hid_hi, n + 1)
                nc.vector.tensor_tensor(hidr[n % 2][1][:], hid[n % 2][:], hidr[n % 2][0][:].bitcast(F32),
                                        ALU.subtract).then_inc(hid_lo, 1)
                if k == NX - 4 and b + 1 < B:
                    load_x(b + 1)
                if n >= NX and k == 0 and n < NS:
                    copy_y(dve, nc.vector.tensor_copy, b - 1, 1)
                if n >= NX and k in (2, 4):
                    add_rows(b - 1, k // 2 - 1)
            copy_y(dve, nc.vector.tensor_copy, B - 1, 1)
            for i in range(2):
                add_rows(B - 1, i)

        block = ctx.enter_context(nc.Block())

        @block.sync
        def _(sp):
            sp_setup(sp)
            attention(sp, "sp")
            sp_moe(sp)

        @block.gpsimd
        def _(pool):
            pool_setup(pool)
            attention(pool, "pool")
            pool.wait_ge(ln_rstd, len(norms))
            nc.gpsimd.memset(neghalf[:], 0.0).then_inc(att_done, 1)

        @block.tensor
        def _(pe):
            pe_setup(pe)
            attention(pe, "pe")
            nc.tensor.transpose(misc_bank[0:NE, 0:P], comb[:, 0, 0:NE], ident[:]).then_inc(att_done, 1)
            pe_moe(pe)

        @block.scalar
        def _(act):
            act_setup(act)
            attention(act, "act")
            nc.scalar.copy(rstd[:, 0:1], small[:, 0:1]).then_inc(att_done, 1)
            act_moe(act)

        @block.vector
        def _(dve):
            dve_setup(dve)
            attention(dve, "dve")
            dve.wait_ge(comb_ready, B)
            nc.vector.memset(pvs[:, 0:1], 0.0).then_inc(att_done, 1)
            dve_moe(dve)


def kernel(x, L0_tok_emb, L0_attn_c_attn_w, L0_attn_c_attn_b, L0_attn_q2l_w, L0_attn_q2l_b, L0_attn_kv2l_w,
           L0_attn_kv2l_b, L0_attn_l2o_w, L0_attn_l2o_b, L0_attn_wqk_w, L0_attn_wqk_b, L0_attn_cproj_w,
           L0_attn_cproj_b, L0_ffn_router_weight, L0_ffn_e_bias, L0_ffn_gate_w, L0_ffn_up_w, L0_ffn_down_w,
           L0_ffn_sh_gate_w, L0_ffn_sh_up_w, L0_ffn_sh_down_w):
    import concourse.bacc as bacc
    import ml_dtypes
    from concourse.bass_utils import run_bass_kernel_spmd

    f4 = np.float32
    arr = {}
    arr["tok"] = np.ascontiguousarray(np.asarray(x).reshape(B * NT, P).T)
    arr["emb"] = np.asarray(L0_tok_emb)

    pos = np.arange(T, dtype=f4)[:, None]
    col = np.arange(C)
    angle = pos / np.power(f4(10000.0), (2 * (col // 2)).astype(f4) / f4(C)).astype(f4)
    table = np.where(col % 2 == 0, np.sin(angle), np.cos(angle)).astype(f4)
    arr["pos_enc"] = np.ascontiguousarray(table.reshape(NT, P, C).transpose(1, 0, 2)).reshape(P, NT * C)
    inv_freq = (f4(1.0) / np.power(f4(10000.0), np.arange(0, L, 2, dtype=f4) / f4(L))).astype(f4)
    freqs = np.outer(np.arange(T, dtype=f4), inv_freq).astype(f4)
    const = {"rope_cos": np.tile(np.cos(freqs).T, (HALF, 1)).astype(f4),
             "rope_sin": np.tile(np.sin(freqs).T, (HALF, 1)).astype(f4)}
    arr["ident"] = np.eye(P, dtype=f4)
    later = np.tril(np.ones((P, P), f4), -1) * f4(-1e30)
    arr["masks"] = np.stack([np.eye(P), later, later.T], axis=1).astype(ml_dtypes.bfloat16)
    same = np.ones((P, NT, NE), f4)
    same[:, :, 0] = 0
    const["same_row"] = same
    const["earlier"] = np.broadcast_to(np.tril(np.ones((NGRP, NGRP), f4), -1), (P, NT, NGRP, NGRP))
    onehot = np.zeros((48, NE), f4)
    onehot[0:NE] = onehot[32:48] = np.eye(NE)
    arr["onehot"] = onehot

    bqkv, wq2l, wkv2l = (np.asarray(a) for a in (L0_attn_c_attn_b, L0_attn_q2l_w, L0_attn_kv2l_w))
    rows = np.asarray(L0_attn_c_attn_w).reshape(6, P, C).transpose(1, 0, 2)
    bd = np.zeros((HALF, HD, 2, 2, HALF, HD), f4)
    for h in range(HALF):
        for k, w in enumerate((wq2l, wkv2l)):
            for s in range(2):
                bd[h, :, k, s, h, :] = w[s::2].T
    arr["raw_qk"] = np.concatenate([rows[:, 0:4].reshape(P, 4 * C), bd.reshape(P, 4 * P)], axis=1)
    perm = np.concatenate([np.arange(0, L, 2), np.arange(1, L, 2)])
    wqk = np.asarray(L0_attn_wqk_w)
    qk = np.zeros((HALF, HD, 2, HALF, L), f4)
    for h in range(HALF):
        for s in range(2):
            qk[h, :, s, h, :] = wqk[perm][:, s::2].T
    cp = np.asarray(L0_attn_cproj_w).T.reshape(NC, P, C).transpose(1, 0, 2)
    block_mask = np.kron(np.eye(HALF), np.ones((HD, HD))).astype(f4)
    arr["raw_rest"] = np.concatenate([rows[:, 4:6].reshape(P, 2 * C), qk.reshape(P, 2 * HALF * L),
                                      cp.reshape(P, NC * C), block_mask], axis=1)
    arr["lat32"] = np.concatenate([np.tile(wkv2l, (1, HALF)), np.tile(np.asarray(L0_attn_l2o_w).T, (1, HALF)),
                                   np.asarray(L0_attn_kv2l_b)[:, None]], axis=1)
    small = np.zeros((P, 12), f4)
    small[:, 0:6] = bqkv.reshape(6, P).T
    for k, bias in enumerate((np.asarray(L0_attn_q2l_b), np.asarray(L0_attn_kv2l_b))):
        for s in range(2):
            small[:, 6 + 2 * k + s] = np.tile(bias[s::2], HALF)
    small[:, 10] = np.tile(np.asarray(L0_attn_wqk_b)[perm], GH)
    small[:, 11] = np.tile(np.asarray(L0_attn_l2o_b), HALF)
    const["small"] = small
    const["cproj_bias"] = np.broadcast_to(np.asarray(L0_attn_cproj_b), (P, C))
    const["router"] = np.asarray(L0_ffn_router_weight).T.reshape(NC, P, NE).transpose(1, 0, 2)
    const["ebias"] = np.tile(np.broadcast_to(np.asarray(L0_ffn_e_bias), (P, NE)), (1, NT))
    arr["consts"] = np.concatenate([const[name].reshape(P, cols) for name, cols in CONST_COLS.items()], axis=1)

    def rows_in_first(w):
        return w.transpose(0, 2, 1).reshape(-1, NC, P, I).transpose(0, 2, 1, 3).reshape(-1, P, NC * I)

    gate, up = (np.concatenate([np.asarray(a), np.asarray(s).reshape(NSH, I, C)]) for a, s in
                ((L0_ffn_gate_w, L0_ffn_sh_gate_w), (L0_ffn_up_w, L0_ffn_sh_up_w)))
    down = np.concatenate([np.asarray(L0_ffn_down_w).transpose(0, 2, 1),
                           np.asarray(L0_ffn_sh_down_w).T.reshape(NSH, I, C)])
    arr["experts"] = np.ascontiguousarray(np.concatenate([rows_in_first(gate), rows_in_first(up), down], axis=2))

    nc = bacc.Bacc("TRN2", target_bir_lowering=False, num_devices=1)
    from concourse import mybir as mb
    io = {n: nc.dram_tensor(f"in_{n}", a.shape, mb.dt.from_np(a.dtype), kind="ExternalInput").ap()
          for n, a in arr.items()}
    io["out"] = nc.dram_tensor("out_0", (B, T, C), F32, kind="ExternalOutput").ap()
    build_program(nc, io)
    r = run_bass_kernel_spmd(nc, [{f"in_{n}": a for n, a in arr.items()}], core_ids=[0])
    return r.results[0]["out_0"]
```

```python
from contextlib import ExitStack

import numpy as np

import concourse.bass as bass
from concourse import mybir

F32 = mybir.dt.float32
F32R = mybir.dt.float32r
BF16 = mybir.dt.bfloat16
I32 = mybir.dt.int32
ALU = mybir.AluOpType
ACT = mybir.ActivationFunctionType
AX_X = mybir.AxisListType.X

P = 128
B, T, C = 4, 512, 256
NT = T // P
NC = C // P
NH, HD, L = 16, 16, 32
GH = 4
NGB = NH // GH
NG = B * NGB
HALF = 8
NHALF = B * NH // HALF
NE, TOPK, NGRP = 16, 4, 4
EPG = NE // NGRP
NSH = 2
NX = NE + NSH
I = 128
WCOLS = 2 * NC * I + C
LN_EPS = 1e-5
ROUTE_SCALE = 2.5
SCORE_SCALE = float(L) ** -0.5
ST_UNITS = 10
P_SLOTS = 10
NSTACK = 3

ST_TILES = ([[(h, 0, 0)] for h in range(GH)]
            + [[(h, 1, 0), (h, 3, T - P)] for h in range(GH)]
            + [[(h, 2, 0), (h + 1, 2, T - 2 * P)] for h in (0, 2)])
VALUE_ORDER = (0, 1, 3, 2)
WHERE = {(h, j): (u, col) for u, tile in enumerate(ST_TILES) for h, j, col in tile}
MAX_TILES = ([(3, h, 1) for h in range(GH)] + [(2, h, 1) for h in range(GH)]
             + [(1, 0, 2), (1, 2, 2)] + [(0, 0, 4)])
NMX = len(MAX_TILES)
ROUTE_OPS = 32
ROUTE_BEFORE = (0, 3, 10, 14, 17, 21, 25, 29)
ROUTE_PARTS = len(ROUTE_BEFORE)
MAX_LEAD = 3

CONST_COLS = dict(cproj_bias=C, router=NC * NE, ebias=NT * NE, same_row=NT * NE,
                  earlier=NT * NGRP * NGRP, small=12)


def spread_over(main, extras):
    out, extras = [], sorted(extras, key=lambda extra: extra[0])
    for k, piece in enumerate(main):
        while extras and extras[0][0] * len(main) <= k:
            out.append(extras.pop(0)[1])
        out.append(piece)
    return out + [piece for _, piece in extras]


def attention_pieces():
    def both(kind, *piece):
        return [(kind, *piece, x) for x in range(2)]

    pieces = [("embed", 0), *both("stats", "norm1", 0), ("fold_qk", 0), ("xnorm", "norm1", 0), ("fold_qk", 1),
              ("fold_qk", 2), ("fold_qk", 3), ("xT", 0, 0), ("latent_biases",), ("xT", 0, 1), ("fold_values",),
              ("embed", 1), *both("bias", 0)]
    pieces += [*both("rope", 0), *both("rope_sum", 0), *both("rope_parts", 0), *both("rope", 1), ("latq", 0),
               ("latq_lo", 0), *both("rope_sum", 1), *both("rope_parts", 1), *both("rope", 2), *both("rope_sum", 2),
               ("latq", 1), ("latq_lo", 1), ("fold_rest",), *both("rope_parts", 2), *both("stats", "norm1", 1),
               *both("vproj", 0), *both("rope", 3), *both("rope_sum", 3)]
    pieces += spread_over([("max", 0, u) for u in range(NMX)] + [("maxT", 0)],
                          [(0.40, ("rope_parts", 3, 0)), (0.45, ("rope_parts", 3, 1)), (0.68, ("xnorm", "norm1", 1)),
                           (0.85, ("bias", 1, 0)), (0.90, ("bias", 1, 1)), (0.90, ("embed", 2))])
    for g in range(NG):
        b, phase, main, extras = g // NGB, g % NGB, [], []
        if g >= 1:
            extras += [(0.00, ("values", g - 1, 1)), (0.00, ("maxT", g)),
                       (0.00, ("values", g - 1, 3)), (0.00, ("values", g - 1, 2)),
                       (0.00, ("pv_out", g - 1))]
            extras.append((0.37, ("renorm", g - 1)))
        if g + 2 < NG:
            extras += [((0.08, 0.08)[g % 2], ("latq", g + 2)), ((0.12, 0.10)[g % 2], ("latq_lo", g + 2))]
        if g + 4 < 2 * NHALF:
            places = ((0.49, 0.50, 0.52, 0.55, 0.89, 0.99), (0.07, 0.20, 0.28, 0.35, 0.50, 0.64))[g % 2]
            rope = [("rope", g + 4, s) for s in range(2)]
            rope += [(kind, g + 4, x) for kind in ("rope_sum", "rope_parts") for x in range(2)]
            extras += list(zip(places, rope))
        if phase == 0 and b >= 1:
            extras += [(0.00, ("vproj", b, 0)), (0.18, ("vproj", b, 1))]
        if phase == 0 and b + 1 < B:
            extras += [(0.25, ("xT", b + 1, 0)), (0.33, ("xT", b + 1, 1))]
        if phase == 3 and b + 2 < B:
            extras += [(0.02, ("stats", "norm1", b + 2, 0)), (0.49, ("stats", "norm1", b + 2, 1)),
                       (0.70, ("xnorm", "norm1", b + 2)),
                       (0.80, ("bias", b + 2, 0)), (0.90, ("bias", b + 2, 1))]
            if b + 3 < B:
                extras.append((0.73, ("embed", b + 3)))
        if b >= 1:
            extras += [[(0.77, ("yT", b - 1, 0)), (0.95, ("yT", b - 1, 1))],
                       [(0.30, ("cproj", b - 1, 0)), (0.50, ("cproj", b - 1, 1)), (0.56, ("stats", "tail", b - 1, 0)),
                        (0.67, ("stats", "tail", b - 1, 1)),
                        (0.94, ("xnorm", "tail", b - 1))],
                       [(0.07, ("x2T", b - 1, 0)), (0.12, ("x2T", b - 1, 1)), (0.31, ("router", b - 1))]
                       + [(at, ("route", b - 1, k)) for k, at in enumerate((0.35, 0.65, 0.72, 0.93, 0.99))],
                       [(at, ("route", b - 1, k)) for k, at in ((5, 0.55), (6, 0.72), (7, 0.89))]][phase]
        for u in range(NMX + MAX_LEAD):
            if g + 1 < NG and u < NMX:
                main.append(("max", g + 1, u))
            if 0 <= u - MAX_LEAD + 1 < ST_UNITS:
                main.append(("score", g, u - MAX_LEAD + 1))
                if u - MAX_LEAD + 1 == 6:
                    main.append(("values", g, 0))
        if g == NG - 1:
            extras += [(0.00, ("load_x", 0)), (0.14, ("combT", 0)), (0.30, ("weights", 0)), (0.99, ("weights", 1))]
        if g == NG - 2:
            extras += [(0.65, ("stage", 0)), (0.72, ("stage", 1))]
        pieces += spread_over(main, extras)
    g, b = NG - 1, B - 1
    pieces += [("values", g, j) for j in VALUE_ORDER[1:]] + [("pv_out", g), ("gate_up", 0), ("renorm", g)]
    return pieces + [("hidden", 0), ("yT", b, 0), ("yT", b, 1)]


def moe_pieces():
    b = B - 1
    last = ([("cproj", b, 0), ("cproj", b, 1), ("stats", "tail", b, 0), ("stats", "tail", b, 1)]
            + [("xnorm", "tail", b), ("x2T", b, 0), ("x2T", b, 1), ("router", b)]
            + [("route", b, k) for k in range(ROUTE_PARTS)])
    pieces = [("stage", 2), ("stage", 3), ("weights", 2), ("stage", 4), ("spread", NSH)]
    for n in range(1, B * NX):
        b, k = divmod(n, NX)
        pieces.append(("gate_up", n))
        if n + 2 < NX:
            pieces.append(("weights", n + 2))
        if n + 4 < NX:
            pieces.append(("stage", n + 4))
        pieces.append(("hidden", n))
        if n + 2 < B * NX:
            pieces.append(("spread", n + 2))
        pieces += last[0:1]
        last = last[1:]
        if k == NX - 5 and b + 1 < B:
            pieces += [("combT", b + 1), ("load_x", b + 1)]
        if b >= 1 and k == 0:
            pieces.append(("copy_y", b - 1))
        if b >= 1 and k in (2, 4):
            pieces.append(("back", b - 1, k // 2 - 1))
    return pieces + [("down", B * NX - 1), ("copy_y", B - 1), ("back", B - 1, 0), ("back", B - 1, 1)]


def fill_order(pieces):
    fills = [p for p in pieces if p[0] in ("xT", "yT", "x2T", "cproj", "vproj", "rope", "latq", "maxT", "router",
                                           "renorm", "combT", "back")]
    return {name: k for k, name in enumerate(fills)}


def passes(w, x):
    return (w[0], x[0]), (w[1], x[0]), (w[0], x[1])


def build_program(nc, io):
    attention, experts = attention_pieces(), moe_pieces()
    pieces = attention + experts
    fills = fill_order(pieces)
    n_alternate = sum(piece in fills for piece in attention)
    fill_names = list(fills)
    norms = [piece[1:] for piece in pieces if piece[0] == "xnorm"]
    with ExitStack() as ctx:
        def sem(name):
            return ctx.enter_context(nc.semaphore(name))

        def sb(scope, name, shape, dt=F32):
            return scope.enter_context(nc.sbuf_tensor(name, shape, dt))

        def pair(scope, name, shape):
            return [sb(scope, f"{name}_{x}", shape, F32R) for x in ("hi", "lo")]

        ident = sb(ctx, "ident", [P, P])
        h_all = sb(ctx, "h_all", [P, B * NT, C])
        x2T = sb(ctx, "x2T", [P, NC, B * T])
        comb = sb(ctx, "comb", [P, B, NT * NE])

        tok_idx = sb(ctx, "tok_idx", [P, B * NT], I32)
        consts = sb(ctx, "consts", [P, sum(CONST_COLS.values())])
        masks = sb(ctx, "masks", [P, 3, P], BF16)
        wcp = pair(ctx, "wcp", [P, NC, C])
        blat = sb(ctx, "blat", [P, 8])
        vconst = sb(ctx, "vconst", [P, NC])
        stats = sb(ctx, "stats", [P, NT, 6])
        meanvar = sb(ctx, "meanvar", [P, NT, 2])
        rstd = sb(ctx, "rstd", [P, NT])
        neghalf = sb(ctx, "neghalf", [P, NT])
        xn = sb(ctx, "xn", [P, NT, C])
        rowmax = sb(ctx, "rowmax", [P, GH, NT])
        rden = sb(ctx, "rden", [P, NT, GH])
        ytok = sb(ctx, "ytok", [P, NT, C])
        yT = pair(ctx, "yT", [P, NC, T])
        rt = sb(ctx, "rt", [P, 12, NT * NE])

        att = ctx.enter_context(ExitStack())
        wlat = pair(att, "wlat", [P, 2, 2, NC, 2, P])
        wval = pair(att, "wval", [P, NC, C])
        wqk = pair(att, "wqk", [P, 2, HALF, L])
        xT = pair(att, "xT", [P, NC, T])
        rope_cos = sb(att, "rope_cos", [P, T])
        rope_sin = sb(att, "rope_sin", [P, T])
        prod = sb(att, "prod", [P, 4, T])
        qrope = pair(att, "qrope", [P, 2, T])
        krope = pair(att, "krope", [P, 2, T])
        qlat = pair(att, "qlat", [P, T])
        pos_enc = sb(att, "pos_enc", [P, NT * C])
        lat32 = sb(att, "lat32", [L, 2 * P + 1])
        qstack = [sb(att, f"qstack{p}", [97, GH, T], F32R) for p in range(NSTACK)]
        kstack = [sb(att, f"kstack{p}", [97, GH, T], F32R) for p in range(NSTACK)]
        rowmaxT = sb(att, "rowmaxT", [NT * GH, P], F32R)
        val = sb(att, "val", [P, NT, NH, L])
        probs = sb(att, "probs", [P, P_SLOTS, T])
        pvs = sb(att, "pvs", [P, T])

        cut, parts = 0, {}
        for name, cols in CONST_COLS.items():
            parts[name] = consts[:, cut:cut + cols]
            cut += cols
        cproj_bias, small = parts["cproj_bias"], parts["small"]
        router_w = parts["router"].rearrange("p (c e) -> p c e", c=NC)
        ebias, same_row = parts["ebias"], parts["same_row"]
        earlier = parts["earlier"].rearrange("p (t i j) -> p t i j", t=NT, i=NGRP)
        ident_b, mask_kq, mask_qk = (masks[:, k, :] for k in range(3))

        ring = probs[:, :, :].rearrange("p s t -> p (s t)")
        cuts = np.cumsum([0, 4 * C, 4 * P, 2 * C, 2 * HALF * L, NC * C, P, P]).tolist()
        raw_qk, raw_rest = ring[:, 0:cuts[2]], ring[:, cuts[2]:cuts[6]]
        raw = [ring[:, a:b] for a, b in zip(cuts[:-1], cuts[1:])]
        raw_rows = raw[0].rearrange("p (n c) -> p n c", n=4)
        raw_bd = raw[1].rearrange("p (x c) -> p x c", x=2)
        raw_vrows = raw[2].rearrange("p (n c) -> p n c", n=2)
        raw_wqk, raw_wcp, block_mask, l2o_kv2l = raw[3:7]

        k_dram = nc.dram_tensor("k_dram", (2, 2, 2, HD, HALF, T), F32, kind="Internal").ap()
        comb_dram = nc.dram_tensor("comb_dram", (B, NE, T), F32, kind="Internal").ap()
        q_dram = nc.dram_tensor("q_dram", (2, 2, L, GH, T), F32, kind="Internal").ap()

        banks = [ctx.enter_context(nc.psum_tensor(f"bank{i}", [P, T], F32)) for i in range(8)]
        work_banks, st_banks, mx_banks, pv_bank = banks[0:2], banks[2:5], banks[5:7], banks[7]
        gate_banks, up_banks, y_banks = banks[2:4], banks[5:7], (banks[7], banks[0])
        fold_banks = banks[2:7]

        tok_in, raw_qk_in, raw_in, consts_in = sem("tok_in"), sem("raw_qk_in"), sem("raw_in"), sem("consts_in")
        const_in = sem("const_in")
        pos_in, ident_in = sem("pos_in"), sem("ident_in")
        rows_in = [sem(f"rows_in{b}") for b in range(B)]
        ones_init, half_init, minus_ready = sem("ones_init"), sem("half_init"), sem("minus_ready")
        m_mm, m_ready = sem("m_mm"), sem("m_ready")
        fold_mm, fold_hi, fold_lo = sem("fold_mm"), sem("fold_hi"), sem("fold_lo")
        bias_ready, raw_hi, raw_lo = sem("bias_ready"), sem("raw_hi"), sem("raw_lo")
        h_ready, h_biased, h2_ready = sem("h_ready"), sem("h_biased"), sem("h2_ready")
        ln_stats, ln_aggr, ln_eps, ln_rstd = sem("ln_stats"), sem("ln_aggr"), sem("ln_eps"), sem("ln_rstd")
        xn_ready = sem("xn_ready")
        filled = sem("filled")
        xT_hi, xT_lo = sem("xT_hi"), sem("xT_lo")
        prod_ready, sum_roped, rope_hi, rope_lo = sem("prod_ready"), sem("sum_roped"), sem("rope_hi"), sem("rope_lo")
        latq_hi, latq_lo = sem("latq_hi"), sem("latq_lo")
        k_stored, q_stored = ([sem(f"{x}_stored{p}") for p in range(2)] for x in "kq")
        stack_in = [sem(f"stack_in{p}") for p in range(NSTACK)]
        maxrow_in = [sem(f"maxrow_in{p}") for p in range(NSTACK)]
        mx_mm, mx_red, maxT_ready = sem("mx_mm"), sem("mx_red"), sem("maxT_ready")
        st_mm, st_exp = sem("st_mm"), sem("st_exp")
        val_ready, pv_mm = sem("val_ready"), sem("pv_mm")
        pv_copied, rden_ready, ytok_ready = sem("pv_copied"), sem("rden_ready"), sem("ytok_ready")
        y_hi, y_lo = sem("y_hi"), sem("y_lo")
        x2T_ready, sig_ready, routed = sem("x2T_ready"), sem("sig_ready"), sem("routed")
        comb_ready = sem("comb_ready")
        wstage_in = [sem(f"wstage_in{i}") for i in range(2)]
        ex_hi, ex_lo = sem("ex_hi"), sem("ex_lo")
        xs_hi, xs_lo = sem("xs_hi"), sem("xs_lo")
        combT_ready, comb_stored = sem("combT_ready"), sem("comb_stored")
        spread_in = [sem(f"spread_in{p}") for p in range(2)]
        gate_mm, up_mm, down_mm = sem("gate_mm"), sem("up_mm"), sem("down_mm")
        silu_ready, weighted, hid_ready = sem("silu_ready"), sem("weighted"), sem("hid_ready")
        hid_hi, hid_lo = sem("hid_hi"), sem("hid_lo")
        y_copied = [sem(f"y_copied{c}") for c in range(NC)]
        sum_ready = sem("sum_ready")
        out_done = [sem(f"out_done{i}") for i in range(2)]

        BQKV, LATB, WQKB, L2OB = 0, 6, 10, 11
        STACK_DMAS = 4

        def is_q(u):
            return u % 2 == (u >= 2)

        def parts_of(n, q):
            return 2 * (2 * n + (1 if q == (n >= 1) else 0)) + 2

        EARLY_ROPES = 2
        FOLDS = (0, 2, 3, 1)

        def hof(g):
            return g % 2 * GH

        def wait_stack(eng, g):
            eng.wait_ge(stack_in[g % NSTACK], 16 * STACK_DMAS * (g // NSTACK + 1))

        def wait_maxrow(eng, g):
            eng.wait_ge(maxrow_in[g % NSTACK], 16 * (g // NSTACK + 1))

        def wait_read(eng, name):
            kind, n = name[0], name[1]
            if kind == "xT":
                eng.wait_ge(xT_hi, NC * n + name[2] + 1)
                eng.wait_ge(xT_lo, NC * n + name[2] + 1)
            elif kind == "rope":
                eng.wait_ge(prod_ready, 4 * n + 2 * (name[2] + 1))
            elif kind == "latq":
                eng.wait_ge(latq_hi, n + 1)
                eng.wait_ge(latq_lo, n + 1)
            elif kind == "maxT":
                eng.wait_ge(maxT_ready, n + 1)
            elif kind == "renorm":
                eng.wait_ge(ytok_ready, n + 1)
            elif kind == "yT":
                eng.wait_ge(y_hi, NC * n + name[2] + 1)
                eng.wait_ge(y_lo, NC * n + name[2] + 1)
            elif kind == "vproj":
                eng.wait_ge(val_ready, NT // 2 * n + name[2] + 1)
            elif kind == "cproj":
                eng.wait_ge(h2_ready, NT // 2 * n + name[2] + 1)
            elif kind == "x2T":
                eng.wait_ge(x2T_ready, NC * n + name[2] + 1)
            elif kind == "router":
                eng.wait_ge(sig_ready, n + 1)
            elif kind == "combT":
                eng.wait_ge(combT_ready, n + 1)
            elif kind == "back":
                eng.wait_ge(sum_ready, NT // 2 * n + name[2] + 1)

        def work_bank(k):
            return work_banks[k % 2 if k < n_alternate else 1]

        def bank_to_fill(pe, name):
            k = fills[name]
            if k > n_alternate:
                wait_read(pe, fill_names[k - 1])
            elif k == n_alternate:
                wait_read(pe, fill_names[k - 2])
                wait_read(pe, fill_names[k - 1])
            elif k >= 2:
                wait_read(pe, fill_names[k - 2])
            return work_bank(k)

        def filled_bank(eng, name):
            eng.wait_ge(filled, fills[name] + 1)
            return work_bank(fills[name])

        def sp_setup(sp):
            sp.dma_start(tok_idx[:], io["tok"]).then_inc(tok_in, 16)
            sp.dma_start(raw_qk, io["raw_qk"]).then_inc(raw_qk_in, 16)
            sp.dma_start(pos_enc[:], io["pos_enc"]).then_inc(pos_in, 16)
            sp.dma_start(ident[:], io["ident"]).then_inc(ident_in, 16)
            sp.wait_ge(rows_in[0], 16 * NT)
            for dst, name in ((consts[:], "consts"), (rope_cos[:], "rope_cos"), (rope_sin[:], "rope_sin")):
                sp.dma_start(dst, io[name]).then_inc(const_in, 16)
            sp.dma_start(lat32[:], io["lat32"]).then_inc(consts_in, 16)
            sp.dma_start(raw_rest, io["raw_rest"]).then_inc(raw_in, 16)
            sp.dma_start(masks[:], io["masks"]).then_inc(consts_in, 16)

        def sp_latq(sp, g):
            n, kp, qp, heads = g // 2, g // 2 % 2, g % 2, slice(hof(g), hof(g) + GH)

            def store_k():
                sp.wait_ge(rope_hi, parts_of(n, False))
                sp.wait_ge(rope_lo, parts_of(n, False))
                if n >= 2:
                    wait_stack(sp, g - 3)
                for x in range(2):
                    for s in range(2):
                        sp.dma_start(k_dram[kp, x, s].rearrange("f h t -> h f t"),
                                     krope[x][:, s, :].bitcast(F32)).then_inc(k_stored[kp], 16)

            def store_q():
                sp.wait_ge(latq_hi, g + 1)
                sp.wait_ge(latq_lo, g + 1)
                if g >= 2:
                    wait_stack(sp, g - 2)
                for x in range(2):
                    sp.dma_start(q_dram[qp, x].rearrange("l h t -> h l t"),
                                 qlat[x][:].bitcast(F32)).then_inc(q_stored[qp], 16)

            if g == 0:
                store_q()
            if g % 2 == 0:
                store_k()
            if g >= NSTACK:
                sp.wait_ge(st_mm, ST_UNITS * (g - NSTACK + 1))
            sp.wait_ge(k_stored[kp], 64 * (n // 2 + 1))
            rows = k_dram[kp].rearrange("x s f h t -> (x s f) h t")
            stack_q, stack_k = qstack[g % NSTACK], kstack[g % NSTACK]
            sp.dma_start(stack_k[0:2 * L, :, :].bitcast(F32), rows[:, heads, :]).then_inc(stack_in[g % NSTACK], 16)
            sp.dma_start(stack_k[2 * L:3 * L, :, :].bitcast(F32),
                         rows[0:L, heads, :]).then_inc(stack_in[g % NSTACK], 16)
            if g >= 1:
                store_q()
            sp.wait_ge(q_stored[qp], 32 * (g // 2 + 1))
            sp.dma_start(stack_q[0:2 * L, :, :].bitcast(F32),
                         q_dram[qp, 0].unsqueeze(0).broadcast_to([2, L, GH, T])).then_inc(stack_in[g % NSTACK], 16)
            sp.dma_start(stack_q[2 * L:3 * L, :, :].bitcast(F32), q_dram[qp, 1]).then_inc(stack_in[g % NSTACK], 16)

        def sp_maxT(sp, g):
            sp.wait_ge(maxT_ready, g + 1)
            sp.dma_start(qstack[g % NSTACK][96:97, :, :].rearrange("o h (i t) -> o (h i) t", t=P).bitcast(F32),
                         rowmaxT[:].bitcast(F32)).then_inc(maxrow_in[g % NSTACK], 16)

        def embed(eng, tt, b):
            eng.wait_ge(rows_in[b], 16 * NT)
            eng.wait_ge(pos_in, 16)
            rows = h_all[:, b * NT:(b + 1) * NT, :]
            tt(rows, rows, pos_enc[:].rearrange("p (t c) -> p t c", t=NT), ALU.add).then_inc(h_ready, 1)

        def pool_gather(pool, b):
            for t in range(NT * b, NT * b + NT):
                nc.gpsimd.indirect_dma_start(
                    out=h_all[:, t, :], out_offset=None, in_=io["emb"],
                    in_offset=bass.IndirectOffsetOnAxis(ap=tok_idx[:, t:t + 1], axis=0)).then_inc(rows_in[b], 16)

        def pool_setup(pool):
            nc.gpsimd.memset(neghalf[:], -0.5).then_inc(half_init, 1)
            pool.wait_ge(tok_in, 16)
            pool_gather(pool, 0)
            pool_gather(pool, 1)
            pool.wait_ge(half_init, 1)

        def pool_stats(pool, kind, b, part):
            if part == 0:
                return
            m = norms.index((kind, b))
            pool.wait_ge(ln_aggr, NT * (m + 1))
            if m >= 1:
                pool.wait_ge(xn_ready, NT * m)
            nc.gpsimd.tensor_scalar(rstd[:], meanvar[:, :, 1], LN_EPS, None, ALU.add).then_inc(ln_eps, 1)
            pool.wait_ge(ln_eps, m + 1)
            nc.gpsimd.tensor_tensor(rstd[:], rstd[:], neghalf[:], ALU.pow).then_inc(ln_rstd, 1)
            if m == 0:
                pool_gather(pool, 2)
                pool_gather(pool, 3)
                nc.gpsimd.memset(val[:, :, :, HD:L], 1.0).then_inc(ones_init, 1)

        def pool_embed(pool, b):
            if b >= 1:
                embed(pool, nc.gpsimd.tensor_tensor, b)

        def pool_bias(pool, b, i):
            if b == 0:
                pool.wait_ge(const_in, 48)
            pool.wait_ge(xn_ready, NT * (norms.index(("norm1", b)) + 1))
            for t in range(b * NT + 2 * i, b * NT + 2 * i + 2):
                nc.gpsimd.tensor_tensor(h_all[:, t, :], h_all[:, t, :], cproj_bias, ALU.add).then_inc(h_biased, 1)

        def rope_sum(eng, tt, u, x):
            eng.wait_ge(prod_ready, 4 * (u + 1))
            tt(prod[:, x, :], prod[:, x, :], prod[:, 3 - x, :], (ALU.subtract, ALU.add)[x]).then_inc(sum_roped, 1)

        def rope_lo_part(eng, tt, u, x):
            hi, lo = qrope if is_q(u) else krope
            if u >= 2:
                wait_rope_used(eng, u)
            eng.wait_ge(rope_hi, 2 * u + x + 1)
            tt(lo[:, x, :], prod[:, x, :], hi[:, x, :].bitcast(F32), ALU.subtract).then_inc(rope_lo, 1)

        def pool_rope_sum(pool, u, x):
            if u >= EARLY_ROPES:
                rope_sum(pool, nc.gpsimd.tensor_tensor, u, x)

        def pool_rope_parts(pool, u, x):
            if u >= EARLY_ROPES:
                rope_lo_part(pool, nc.gpsimd.tensor_tensor, u, x)

        def dve_embed(dve, b):
            if b == 0:
                embed(dve, nc.vector.tensor_tensor, b)

        def dve_rope_sum(dve, u, x):
            if u < EARLY_ROPES:
                rope_sum(dve, nc.vector.tensor_tensor, u, x)

        def dve_rope_parts(dve, u, x):
            if u < EARLY_ROPES:
                rope_lo_part(dve, nc.vector.tensor_tensor, u, x)

        def pe_setup(pe):
            pe.wait_ge(raw_qk_in, 16)
            for k in FOLDS:
                kq, hf = k // 2, k % 2
                for c in range(NC):
                    mm = nc.tensor.matmul(fold_banks[k][:, c * C:(c + 1) * C],
                                          raw_rows[:, k, c * P:(c + 1) * P], raw_bd[:, kq, :], start=True, stop=True)
                mm.then_inc(fold_mm, 1)
            pe.wait_ge(const_in, 48)
            for k in range(8):
                mm = nc.tensor.matmul(pv_bank[:, k:k + 1], raw_bd[:, k // 4, k % 2 * P:(k % 2 + 1) * P],
                                      small[:, BQKV + k // 2:BQKV + k // 2 + 1], start=True, stop=True)
            mm.then_inc(fold_mm, 1)

        def pe_fold_values(pe):
            pe.wait_ge(consts_in, 32)
            pe.wait_ge(bias_ready, 1)
            nc.tensor.matmul(pv_bank[:, 0:P], lat32[:, 0:P], lat32[:, P:2 * P], start=True,
                             stop=True).then_inc(m_mm, 1)

        def pe_fold_rest(pe):
            pe.wait_ge(raw_in, 16)
            pe.wait_ge(m_ready, 1)
            for c in range(NC):
                for hf in range(2):
                    mm = nc.tensor.matmul(fold_banks[4][:, c * C + hf * P:c * C + (hf + 1) * P],
                                          raw_vrows[:, hf, c * P:(c + 1) * P], l2o_kv2l, start=True, stop=True)
            mm.then_inc(fold_mm, 1)
            for c in range(NC):
                col = pv_bank[:, c:c + 1]
                nc.tensor.matmul(col, l2o_kv2l, small[:, BQKV + 4 + c:BQKV + 5 + c], start=True, stop=False)
                mm = nc.tensor.matmul(col, lat32[:, P:2 * P], lat32[:, 2 * P:2 * P + 1], start=False, stop=True)
            mm.then_inc(fold_mm, 1)

        def pe_transposes(pe, kind, b, c, rows):
            bank = bank_to_fill(pe, (kind, b, c))
            for i in range(NT):
                mm = nc.tensor.transpose(bank[:, i * P:(i + 1) * P], rows[:, i, c * P:(c + 1) * P], ident[:])
            mm.then_inc(filled, 1)

        def pe_xT(pe, b, c):
            if b == 0:
                pe.wait_ge(ident_in, 16)
            pe.wait_ge(xn_ready, NT * (norms.index(("norm1", b)) + 1))
            pe_transposes(pe, "xT", b, c, xn)

        def pe_x2T(pe, b, c):
            pe.wait_ge(xn_ready, NT * (norms.index(("tail", b)) + 1))
            pe_transposes(pe, "x2T", b, c, xn)

        def pe_yT(pe, b, c):
            pe.wait_ge(ytok_ready, NGB * (b + 1))
            pe_transposes(pe, "yT", b, c, ytok)

        def pe_rope(pe, u, s):
            n = u // 2
            pe.wait_ge(xT_hi, NC * (n // 2 + 1))
            pe.wait_ge(xT_lo, NC * (n // 2 + 1))
            if n < 2:
                pe.wait_ge(fold_hi, u + 1)
                pe.wait_ge(fold_lo, u + 1)
            bank = bank_to_fill(pe, ("rope", u, s))
            kq = 0 if is_q(u) else 1
            terms = [(w[:, kq, n % 2, c, s, :], x[:, c, :]) for c in range(NC) for w, x in passes(wlat, xT)]
            for k, (w, x) in enumerate(terms):
                mm = nc.tensor.matmul(bank[:], w, x, start=(k == 0), stop=(k == len(terms) - 1))
            mm.then_inc(filled, 1)

        def pe_latq(pe, g):
            pe.wait_ge(rope_hi, parts_of(g // 2, True))
            pe.wait_ge(rope_lo, parts_of(g // 2, True))
            if g == 0:
                pe.wait_ge(raw_hi, 1)
                pe.wait_ge(raw_lo, 1)
            bank = bank_to_fill(pe, ("latq", g))
            terms = [(w[:, s, hof(g):hof(g) + GH, :], x[:, s, :]) for s in range(2) for w, x in passes(wqk, qrope)]
            for k, (w, x) in enumerate(terms):
                mm = nc.tensor.matmul(bank[:], w, x, start=(k == 0), stop=(k == len(terms) - 1))
            mm.then_inc(filled, 1)

        def pe_max(pe, g, u):
            i, h0, heads = MAX_TILES[u]
            k = g * NMX + u
            if u == 0:
                wait_stack(pe, g)
                if g == 0:
                    pe.wait_ge(fold_hi, 5)
                    pe.wait_ge(fold_lo, 5)
            if k >= 2:
                pe.wait_ge(mx_red, k - 1)
            bank, width = mx_banks[k % 2], P * (i + 1)
            for h in range(heads):
                col = h * width
                nc.tensor.matmul(bank[:, col:col + width], qstack[g % NSTACK][0:96, h0 + h, i * P:(i + 1) * P],
                                 kstack[g % NSTACK][0:96, h0 + h, 0:width], start=True, stop=False)
                mm = nc.tensor.matmul(bank[:, col + i * P:col + width], ident_b, mask_qk, start=False, stop=True)
            mm.then_inc(mx_mm, 1)

        def pe_maxT(pe, g):
            bank = bank_to_fill(pe, ("maxT", g))
            pe.wait_ge(mx_red, NMX * (g + 1))
            nc.tensor.transpose(bank[0:NT * GH, 0:P], rowmax[:], ident[:]).then_inc(filled, 1)

        def pe_score(pe, g, u):
            if u == 0:
                wait_maxrow(pe, g)
            if g == 0:
                pe.wait_ge(minus_ready, NSTACK)
            k = g * ST_UNITS + u
            if k >= 3:
                pe.wait_ge(st_exp, k - 2)
            bank = st_banks[k % 3]
            for h, j, col in ST_TILES[u]:
                nc.tensor.matmul(bank[:, col:col + T - P * j], kstack[g % NSTACK][:, h, j * P:(j + 1) * P],
                                 qstack[g % NSTACK][:, h, j * P:T], start=True, stop=False)
                mm = nc.tensor.matmul(bank[:, col:col + P], ident_b, mask_kq, start=False, stop=True)
            mm.then_inc(st_mm, 1)

        def pe_values(pe, g, j):
            pe.wait_ge(st_exp, ST_UNITS * g + 1 + max(WHERE[(h, j)][0] for h in range(GH)))
            if j == 0:
                if g % NGB == 0:
                    pe.wait_ge(val_ready, NT // 2 * (g // NGB + 1))
                if g >= 1:
                    pe.wait_ge(pv_copied, g)
                else:
                    pe.wait_ge(bias_ready, 2)
            for h in range(GH):
                u, col = WHERE[(h, j)]
                mm = nc.tensor.matmul(pv_bank[32 * h:32 * h + 32, j * P:T], val[:, j, g % NGB * GH + h, :],
                                      probs[:, (g * ST_UNITS + u) % P_SLOTS, col:col + T - P * j],
                                      start=(j == VALUE_ORDER[0]), stop=(j == VALUE_ORDER[-1]))
            mm.then_inc(pv_mm, 1)

        def pe_renorm(pe, g):
            bank = bank_to_fill(pe, ("renorm", g))
            pe.wait_ge(pv_copied, g + 1)
            for i in range(NT):
                mm = nc.tensor.transpose(bank[:, i * P:(i + 1) * P], pvs[:, i * P:(i + 1) * P], ident[:])
            mm.then_inc(filled, 1)

        def pe_token_rows(pe, kind, b, i, lhs, w):
            bank = bank_to_fill(pe, (kind, b, i))
            for t in range(2):
                tok = (2 * i + t) * P
                terms = [(x[:, c, tok:tok + P], y[:, c, :]) for c in range(NC) for x, y in passes(lhs, w)]
                for k, (x, y) in enumerate(terms):
                    mm = nc.tensor.matmul(bank[:, t * C:(t + 1) * C], x, y, start=(k == 0),
                                          stop=(k == len(terms) - 1))
            mm.then_inc(filled, 1)

        def pe_vproj(pe, b, i):
            if b == 0:
                pe.wait_ge(fold_hi, 5)
                pe.wait_ge(fold_lo, 5)
            pe_token_rows(pe, "vproj", b, i, xT, wval)

        def pe_cproj(pe, b, i):
            if b == 0:
                pe.wait_ge(raw_hi, 2)
                pe.wait_ge(raw_lo, 2)
            pe.wait_ge(y_hi, NC * (b + 1))
            pe.wait_ge(y_lo, NC * (b + 1))
            pe_token_rows(pe, "cproj", b, i, yT, wcp)

        def pe_router(pe, b):
            pe.wait_ge(x2T_ready, NC * (b + 1))
            bank = bank_to_fill(pe, ("router", b))
            for i in range(NT):
                tok = b * T + i * P
                for c in range(NC):
                    mm = nc.tensor.matmul(bank[:, i * NE:(i + 1) * NE], x2T[:, c, tok:tok + P], router_w[:, c, :],
                                          start=(c == 0), stop=(c == NC - 1))
            mm.then_inc(filled, 1)

        def act_fold_qk(act, n):
            act.wait_ge(fold_mm, n + 1)
            nc.scalar.copy(folded(0, FOLDS[n]), fold_banks[FOLDS[n]][:]).then_inc(fold_hi, 1)

        def act_fold_values(act):
            act.wait_ge(raw_in, 16)
            nc.scalar.copy(wqk[0][:].rearrange("p s h l -> p (s h l)"), raw_wqk).then_inc(raw_hi, 1)

        def act_fold_rest(act):
            nc.scalar.copy(wcp[0][:].rearrange("p g c -> p (g c)"), raw_wcp).then_inc(raw_hi, 1)
            act.wait_ge(fold_mm, 6)
            nc.scalar.copy(folded(0, 4), fold_banks[4][:]).then_inc(fold_hi, 1)

        def wait_rope_used(eng, u):
            n = u // 2
            if u % 2 == 0:
                eng.wait_ge(k_stored[(n - 1) % 2], 64 * ((n - 1) // 2 + 1))
            else:
                eng.wait_ge(filled, fills[("latq", 2 * n - 1)] + 1)

        def folded(part, k):
            return wlat[part][:, k // 2, k % 2, :, :, :].rearrange("p c s r -> p (c s r)") if k < 4 else \
                wval[part][:].rearrange("p c n -> p (c n)")

        def act_xT(act, b, c):
            if b >= 1:
                act.wait_ge(filled, fills[("vproj", b - 1, NT // 2 - 1)] + 1)
            bank = filled_bank(act, ("xT", b, c))
            nc.scalar.copy(xT[0][:, c, :], bank[:]).then_inc(xT_hi, 1)

        def act_rope_parts(act, u, x):
            act.wait_ge(sum_roped, 2 * u + x + 1)
            if u >= 2:
                wait_rope_used(act, u)
            nc.scalar.copy((qrope if is_q(u) else krope)[0][:, x, :], prod[:, x, :]).then_inc(rope_hi, 1)

        def act_latq(act, g):
            if g == 0:
                act.wait_ge(const_in, 48)
            else:
                act.wait_ge(q_stored[(g - 1) % 2], 32 * ((g - 1) // 2 + 1))
            bank = filled_bank(act, ("latq", g))
            nc.scalar.activation(qlat[0][:], bank[:], ACT.Identity, bias=small[:, WQKB:WQKB + 1]).then_inc(latq_hi, 1)

        def act_score(act, g, u):
            k = g * ST_UNITS + u
            act.wait_ge(st_mm, k + 1)
            if k >= P_SLOTS:
                gg, uu = divmod(k - P_SLOTS, ST_UNITS)
                act.wait_ge(pv_mm, NT * gg + 1 + max(VALUE_ORDER.index(j) for _, j, _ in ST_TILES[uu]))
            nc.scalar.activation(probs[:, k % P_SLOTS, :], st_banks[k % 3][:], ACT.Exp,
                                 scale=SCORE_SCALE).then_inc(st_exp, 1)

        def act_pv_out(act, g):
            act.wait_ge(pv_mm, NT * (g + 1))
            if g >= 1:
                act.wait_ge(filled, fills[("renorm", g - 1)] + 1)
            nc.scalar.copy(pvs[:], pv_bank[:]).then_inc(pv_copied, 1)

        def act_yT(act, b, c):
            if b >= 1:
                act.wait_ge(filled, fills[("cproj", b - 1, NT // 2 - 1)] + 1)
            bank = filled_bank(act, ("yT", b, c))
            nc.scalar.activation(yT[0][:, c, :], bank[:], ACT.Identity, bias=vconst[:, c:c + 1]).then_inc(y_hi, 1)

        def act_vproj(act, b, i):
            if b == 0:
                act.wait_ge(ones_init, 1)
                act.wait_ge(bias_ready, 2)
            else:
                act.wait_ge(pv_mm, NT * NGB * b)
            bank = filled_bank(act, ("vproj", b, i))
            nc.scalar.copy(val[:, 2 * i:2 * i + 2, :, 0:HD],
                           bank[:].rearrange("p (t h d) -> p t h d", t=2, h=NH)).then_inc(val_ready, 1)

        def act_x2T(act, b, c):
            bank = filled_bank(act, ("x2T", b, c))
            nc.scalar.copy(x2T[:, c, b * T:(b + 1) * T], bank[:]).then_inc(x2T_ready, 1)

        def act_router(act, b):
            bank = filled_bank(act, ("router", b))
            if b >= 1:
                act.wait_ge(comb_ready, b)
            nc.scalar.activation(rt[:, 0, :], bank[:, 0:NT * NE], ACT.Exp, scale=-1.0).then_inc(sig_ready, 1)

        def dve_setup(dve):
            for stack in kstack:
                nc.vector.memset(stack[96:97, :, :].bitcast(F32), -1.0).then_inc(minus_ready, 1)

        def dve_fold_qk(dve, n):
            dve.wait_ge(fold_hi, n + 1)
            nc.vector.tensor_tensor(folded(1, FOLDS[n]), fold_banks[FOLDS[n]][:], folded(0, FOLDS[n]).bitcast(F32),
                                    ALU.subtract).then_inc(fold_lo, 1)

        def dve_latent_biases(dve):
            dve.wait_ge(const_in, 48)
            dve.wait_ge(fold_mm, 5)
            lat_b = small[:, LATB:LATB + 4].rearrange("p (x s) -> p x s", x=2).unsqueeze(2).broadcast_to([P, 2, 2, 2])
            nc.vector.tensor_tensor(blat[:].rearrange("p (x f s) -> p x f s", x=2, f=2),
                                    pv_bank[:, 0:8].rearrange("p (x f s) -> p x f s", x=2, f=2), lat_b,
                                    ALU.add).then_inc(bias_ready, 1)

        def dve_fold_values(dve):
            dve.wait_ge(raw_in, 16)
            dve.wait_ge(m_mm, 1)
            nc.vector.tensor_tensor(l2o_kv2l, pv_bank[:, 0:P], block_mask, ALU.mult).then_inc(m_ready, 1)
            dve.wait_ge(raw_hi, 1)
            flat = "p s h l -> p (s h l)"
            nc.vector.tensor_tensor(wqk[1][:].rearrange(flat), raw_wqk, wqk[0][:].rearrange(flat).bitcast(F32),
                                    ALU.subtract).then_inc(raw_lo, 1)

        def dve_fold_rest(dve):
            dve.wait_ge(raw_hi, 2)
            flat = "p g c -> p (g c)"
            nc.vector.tensor_tensor(wcp[1][:].rearrange(flat), raw_wcp, wcp[0][:].rearrange(flat).bitcast(F32),
                                    ALU.subtract).then_inc(raw_lo, 1)
            dve.wait_ge(fold_hi, 5)
            nc.vector.tensor_tensor(folded(1, 4), fold_banks[4][:], folded(0, 4).bitcast(F32),
                                    ALU.subtract).then_inc(fold_lo, 1)
            dve.wait_ge(fold_mm, 7)
            nc.vector.tensor_scalar(vconst[:], pv_bank[:, 0:NC], small[:, L2OB:L2OB + 1], None,
                                    ALU.add).then_inc(bias_ready, 1)

        def wait_xn_used(eng, m):
            kind, b = norms[m]
            eng.wait_ge(filled, fills[("xT" if kind == "norm1" else "x2T", b, NC - 1)] + 1)

        def dve_stats(dve, kind, b, part):
            m = norms.index((kind, b))
            if kind == "norm1":
                dve.wait_ge(h_ready, b + 1)
            else:
                dve.wait_ge(h2_ready, NT // 2 * (b + 1))
            for i in range(NT // 2 * part, NT // 2 * (part + 1)):
                nc.vector.bn_stats(stats[:, i, :], h_all[:, b * NT + i, :]).then_inc(ln_stats, 1)
            if part == 1:
                if m >= 1:
                    dve.wait_ge(ln_rstd, m)
                for i in range(NT):
                    dve.wait_ge(ln_stats, NT * m + i + 1)
                    nc.vector.bn_aggr(meanvar[:, i, :], stats[:, i, :]).then_inc(ln_aggr, 1)

        def dve_xnorm(dve, kind, b):
            m = norms.index((kind, b))
            if m >= 1:
                wait_xn_used(dve, m - 1)
            dve.wait_ge(ln_aggr, NT * (m + 1))
            dve.wait_ge(ln_rstd, m + 1)
            for i in range(NT):
                nc.vector.tensor_scalar(xn[:, i, :], h_all[:, b * NT + i, :], meanvar[:, i, 0:1], rstd[:, i:i + 1],
                                        ALU.subtract, ALU.mult).then_inc(xn_ready, 1)

        def dve_xT(dve, b, c):
            if b >= 1:
                dve.wait_ge(filled, fills[("vproj", b - 1, NT // 2 - 1)] + 1)
            bank = filled_bank(dve, ("xT", b, c))
            dve.wait_ge(xT_hi, NC * b + c + 1)
            nc.vector.tensor_tensor(xT[1][:, c, :], bank[:], xT[0][:, c, :].bitcast(F32),
                                    ALU.subtract).then_inc(xT_lo, 1)

        def dve_rope(dve, u, s):
            if u == 0 and s == 0:
                dve.wait_ge(bias_ready, 1)
            if u >= 1 and s == 0:
                dve.wait_ge(rope_lo, 2 * u)
            bank = filled_bank(dve, ("rope", u, s))
            k = (0 if is_q(u) else 4) + 2 * (u // 2 % 2) + s
            for slot, table in (((0, rope_cos), (1, rope_sin)), ((2, rope_cos), (3, rope_sin)))[s]:
                nc.vector.scalar_tensor_tensor(out=prod[:, slot, :], in0=bank[:], scalar=blat[:, k:k + 1],
                                               in1=table[:], op0=ALU.add, op1=ALU.mult).then_inc(prod_ready, 1)

        def dve_latq_lo(dve, g):
            if g >= 1:
                dve.wait_ge(q_stored[(g - 1) % 2], 32 * ((g - 1) // 2 + 1))
            bank = filled_bank(dve, ("latq", g))
            dve.wait_ge(latq_hi, g + 1)
            nc.vector.scalar_tensor_tensor(out=qlat[1][:], in0=bank[:], scalar=small[:, WQKB:WQKB + 1],
                                           in1=qlat[0][:].bitcast(F32), op0=ALU.add,
                                           op1=ALU.subtract).then_inc(latq_lo, 1)

        def dve_max(dve, g, u):
            if g >= 1 and u == 0:
                dve.wait_ge(filled, fills[("maxT", g - 1)] + 1)
            i, h0, heads = MAX_TILES[u]
            k = g * NMX + u
            dve.wait_ge(mx_mm, k + 1)
            width = P * (i + 1)
            nc.vector.tensor_reduce(rowmax[:, h0:h0 + heads, i],
                                    mx_banks[k % 2][:, 0:heads * width].rearrange("p (h w) -> p h w", h=heads),
                                    AX_X, ALU.max).then_inc(mx_red, 1)

        def dve_maxT(dve, g):
            bank = filled_bank(dve, ("maxT", g))
            if g >= 1:
                wait_maxrow(dve, g - 1)
            nc.vector.tensor_copy(rowmaxT[:], bank[0:NT * GH, 0:P]).then_inc(maxT_ready, 1)

        def dve_renorm(dve, g):
            bank = filled_bank(dve, ("renorm", g))[:].rearrange("p (t h l) -> p t h l", t=NT, h=GH)
            if g >= 1:
                dve.wait_ge(ytok_ready, g)
            nc.vector.reciprocal(rden[:], bank[:, :, :, HD]).then_inc(rden_ready, 1)
            dve.wait_ge(rden_ready, g + 1)
            if g % NGB == 0 and g >= NGB:
                dve.wait_ge(filled, fills[("yT", g // NGB - 1, NC - 1)] + 1)
            cols = g % NGB * GH * HD
            nc.vector.tensor_tensor(ytok[:, :, cols:cols + GH * HD].rearrange("p t (h d) -> p t h d", h=GH),
                                    bank[:, :, :, 0:HD], rden[:].unsqueeze(3).broadcast_to([P, NT, GH, HD]),
                                    ALU.mult).then_inc(ytok_ready, 1)

        def dve_yT(dve, b, c):
            bank = filled_bank(dve, ("yT", b, c))
            dve.wait_ge(y_hi, NC * b + c + 1)
            nc.vector.scalar_tensor_tensor(out=yT[1][:, c, :], in0=bank[:], scalar=vconst[:, c:c + 1],
                                           in1=yT[0][:, c, :].bitcast(F32), op0=ALU.add,
                                           op1=ALU.subtract).then_inc(y_lo, 1)

        def dve_cproj(dve, b, i):
            dve.wait_ge(h_biased, NT * (b + 1))
            bank = filled_bank(dve, ("cproj", b, i))
            rows = h_all[:, b * NT + 2 * i:b * NT + 2 * i + 2, :].rearrange("p t c -> p (t c)")
            nc.vector.tensor_tensor(rows, bank[:], rows, ALU.add).then_inc(h2_ready, 1)

        def dve_route(dve, b, part):
            count = [ROUTE_OPS * b + ROUTE_BEFORE[part]]

            def after(ins):
                count[0] += 1
                ins.then_inc(routed, 1)
                return count[0]

            v, tt = nc.vector, nc.vector.tensor_tensor
            score, sc, masked, gt4, eq4, prefix, chosen = (rt[:, k, :] for k in range(7))
            a1, a2 = rt[:, 7, :], rt[:, 8, :]
            hi2, lo2 = rt[:, 9, 0:32], rt[:, 9, 32:64]
            top1, mid, low, gsum = (rt[:, 10, 16 * k:16 * k + 16] for k in range(4))
            gmask, top8 = rt[:, 11, 0:16], rt[:, 11, 16:48]
            above, wsum = rt[:, 11, 48:52], rt[:, 11, 52:56]
            row, by_group, q4 = "p (t e) -> p t e", "p (x e) -> p x e", "p (t i j) -> p t i j"
            if part == 0:
                dve.wait_ge(sig_ready, b + 1)
                n = after(v.tensor_scalar(score, score, 1.0, None, ALU.add))
                dve.wait_ge(routed, n)
                n = after(v.reciprocal(score, score))
                dve.wait_ge(routed, n)
                n = after(tt(sc, score, ebias, ALU.add))
            elif part == 1:
                dve.wait_ge(routed, count[0])
                pairs = sc.rearrange("p (g a two) -> p g a two", a=2, two=2)
                h2v, l2v = (x.rearrange("p (g a) -> p g a", a=2) for x in (hi2, lo2))
                after(tt(h2v, pairs[:, :, :, 0], pairs[:, :, :, 1], ALU.max))
                n = after(tt(l2v, pairs[:, :, :, 0], pairs[:, :, :, 1], ALU.min))
                dve.wait_ge(routed, n)
                after(tt(top1, h2v[:, :, 0], h2v[:, :, 1], ALU.max))
                after(tt(mid, h2v[:, :, 0], h2v[:, :, 1], ALU.min))
                n = after(tt(low, l2v[:, :, 0], l2v[:, :, 1], ALU.max))
                dve.wait_ge(routed, n)
                n = after(tt(mid, mid, low, ALU.max))
                dve.wait_ge(routed, n)
                n = after(tt(gsum, top1, mid, ALU.add))
            elif part == 2:
                dve.wait_ge(routed, count[0])
                gs = gsum.rearrange("p (t g) -> p t g", t=NT)
                gs_j = gs.unsqueeze(2).broadcast_to([P, NT, NGRP, NGRP])
                gs_i = gs.unsqueeze(3).broadcast_to([P, NT, NGRP, NGRP])
                a1v, a2v = a1.rearrange(q4, t=NT, i=NGRP), a2.rearrange(q4, t=NT, i=NGRP)
                after(tt(a1v, gs_j, gs_i, ALU.is_gt))
                n = after(tt(a2v, gs_j, gs_i, ALU.is_equal))
                dve.wait_ge(routed, n)
                n = after(tt(a2v, a2v, earlier, ALU.mult))
                dve.wait_ge(routed, n)
                n = after(tt(a1, a1, a2, ALU.add))
            elif part == 3:
                dve.wait_ge(routed, count[0])
                n = after(v.tensor_reduce(top1, a1.rearrange("p (x j) -> p x j", j=NGRP), AX_X, ALU.add))
                dve.wait_ge(routed, n)
                n = after(v.tensor_scalar(gmask, top1, 2.0, None, ALU.is_lt))
                dve.wait_ge(routed, n)
                after(tt(masked.rearrange(by_group, e=EPG), sc.rearrange(by_group, e=EPG),
                         gmask.unsqueeze(2).broadcast_to([P, NT * NGRP, EPG]), ALU.mult))
            elif part == 4:
                dve.wait_ge(routed, count[0])
                for t in range(NT):
                    after(v.max(top8[:, 8 * t:8 * t + 8], masked[:, t * NE:(t + 1) * NE]))
            elif part == 5:
                dve.wait_ge(routed, count[0])
                fourth = top8.rearrange("p (t k) -> p t k", t=NT)[:, :, TOPK - 1:TOPK].broadcast_to([P, NT, NE])
                after(tt(gt4.rearrange(row, t=NT), masked.rearrange(row, t=NT), fourth, ALU.is_gt))
                n = after(tt(eq4.rearrange(row, t=NT), masked.rearrange(row, t=NT), fourth, ALU.is_equal))
                dve.wait_ge(routed, n)
                after(v.tensor_reduce(above, gt4.rearrange(row, t=NT), AX_X, ALU.add))
                after(v.tensor_tensor_scan(prefix, same_row, eq4, 0.0, ALU.mult, ALU.add))
            elif part == 6:
                dve.wait_ge(routed, count[0])
                n = after(tt(a1.rearrange(row, t=NT), prefix.rearrange(row, t=NT),
                             above.unsqueeze(2).broadcast_to([P, NT, NE]), ALU.add))
                dve.wait_ge(routed, n)
                n = after(v.scalar_tensor_tensor(out=a2, in0=a1, scalar=float(TOPK), in1=eq4, op0=ALU.is_le,
                                                 op1=ALU.mult))
                dve.wait_ge(routed, n)
                n = after(tt(chosen, gt4, a2, ALU.add))
                dve.wait_ge(routed, n)
                after(tt(a1, score, chosen, ALU.mult))
            else:
                dve.wait_ge(routed, count[0])
                n = after(v.tensor_reduce(wsum, a1.rearrange(row, t=NT), AX_X, ALU.add))
                dve.wait_ge(routed, n)
                n = after(v.tensor_scalar(wsum, wsum, 1e-20, None, ALU.add))
                dve.wait_ge(routed, n)
                n = after(v.reciprocal(wsum, wsum))
                dve.wait_ge(routed, n)
                v.scalar_tensor_tensor(out=comb[:, b, :].rearrange(row, t=NT), in0=a1.rearrange(row, t=NT),
                                       scalar=ROUTE_SCALE, in1=wsum.unsqueeze(2).broadcast_to([P, NT, NE]),
                                       op0=ALU.mult, op1=ALU.mult).then_inc(comb_ready, 1)
            assert count[0] == ROUTE_OPS * b + (ROUTE_BEFORE + (ROUTE_OPS,))[part + 1]

        def nothing(eng, *piece):
            pass

        att.close()
        moe = ctx.enter_context(ExitStack())
        wstage = [sb(moe, f"wstage{i}", [P, WCOLS]) for i in range(2)]
        xs0 = pair(moe, "xs0", [P, NC, T])
        hid = [sb(moe, f"hid{p}", [P, T]) for p in range(2)]
        hidr = [pair(moe, f"hidr{p}", [P, T]) for p in range(2)]
        combT = sb(moe, "combT", [NE, T])
        spread = [sb(moe, f"spread{p}", [P, T]) for p in range(2)]
        wex_all = sb(moe, "wex", [P, NX, 2, WCOLS], F32R)
        wex = [wex_all[:, :, x, :] for x in range(2)]
        xs = [xs0, pair(moe, "xs1", [P, NC, T])]
        ysb = xn[:].rearrange("p t c -> p (t c)").rearrange("p (c t) -> p c t", c=NC)
        outbuf = [ytok[:, 2 * i:2 * i + 2, :] for i in range(2)]
        order = [NE + s for s in range(NSH)] + list(range(NE))
        NS = B * NX
        routed_before = [sum(order[k % NX] < NE for k in range(n)) for n in range(NS + 1)]

        EARLY_EXPERTS = 2

        def wait_latents_done(eng):
            wait_stack(eng, NG - 1)

        def wait_values_done(eng):
            eng.wait_ge(ytok_ready, NG)

        def sp_stage(sp, e):
            if e == 0:
                wait_latents_done(sp)
            if e >= 2:
                sp.wait_ge(ex_hi, e - 1)
                sp.wait_ge(ex_lo, e - 1)
            sp.dma_start(wstage[e % 2][:], io["experts"][order[e]]).then_inc(wstage_in[e % 2], 16)

        def act_weights(act, e):
            if e == EARLY_EXPERTS:
                wait_values_done(act)
            act.wait_ge(wstage_in[e % 2], 16 * (e // 2 + 1))
            nc.scalar.copy(wex[0][:, e, :], wstage[e % 2][:]).then_inc(ex_hi, 1)

        def dve_weights(dve, e):
            if e == EARLY_EXPERTS:
                wait_values_done(dve)
            dve.wait_ge(ex_hi, e + 1)
            nc.vector.tensor_tensor(wex[1][:, e, :], wstage[e % 2][:], wex[0][:, e, :].bitcast(F32),
                                    ALU.subtract).then_inc(ex_lo, 1)

        def pe_combT(pe, b):
            bank = bank_to_fill(pe, ("combT", b))
            pe.wait_ge(comb_ready, b + 1)
            for i in range(NT):
                mm = nc.tensor.transpose(bank[0:NE, i * P:(i + 1) * P], comb[:, b, i * NE:(i + 1) * NE], ident[:])
            mm.then_inc(filled, 1)

        def act_combT(act, b):
            bank = filled_bank(act, ("combT", b))
            if b >= 1:
                act.wait_ge(comb_stored, 16 * b)
            nc.scalar.copy(combT[:], bank[0:NE, :]).then_inc(combT_ready, 1)

        def sp_combT(sp, b):
            sp.wait_ge(combT_ready, b + 1)
            sp.dma_start(comb_dram[b], combT[:]).then_inc(comb_stored, 16)

        def sp_spread(sp, n):
            b, e, r = n // NX, order[n % NX], routed_before[n]
            if e >= NE:
                return
            sp.wait_ge(comb_stored, 16 * (b + 1))
            if r >= 2:
                sp.wait_ge(weighted, r - 1)
            sp.dma_start(spread[r % 2][:],
                         comb_dram[b, e:e + 1, :].broadcast_to([P, T])).then_inc(spread_in[r % 2], 16)

        def act_load_x(act, b):
            if b == 0:
                wait_latents_done(act)
            if b >= 2:
                act.wait_ge(up_mm, NX * (b - 1))
            for c in range(NC):
                nc.scalar.copy(xs[b % 2][0][:, c, :], x2T[:, c, b * T:(b + 1) * T]).then_inc(xs_hi, 1)

        def dve_load_x(dve, b):
            if b >= 2:
                dve.wait_ge(up_mm, NX * (b - 1))
            for c in range(NC):
                dve.wait_ge(xs_hi, NC * b + c + 1)
                nc.vector.tensor_tensor(xs[b % 2][1][:, c, :], x2T[:, c, b * T:(b + 1) * T],
                                        xs[b % 2][0][:, c, :].bitcast(F32), ALU.subtract).then_inc(xs_lo, 1)

        def pe_gate_up(pe, n):
            b, k = divmod(n, NX)
            if k == 0:
                pe.wait_ge(xs_hi, NC * (b + 1))
                pe.wait_ge(xs_lo, NC * (b + 1))
            if b == 0:
                pe.wait_ge(ex_hi, k + 1)
                pe.wait_ge(ex_lo, k + 1)
            if n >= 2:
                pe.wait_ge(silu_ready, n - 1)
                pe.wait_ge(hid_ready, n - 1)
            for bank, first, done in ((gate_banks[n % 2], 0, gate_mm), (up_banks[n % 2], NC * I, up_mm)):
                terms = [(w[:, k, first + c * I:first + (c + 1) * I], x[:, c, :]) for c in range(NC)
                         for w, x in passes(wex, xs[b % 2])]
                for j, (w, x) in enumerate(terms):
                    mm = nc.tensor.matmul(bank[:], w, x, start=(j == 0), stop=(j == len(terms) - 1))
                mm.then_inc(done, 1)
            if n >= 1:
                pe_down(pe, n - 1)

        def pe_down(pe, n):
            b, k = divmod(n, NX)
            pe.wait_ge(hid_hi, n + 1)
            pe.wait_ge(hid_lo, n + 1)
            if n == 0:
                wait_read(pe, fill_names[n_alternate - 1])
                wait_read(pe, fill_names[n_alternate - 2])
            if k == 0 and b >= 1:
                for c in range(NC):
                    pe.wait_ge(y_copied[c], b)
            for c in range(NC):
                cols = 2 * NC * I + c * P
                for j, (w, x) in enumerate(passes(wex, hidr[n % 2])):
                    mm = nc.tensor.matmul(y_banks[c][:], w[:, k, cols:cols + P], x[:], start=(k == 0 and j == 0),
                                          stop=(k == NX - 1 and j == 2))
            mm.then_inc(down_mm, 1)

        def act_gate_up(act, n):
            act.wait_ge(gate_mm, n + 1)
            if n >= 2:
                act.wait_ge(hid_lo, n - 1)
            nc.scalar.activation(hid[n % 2][:], gate_banks[n % 2][:], ACT.Silu).then_inc(silu_ready, 1)

        def dve_gate_up(dve, n):
            dve.wait_ge(silu_ready, n + 1)
            if order[n % NX] < NE:
                r = routed_before[n]
                dve.wait_ge(spread_in[r % 2], 16 * (r // 2 + 1))
                nc.vector.tensor_tensor(hid[n % 2][:], hid[n % 2][:], spread[r % 2][:],
                                        ALU.mult).then_inc(weighted, 1)
                dve.wait_ge(weighted, r + 1)
            dve.wait_ge(up_mm, n + 1)
            nc.vector.tensor_tensor(hid[n % 2][:], up_banks[n % 2][:], hid[n % 2][:], ALU.mult).then_inc(hid_ready, 1)

        def act_hidden(act, n):
            act.wait_ge(hid_ready, n + 1)
            if n >= 2:
                act.wait_ge(down_mm, n - 1)
            nc.scalar.copy(hidr[n % 2][0][:], hid[n % 2][:]).then_inc(hid_hi, 1)

        def dve_hidden(dve, n):
            dve.wait_ge(hid_hi, n + 1)
            nc.vector.tensor_tensor(hidr[n % 2][1][:], hid[n % 2][:], hidr[n % 2][0][:].bitcast(F32),
                                    ALU.subtract).then_inc(hid_lo, 1)

        def copy_y(eng, copy, b, c):
            eng.wait_ge(down_mm, NX * (b + 1))
            if b == 0:
                eng.wait_ge(filled, fills[("x2T", B - 1, NC - 1)] + 1)
            else:
                eng.wait_ge(filled, fills[("back", b - 1, 1)] + 1)
            copy(ysb[:, c, :], y_banks[c][:]).then_inc(y_copied[c], 1)

        def act_copy_y(act, b):
            copy_y(act, nc.scalar.copy, b, 0)

        def dve_copy_y(dve, b):
            copy_y(dve, nc.vector.tensor_copy, b, 1)

        def pe_back(pe, b, i):
            for c in range(NC):
                pe.wait_ge(y_copied[c], b + 1)
            bank = bank_to_fill(pe, ("back", b, i))
            for t in range(2):
                for c in range(NC):
                    tok = (2 * i + t) * P
                    mm = nc.tensor.transpose(bank[:, t * C + c * P:t * C + (c + 1) * P],
                                             ysb[:, c, tok:tok + P], ident[:])
            mm.then_inc(filled, 1)

        def dve_back(dve, b, i):
            bank = filled_bank(dve, ("back", b, i))
            if b >= 1:
                dve.wait_ge(out_done[i], 16 * b)
            rows = h_all[:, b * NT + 2 * i:b * NT + 2 * i + 2, :].rearrange("p t c -> p (t c)")
            nc.vector.tensor_tensor(outbuf[i].rearrange("p t c -> p (t c)"), bank[:], rows,
                                    ALU.add).then_inc(sum_ready, 1)

        def sp_back(sp, b, i):
            sp.wait_ge(sum_ready, NT // 2 * b + i + 1)
            sp.dma_start(io["out"][b].rearrange("(i t p) c -> i p t c", t=2, p=P)[i],
                         outbuf[i]).then_inc(out_done[i], 16)

        STAGES = {
            "sp": dict(latq=sp_latq, maxT=sp_maxT, combT=sp_combT, spread=sp_spread, stage=sp_stage, back=sp_back),
            "pool": dict(embed=pool_embed, stats=pool_stats, bias=pool_bias, rope_sum=pool_rope_sum,
                         rope_parts=pool_rope_parts),
            "pe": dict(fold_values=pe_fold_values, fold_rest=pe_fold_rest, xT=pe_xT, rope=pe_rope, latq=pe_latq,
                       max=pe_max, maxT=pe_maxT, score=pe_score, values=pe_values, renorm=pe_renorm, yT=pe_yT,
                       vproj=pe_vproj, cproj=pe_cproj, x2T=pe_x2T, router=pe_router, combT=pe_combT,
                       gate_up=pe_gate_up, down=pe_down, back=pe_back),
            "act": dict(fold_qk=act_fold_qk, fold_values=act_fold_values, fold_rest=act_fold_rest, xT=act_xT,
                        rope_parts=act_rope_parts, latq=act_latq, score=act_score, pv_out=act_pv_out, yT=act_yT,
                        vproj=act_vproj, x2T=act_x2T, router=act_router, weights=act_weights, combT=act_combT,
                        load_x=act_load_x, gate_up=act_gate_up, hidden=act_hidden, copy_y=act_copy_y),
            "dve": dict(embed=dve_embed, fold_qk=dve_fold_qk, latent_biases=dve_latent_biases,
                        fold_values=dve_fold_values, rope_sum=dve_rope_sum, fold_rest=dve_fold_rest, stats=dve_stats,
                        xnorm=dve_xnorm, xT=dve_xT, rope=dve_rope, rope_parts=dve_rope_parts, latq_lo=dve_latq_lo,
                        max=dve_max, maxT=dve_maxT, renorm=dve_renorm, yT=dve_yT, cproj=dve_cproj, route=dve_route,
                        weights=dve_weights, load_x=dve_load_x, gate_up=dve_gate_up, hidden=dve_hidden,
                        copy_y=dve_copy_y, back=dve_back),
        }

        def all_pieces(eng, engine):
            for piece in pieces:
                STAGES[engine].get(piece[0], nothing)(eng, *piece[1:])

        block = ctx.enter_context(nc.Block())

        @block.sync
        def _(sp):
            sp_setup(sp)
            all_pieces(sp, "sp")
            for i in range(2):
                sp.wait_ge(out_done[i], 16 * B)

        @block.gpsimd
        def _(pool):
            pool_setup(pool)
            all_pieces(pool, "pool")

        @block.tensor
        def _(pe):
            pe_setup(pe)
            all_pieces(pe, "pe")

        @block.scalar
        def _(act):
            all_pieces(act, "act")

        @block.vector
        def _(dve):
            dve_setup(dve)
            all_pieces(dve, "dve")


def kernel(x, L0_tok_emb, L0_attn_c_attn_w, L0_attn_c_attn_b, L0_attn_q2l_w, L0_attn_q2l_b, L0_attn_kv2l_w,
           L0_attn_kv2l_b, L0_attn_l2o_w, L0_attn_l2o_b, L0_attn_wqk_w, L0_attn_wqk_b, L0_attn_cproj_w,
           L0_attn_cproj_b, L0_ffn_router_weight, L0_ffn_e_bias, L0_ffn_gate_w, L0_ffn_up_w, L0_ffn_down_w,
           L0_ffn_sh_gate_w, L0_ffn_sh_up_w, L0_ffn_sh_down_w):
    import concourse.bacc as bacc
    import ml_dtypes
    from concourse.bass_utils import run_bass_kernel_spmd

    f4 = np.float32
    arr = {}
    arr["tok"] = np.ascontiguousarray(np.asarray(x).reshape(B * NT, P).T)
    arr["emb"] = np.asarray(L0_tok_emb)

    pos = np.arange(T, dtype=f4)[:, None]
    col = np.arange(C)
    angle = pos / np.power(f4(10000.0), (2 * (col // 2)).astype(f4) / f4(C)).astype(f4)
    table = np.where(col % 2 == 0, np.sin(angle), np.cos(angle)).astype(f4)
    arr["pos_enc"] = np.ascontiguousarray(table.reshape(NT, P, C).transpose(1, 0, 2)).reshape(P, NT * C)
    inv_freq = (f4(1.0) / np.power(f4(10000.0), np.arange(0, L, 2, dtype=f4) / f4(L))).astype(f4)
    freqs = np.outer(np.arange(T, dtype=f4), inv_freq).astype(f4)
    arr["rope_cos"] = np.tile(np.cos(freqs).T, (HALF, 1)).astype(f4)
    arr["rope_sin"] = np.tile(np.sin(freqs).T, (HALF, 1)).astype(f4)
    const = {}
    arr["ident"] = np.eye(P, dtype=f4)
    later = np.tril(np.ones((P, P), f4), -1) * f4(-1e30)
    arr["masks"] = np.stack([np.eye(P), later, later.T], axis=1).astype(ml_dtypes.bfloat16)
    same = np.ones((P, NT, NE), f4)
    same[:, :, 0] = 0
    const["same_row"] = same
    const["earlier"] = np.broadcast_to(np.tril(np.ones((NGRP, NGRP), f4), -1), (P, NT, NGRP, NGRP))
    bqkv, wq2l, wkv2l = (np.asarray(a) for a in (L0_attn_c_attn_b, L0_attn_q2l_w, L0_attn_kv2l_w))
    rows = np.asarray(L0_attn_c_attn_w).reshape(6, P, C).transpose(1, 0, 2)
    bd = np.zeros((HALF, HD, 2, 2, HALF, HD), f4)
    for h in range(HALF):
        for k, w in enumerate((wq2l, wkv2l)):
            for s in range(2):
                bd[h, :, k, s, h, :] = w[s::2].T
    arr["raw_qk"] = np.concatenate([rows[:, 0:4].reshape(P, 4 * C), bd.reshape(P, 4 * P)], axis=1)
    perm = np.concatenate([np.arange(0, L, 2), np.arange(1, L, 2)])
    wqk = np.asarray(L0_attn_wqk_w)
    qk = np.zeros((HALF, HD, 2, HALF, L), f4)
    for h in range(HALF):
        for s in range(2):
            qk[h, :, s, h, :] = wqk[perm][:, s::2].T
    cp = np.asarray(L0_attn_cproj_w).T.reshape(NC, P, C).transpose(1, 0, 2)
    block_mask = np.kron(np.eye(HALF), np.ones((HD, HD))).astype(f4)
    arr["raw_rest"] = np.concatenate([rows[:, 4:6].reshape(P, 2 * C), qk.reshape(P, 2 * HALF * L),
                                      cp.reshape(P, NC * C), block_mask], axis=1)
    arr["lat32"] = np.concatenate([np.tile(wkv2l, (1, HALF)), np.tile(np.asarray(L0_attn_l2o_w).T, (1, HALF)),
                                   np.asarray(L0_attn_kv2l_b)[:, None]], axis=1)
    small = np.zeros((P, 12), f4)
    small[:, 0:6] = bqkv.reshape(6, P).T
    for k, bias in enumerate((np.asarray(L0_attn_q2l_b), np.asarray(L0_attn_kv2l_b))):
        for s in range(2):
            small[:, 6 + 2 * k + s] = np.tile(bias[s::2], HALF)
    small[:, 10] = np.tile(np.asarray(L0_attn_wqk_b)[perm], GH)
    small[:, 11] = np.tile(np.asarray(L0_attn_l2o_b), HALF)
    const["small"] = small
    const["cproj_bias"] = np.broadcast_to(np.asarray(L0_attn_cproj_b), (P, C))
    const["router"] = np.asarray(L0_ffn_router_weight).T.reshape(NC, P, NE).transpose(1, 0, 2)
    const["ebias"] = np.tile(np.broadcast_to(np.asarray(L0_ffn_e_bias), (P, NE)), (1, NT))
    arr["consts"] = np.concatenate([const[name].reshape(P, cols) for name, cols in CONST_COLS.items()], axis=1)

    def rows_in_first(w):
        return w.transpose(0, 2, 1).reshape(-1, NC, P, I).transpose(0, 2, 1, 3).reshape(-1, P, NC * I)

    gate, up = (np.concatenate([np.asarray(a), np.asarray(s).reshape(NSH, I, C)]) for a, s in
                ((L0_ffn_gate_w, L0_ffn_sh_gate_w), (L0_ffn_up_w, L0_ffn_sh_up_w)))
    down = np.concatenate([np.asarray(L0_ffn_down_w).transpose(0, 2, 1),
                           np.asarray(L0_ffn_sh_down_w).T.reshape(NSH, I, C)])
    arr["experts"] = np.ascontiguousarray(np.concatenate([rows_in_first(gate), rows_in_first(up), down], axis=2))

    nc = bacc.Bacc("TRN2", target_bir_lowering=False, num_devices=1)
    from concourse import mybir as mb
    io = {n: nc.dram_tensor(f"in_{n}", a.shape, mb.dt.from_np(a.dtype), kind="ExternalInput").ap()
          for n, a in arr.items()}
    io["out"] = nc.dram_tensor("out_0", (B, T, C), F32, kind="ExternalOutput").ap()
    build_program(nc, io)
    r = run_bass_kernel_spmd(nc, [{f"in_{n}": a for n, a in arr.items()}], core_ids=[0])
    return r.results[0]["out_0"]
```
